# Optimizing a Trainium2 kernel written in Bass

```python
import numpy as np
import jax
import jax.numpy as jnp

def _softmax(x, axis=-1):
    return jax.nn.softmax(x, axis=axis)

def _gelu(x):
    return jax.nn.gelu(x, approximate=True)

def _silu(x):
    return jax.nn.silu(x)

def _sigmoid(x):
    return jax.nn.sigmoid(x)

def _layernorm(x, axis=-1, eps=1e-05):
    m = jnp.mean(x, axis=axis, keepdims=True)
    v = jnp.var(x, axis=axis, keepdims=True)
    return (x - m) / jnp.sqrt(v + eps)

def _scatter_add(tgt, idx, src, axis=0):
    return tgt.at[idx].add(src)

def _segment_sum(src, seg, n):
    return jax.ops.segment_sum(src, seg, n)
kernel_name = 'mk_flamingo_gated_d4_seqx_r4_f8ffdf'

def setup_inputs(seed: int=0):
    np.random.seed(seed)
    _w = jnp.asarray

    def _rec_inputs():
        import jax
        import jax.numpy as jnp
        _rk = jax.random.key(seed)
        x = 0.5 + 0.2887 * jax.random.normal(jax.random.fold_in(_rk, 1), (4, 512, 512), jnp.float32)
        _lenS = 512 - jax.random.randint(jax.random.fold_in(_rk, 7), (4,), 0, max(1, 512 // 4) + 1, jnp.int32)
        _lenS2 = 512 - jax.random.randint(jax.random.fold_in(_rk, 8), (4,), 0, max(1, 512 // 4) + 1, jnp.int32)
        _ctx_512P = jax.random.normal(jax.random.fold_in(_rk, 11), (4, 16, 128), jnp.float32)
        _ctx_512c = jax.random.dirichlet(jax.random.fold_in(_rk, 511), 0.3 * jnp.ones((16,), jnp.float32), (4, 512))
        _ctx_512t = jnp.einsum('bsk,bkd->bsd', _ctx_512c, _ctx_512P)
        _ctx_512t = _ctx_512t * jax.lax.rsqrt(jnp.mean(jnp.square(_ctx_512t)) + 1e-12) * 0.953939
        ctx_512 = -0.000392918 + 0.999932 * (_ctx_512t + 0.3 * jax.random.normal(jax.random.fold_in(_rk, 611), (4, 512, 128), jnp.float32))
        _g = jax.random.normal(jax.random.fold_in(_rk, 9001), (2, 4), jnp.float32)
        _g = jnp.sign(_g) * jnp.maximum(jnp.abs(_g), 1.0) + (_g == 0) * 1.0
        g_xattn = _g[0]
        g_ffn = _g[1]
        return (x, ctx_512, g_xattn, g_ffn)
    x, ctx_512, g_xattn, g_ffn = _rec_inputs()

    def _L0_xattn_setup():
        import jax, jax.numpy as jnp
        import numpy as np
        B, N, D = (16, 512, 128)
        H = 4
        TOP_K_RATIO = 0.3
        key = jax.random.key(seed)
        k1, k2, k3, k4 = jax.random.split(key, 4)
        h = jax.random.normal(k1, (B, N, D), dtype=jnp.float32)
        adj_raw = jax.random.uniform(k2, (B, N, N), dtype=jnp.float32)
        lim = 1.0 / np.sqrt(D)
        Wq = jax.random.uniform(k3, (D, D), minval=-lim, maxval=lim, dtype=jnp.float32)
        Wk = jax.random.uniform(k4, (D, D), minval=-lim, maxval=lim, dtype=jnp.float32)
        gamma_raw = jnp.float32(-0.85)
        return {'h': h, 'adj_raw': adj_raw, 'Wq': Wq, 'Wk': Wk, 'gamma_raw': gamma_raw}
    _L0_xattn_all = _L0_xattn_setup()
    _L0_xattn_in = {k: v for k, v in _L0_xattn_all.items() if k in ('Wq', 'Wk', 'gamma_raw')}
    del _L0_xattn_all

    def _L0_ffn_setup():
        import jax, jax.numpy as jnp
        import numpy as np
        B, S, D, H = (4, 512, 512, 2048)

        def fwht(x):
            orig_shape = x.shape
            n = orig_shape[-1]
            x = x.reshape(-1, n)
            h = 1
            while h < n:
                xb = x.reshape(-1, n // (2 * h), 2, h)
                a = xb[:, :, 0, :]
                b = xb[:, :, 1, :]
                x = jnp.stack([a + b, a - b], axis=2).reshape(-1, n)
                h *= 2
            scale = jnp.asarray(1.0 / np.sqrt(n), dtype=x.dtype)
            return (x * scale).reshape(orig_shape)
        key = jax.random.key(seed)
        kx, k1, k2, k3 = jax.random.split(key, 4)
        x = jax.random.normal(kx, (B, S, D), dtype=jnp.float32)
        W1 = jax.random.normal(k1, (H, D), dtype=jnp.float32) * (1.0 / np.sqrt(D))
        W2 = jax.random.normal(k2, (D, H), dtype=jnp.float32) * (1.0 / np.sqrt(H))
        W3 = jax.random.normal(k3, (H, D), dtype=jnp.float32) * (1.0 / np.sqrt(D))
        return {'x': x, 'W1': W1, 'W2': W2, 'W3': W3}
    _L0_ffn_all = _L0_ffn_setup()
    _L0_ffn_in = {k: v for k, v in _L0_ffn_all.items() if k in ('W1', 'W2', 'W3')}
    del _L0_ffn_all

    def _L1_xattn_setup():
        import jax, jax.numpy as jnp
        import numpy as np
        EPS = 1e-06
        IMAGE_DIMS = 512
        key = jax.random.key(seed)
        k1, k2, k3 = jax.random.split(key, 3)
        B, I, J, D = (16, 512, 512, 128)
        p = jax.random.normal(k1, (B, I, J), dtype=jnp.float32)
        k_v = jax.random.normal(k2, (B, J, D), dtype=jnp.float32)
        W_k = jax.random.normal(k3, (D, D), dtype=jnp.float32) * (1.0 / np.sqrt(D))
        b_k = jnp.zeros((D,), dtype=jnp.float32)
        ln_gamma = jnp.ones((J,), dtype=jnp.float32)
        ln_beta = jnp.zeros((J,), dtype=jnp.float32)
        return {'p': p, 'k_v': k_v, 'W_k': W_k, 'b_k': b_k, 'ln_gamma': ln_gamma, 'ln_beta': ln_beta}
    _L1_xattn_all = _L1_xattn_setup()
    _L1_xattn_in = {k: v for k, v in _L1_xattn_all.items() if k in ('W_k', 'b_k', 'ln_gamma', 'ln_beta')}
    del _L1_xattn_all

    def _L1_ffn_setup():
        import jax, jax.numpy as jnp
        import numpy as np
        EPS = 1e-06
        K_STEPS = 4
        USE_GATING = True

        def layer_norm(x, gamma, beta):
            mu = jnp.mean(x, axis=-1, keepdims=True)
            var = jnp.mean(jnp.square(x - mu), axis=-1, keepdims=True)
            return (x - mu) * jax.lax.rsqrt(var + EPS) * gamma + beta
        key = jax.random.key(seed)
        B, L, D, H = (4, 1024, 512, 2048)
        ks = jax.random.split(key, 16)
        s = 0.02
        return {'x': jax.random.normal(ks[0], (B, L, D), dtype=jnp.float32), 'in_gamma': jnp.ones((D,), jnp.float32), 'in_beta': jnp.zeros((D,), jnp.float32), 'agg_w': jax.random.normal(ks[1], (D, D), jnp.float32) * s, 'agg_b': jnp.zeros((D,), jnp.float32), 'pn_gamma': jnp.ones((D,), jnp.float32), 'pn_beta': jnp.zeros((D,), jnp.float32), 'd1_w': jax.random.normal(ks[2], (D, H), jnp.float32) * s, 'd1_b': jnp.zeros((H,), jnp.float32), 'd2_w': jax.random.normal(ks[3], (H, D), jnp.float32) * s, 'd2_b': jnp.zeros((D,), jnp.float32), 'bc_w': jax.random.normal(ks[4], (D, D), jnp.float32) * s, 'bc_b': jnp.zeros((D,), jnp.float32), 'gate_w': jax.random.normal(ks[5], (D, D), jnp.float32) * s, 'gate_b': jnp.zeros((D,), jnp.float32), 'out_gamma': jnp.ones((D,), jnp.float32), 'out_beta': jnp.zeros((D,), jnp.float32)}
    _L1_ffn_all = _L1_ffn_setup()
    _L1_ffn_in = {k: v for k, v in _L1_ffn_all.items() if k in ('in_gamma', 'in_beta', 'agg_w', 'agg_b', 'pn_gamma', 'pn_beta', 'd1_w', 'd1_b', 'd2_w', 'd2_b', 'bc_w', 'bc_b', 'gate_w', 'gate_b', 'out_gamma', 'out_beta')}
    del _L1_ffn_all

    def _L2_xattn_setup():
        import jax, jax.numpy as jnp
        import numpy as np
        B, S, E = (2, 512, 512)
        QH, KVH = (32, 8)
        D = E // QH
        G = QH // KVH
        DROPOUT = 1.0
        key = jax.random.key(seed)
        k1, k2, k3 = jax.random.split(key, 3)
        q = jax.random.normal(k1, (B, S, E), dtype=jnp.float32)
        k = jax.random.normal(k2, (B, S, E // G), dtype=jnp.float32)
        v = jax.random.normal(k3, (B, S, E // G), dtype=jnp.float32)
        return {'q': q, 'k': k, 'v': v}
    _L2_xattn_all = _L2_xattn_setup()
    _L2_xattn_in = {k: v for k, v in _L2_xattn_all.items() if k in ()}
    del _L2_xattn_all

    def _L2_ffn_setup():
        import jax, jax.numpy as jnp
        import numpy as np
        H = 512
        I = 352
        E = 8
        K = 2
        B, S = (4, 512)

        def _moe(x, router_w, w1, w2):
            b, s, h = x.shape
            xf = x.reshape(-1, h)
            T = xf.shape[0]
            logits = xf @ router_w.T
            topk_vals, topk_idx = jax.lax.top_k(logits, K)
            topk_w = jax.nn.softmax(topk_vals, axis=-1)
            exp_id = topk_idx.reshape(-1)
            exp_w = topk_w.reshape(-1)
            order = jnp.argsort(exp_id)
            x_sorted = xf[order // K]
            counts = jnp.bincount(exp_id, length=E).astype(jnp.int32)
            y1 = jax.lax.ragged_dot(x_sorted, jnp.swapaxes(w1, 1, 2), counts)
            gate, up = jnp.split(y1, 2, axis=-1)
            y_act = jax.nn.silu(gate) * up
            y2 = jax.lax.ragged_dot(y_act, jnp.swapaxes(w2, 1, 2), counts)
            inv = jnp.argsort(order)
            y_pairs = y2[inv] * exp_w[:, None]
            y = y_pairs.reshape(T, K, h).sum(axis=1)
            return y.reshape(b, s, h)
        key = jax.random.key(seed)
        k1, k2, k3, k4 = jax.random.split(key, 4)
        x = jax.random.normal(k1, (B, S, H), dtype=jnp.float32)
        router_w = jax.random.normal(k2, (E, H), dtype=jnp.float32) * 0.02
        w1 = jax.random.normal(k3, (E, 2 * I, H), dtype=jnp.float32) * 0.02
        w2 = jax.random.normal(k4, (E, H, I), dtype=jnp.float32) * 0.02
        return {'x': x, 'router_w': router_w, 'w1': w1, 'w2': w2}
    _L2_ffn_all = _L2_ffn_setup()
    _L2_ffn_in = {k: v for k, v in _L2_ffn_all.items() if k in ('router_w', 'w1', 'w2')}
    del _L2_ffn_all

    def _L3_xattn_setup():
        import jax, jax.numpy as jnp
        import numpy as np
        B, S, L = (2, 256, 256)
        DIM_Q, H, K, D_C, D_CQ, R = (512, 16, 128, 128, 384, 64)

        def _rope_tables(length, dim):
            inv = 1.0 / 10000.0 ** (jnp.arange(0, dim, 2, dtype=jnp.float32) / dim)
            f = jnp.arange(length, dtype=jnp.float32)[:, None] * inv[None, :]
            sin = jnp.repeat(jnp.sin(f), 2, axis=-1)
            cos = jnp.repeat(jnp.cos(f), 2, axis=-1)
            return (sin, cos)

        def _rotate_half(x):
            half = x.shape[-1] // 2
            return jnp.concatenate([-x[..., half:], x[..., :half]], axis=-1)

        def _apply_rope(x, sin, cos):
            return x * cos + _rotate_half(x) * sin
        key = jax.random.key(seed)
        ks = jax.random.split(key, 8)
        return {'hidden_q': jax.random.normal(ks[0], (B, S, DIM_Q), jnp.float32), 'kv_c': jax.random.normal(ks[1], (B, L, D_C), jnp.float32), 'Wq': jax.random.normal(ks[2], (H * K, DIM_Q), jnp.float32) / np.sqrt(DIM_Q).astype(np.float32), 'w_kc_q': jax.random.normal(ks[3], (H, K, D_CQ), jnp.float32) / np.sqrt(K).astype(np.float32), 'w_kc_kv': jax.random.normal(ks[4], (H, K, D_C), jnp.float32) / np.sqrt(K).astype(np.float32), 'W_qr': jax.random.normal(ks[5], (H, D_CQ, R), jnp.float32) / np.float32(np.sqrt(D_CQ) * np.sqrt(R)), 'W_kr': jax.random.normal(ks[6], (H, D_C, R), jnp.float32) / np.sqrt(D_C).astype(np.float32), 'Wo': jax.random.normal(ks[7], (DIM_Q, H * K), jnp.float32) / np.sqrt(H * K).astype(np.float32)}
    _L3_xattn_all = _L3_xattn_setup()
    _L3_xattn_in = {k: v for k, v in _L3_xattn_all.items() if k in ('Wq', 'w_kc_q', 'w_kc_kv', 'W_qr', 'W_kr', 'Wo')}
    del _L3_xattn_all

    def _L3_ffn_setup():
        import jax, jax.numpy as jnp
        import numpy as np
        DIM_IN = 512
        DIM_HIDDEN = 2048
        key = jax.random.key(seed)
        k_x, k_g, k_u, k_d = jax.random.split(key, 4)
        s_in = 1.0 / np.sqrt(DIM_IN)
        s_hid = 1.0 / np.sqrt(DIM_HIDDEN)
        x = jax.random.normal(k_x, (4, 512, DIM_IN), dtype=jnp.float32)
        w_gate = jax.random.uniform(k_g, (DIM_HIDDEN, DIM_IN), jnp.float32, -s_in, s_in)
        w_up = jax.random.uniform(k_u, (DIM_HIDDEN, DIM_IN), jnp.float32, -s_in, s_in)
        w_down = jax.random.uniform(k_d, (DIM_IN, DIM_HIDDEN), jnp.float32, -s_hid, s_hid)
        return {'x': x, 'w_gate': w_gate, 'w_up': w_up, 'w_down': w_down}
    _L3_ffn_all = _L3_ffn_setup()
    _L3_ffn_in = {k: v for k, v in _L3_ffn_all.items() if k in ('w_gate', 'w_up', 'w_down')}
    del _L3_ffn_all
    return {'x': x, 'ctx_512': ctx_512, 'g_xattn': g_xattn, 'g_ffn': g_ffn, 'L0_xattn_Wq': _L0_xattn_in['Wq'], 'L0_xattn_Wk': _L0_xattn_in['Wk'], 'L0_xattn_gamma_raw': _L0_xattn_in['gamma_raw'], 'L0_ffn_W1': _L0_ffn_in['W1'], 'L0_ffn_W2': _L0_ffn_in['W2'], 'L0_ffn_W3': _L0_ffn_in['W3'], 'L1_xattn_W_k': _L1_xattn_in['W_k'], 'L1_xattn_b_k': _L1_xattn_in['b_k'], 'L1_xattn_ln_gamma': _L1_xattn_in['ln_gamma'], 'L1_xattn_ln_beta': _L1_xattn_in['ln_beta'], 'L1_ffn_in_gamma': _L1_ffn_in['in_gamma'], 'L1_ffn_in_beta': _L1_ffn_in['in_beta'], 'L1_ffn_agg_w': _L1_ffn_in['agg_w'], 'L1_ffn_agg_b': _L1_ffn_in['agg_b'], 'L1_ffn_pn_gamma': _L1_ffn_in['pn_gamma'], 'L1_ffn_pn_beta': _L1_ffn_in['pn_beta'], 'L1_ffn_d1_w': _L1_ffn_in['d1_w'], 'L1_ffn_d1_b': _L1_ffn_in['d1_b'], 'L1_ffn_d2_w': _L1_ffn_in['d2_w'], 'L1_ffn_d2_b': _L1_ffn_in['d2_b'], 'L1_ffn_bc_w': _L1_ffn_in['bc_w'], 'L1_ffn_bc_b': _L1_ffn_in['bc_b'], 'L1_ffn_gate_w': _L1_ffn_in['gate_w'], 'L1_ffn_gate_b': _L1_ffn_in['gate_b'], 'L1_ffn_out_gamma': _L1_ffn_in['out_gamma'], 'L1_ffn_out_beta': _L1_ffn_in['out_beta'], 'L2_ffn_router_w': _L2_ffn_in['router_w'], 'L2_ffn_w1': _L2_ffn_in['w1'], 'L2_ffn_w2': _L2_ffn_in['w2'], 'L3_xattn_Wq': _L3_xattn_in['Wq'], 'L3_xattn_w_kc_q': _L3_xattn_in['w_kc_q'], 'L3_xattn_w_kc_kv': _L3_xattn_in['w_kc_kv'], 'L3_xattn_W_qr': _L3_xattn_in['W_qr'], 'L3_xattn_W_kr': _L3_xattn_in['W_kr'], 'L3_xattn_Wo': _L3_xattn_in['Wo'], 'L3_ffn_w_gate': _L3_ffn_in['w_gate'], 'L3_ffn_w_up': _L3_ffn_in['w_up'], 'L3_ffn_w_down': _L3_ffn_in['w_down']}

def reference(x, ctx_512, g_xattn, g_ffn, L0_xattn_Wq, L0_xattn_Wk, L0_xattn_gamma_raw, L0_ffn_W1, L0_ffn_W2, L0_ffn_W3, L1_xattn_W_k, L1_xattn_b_k, L1_xattn_ln_gamma, L1_xattn_ln_beta, L1_ffn_in_gamma, L1_ffn_in_beta, L1_ffn_agg_w, L1_ffn_agg_b, L1_ffn_pn_gamma, L1_ffn_pn_beta, L1_ffn_d1_w, L1_ffn_d1_b, L1_ffn_d2_w, L1_ffn_d2_b, L1_ffn_bc_w, L1_ffn_bc_b, L1_ffn_gate_w, L1_ffn_gate_b, L1_ffn_out_gamma, L1_ffn_out_beta, L2_ffn_router_w, L2_ffn_w1, L2_ffn_w2, L3_xattn_Wq, L3_xattn_w_kc_q, L3_xattn_w_kc_kv, L3_xattn_W_qr, L3_xattn_W_kr, L3_xattn_Wo, L3_ffn_w_gate, L3_ffn_w_up, L3_ffn_w_down):
    import jax
    import jax.numpy as jnp

    def _L0_xattn_ref(h, adj_raw, Wq, Wk, gamma_raw):
        import jax, jax.numpy as jnp
        import numpy as np
        B, N, D = (16, 512, 128)
        H = 4
        TOP_K_RATIO = 0.3
        b, n, dm = h.shape
        d = dm // H
        Q = (h @ Wq.T).reshape(b, n, H, d).transpose(0, 2, 1, 3)
        K = (h @ Wk.T).reshape(b, n, H, d).transpose(0, 2, 1, 3)
        sim = jnp.einsum('bhnd,bhmd->bnm', Q, K) / (jnp.sqrt(jnp.float32(d)) * H)
        k = max(1, int(n * TOP_K_RATIO))
        topk_vals = jax.lax.top_k(sim, k)[0]
        threshold = topk_vals[:, :, -1:]
        sparse_mask = (sim >= threshold).astype(sim.dtype)
        A_learned = jax.nn.sigmoid(sim) * sparse_mask
        A_learned = (A_learned + jnp.swapaxes(A_learned, -1, -2)) * 0.5
        gamma = jax.nn.sigmoid(gamma_raw)
        return (1.0 - gamma) * adj_raw + gamma * A_learned

    def _L0_ffn_ref(x, W1, W2, W3):
        import jax, jax.numpy as jnp
        import numpy as np
        B, S, D, H = (4, 512, 512, 2048)

        def fwht(x):
            orig_shape = x.shape
            n = orig_shape[-1]
            x = x.reshape(-1, n)
            h = 1
            while h < n:
                xb = x.reshape(-1, n // (2 * h), 2, h)
                a = xb[:, :, 0, :]
                b = xb[:, :, 1, :]
                x = jnp.stack([a + b, a - b], axis=2).reshape(-1, n)
                h *= 2
            scale = jnp.asarray(1.0 / np.sqrt(n), dtype=x.dtype)
            return (x * scale).reshape(orig_shape)
        up_gate = jnp.einsum('bsd,hd->bsh', x, W1)
        up_lin = jnp.einsum('bsd,hd->bsh', x, W3)
        hidden = jax.nn.silu(up_gate) * up_lin
        hidden = fwht(hidden)
        out = jnp.einsum('bsh,dh->bsd', hidden, W2)
        return out

    def _L1_xattn_ref(p, k_v, W_k, b_k, ln_gamma, ln_beta):
        import jax, jax.numpy as jnp
        import numpy as np
        EPS = 1e-06
        IMAGE_DIMS = 512
        kv = k_v @ W_k.T + b_k
        out = jnp.einsum('bij,bjd->bid', p, kv)
        scale = IMAGE_DIMS ** (-0.5)
        sim = jnp.einsum('bid,bjd->bij', out, kv) * scale
        mu = jnp.mean(sim, axis=-1, keepdims=True)
        var = jnp.var(sim, axis=-1, keepdims=True)
        sim = (sim - mu) * jax.lax.rsqrt(var + EPS) * ln_gamma + ln_beta
        attn = jax.nn.softmax(sim, axis=-1)
        return attn

    def _L1_ffn_ref(x, in_gamma, in_beta, agg_w, agg_b, pn_gamma, pn_beta, d1_w, d1_b, d2_w, d2_b, bc_w, bc_b, gate_w, gate_b, out_gamma, out_beta):
        import jax, jax.numpy as jnp
        import numpy as np
        EPS = 1e-06
        K_STEPS = 4
        USE_GATING = True

        def layer_norm(x, gamma, beta):
            mu = jnp.mean(x, axis=-1, keepdims=True)
            var = jnp.mean(jnp.square(x - mu), axis=-1, keepdims=True)
            return (x - mu) * jax.lax.rsqrt(var + EPS) * gamma + beta
        x_norm = layer_norm(x, in_gamma, in_beta)
        thought = x_norm[:, -1, :] @ agg_w + agg_b
        for _ in range(K_STEPS):
            t = layer_norm(thought, pn_gamma, pn_beta)
            t = jax.nn.gelu(t @ d1_w + d1_b, approximate=False)
            thought = thought + (t @ d2_w + d2_b)
        broadcast = (thought @ bc_w + bc_b)[:, None, :]
        if USE_GATING:
            gate = jax.nn.sigmoid(x @ gate_w + gate_b)
            out = x + gate * broadcast
        else:
            out = x + broadcast
        return layer_norm(out, out_gamma, out_beta)

    def _L2_xattn_ref(q, k, v):
        import jax, jax.numpy as jnp
        import numpy as np
        B, S, E = (2, 512, 512)
        QH, KVH = (32, 8)
        D = E // QH
        G = QH // KVH
        DROPOUT = 1.0
        b, s, _ = q.shape
        qh = q.reshape(b, s, KVH, G, D).transpose(0, 2, 3, 1, 4)
        kh = k.reshape(b, s, KVH, D).transpose(0, 2, 1, 3)
        vh = v.reshape(b, s, KVH, D).transpose(0, 2, 1, 3)
        scale = 1.0 / jnp.sqrt(jnp.float32(D))
        scores = jnp.einsum('bkgsd,bktd->bkgst', qh, kh) * scale
        attn = jax.nn.softmax(scores, axis=-1) / DROPOUT
        out = jnp.einsum('bkgst,bktd->bkgsd', attn, vh)
        return out.transpose(0, 3, 1, 2, 4).reshape(b, s, E)

    def _L2_ffn_ref(x, router_w, w1, w2):
        import jax, jax.numpy as jnp
        import numpy as np
        H = 512
        I = 352
        E = 8
        K = 2
        B, S = (4, 512)

        def _moe(x, router_w, w1, w2):
            b, s, h = x.shape
            xf = x.reshape(-1, h)
            T = xf.shape[0]
            logits = xf @ router_w.T
            topk_vals, topk_idx = jax.lax.top_k(logits, K)
            topk_w = jax.nn.softmax(topk_vals, axis=-1)
            exp_id = topk_idx.reshape(-1)
            exp_w = topk_w.reshape(-1)
            order = jnp.argsort(exp_id)
            x_sorted = xf[order // K]
            counts = jnp.bincount(exp_id, length=E).astype(jnp.int32)
            y1 = jax.lax.ragged_dot(x_sorted, jnp.swapaxes(w1, 1, 2), counts)
            gate, up = jnp.split(y1, 2, axis=-1)
            y_act = jax.nn.silu(gate) * up
            y2 = jax.lax.ragged_dot(y_act, jnp.swapaxes(w2, 1, 2), counts)
            inv = jnp.argsort(order)
            y_pairs = y2[inv] * exp_w[:, None]
            y = y_pairs.reshape(T, K, h).sum(axis=1)
            return y.reshape(b, s, h)
        return _moe(x, router_w, w1, w2)

    def _L3_xattn_ref(hidden_q, kv_c, Wq, w_kc_q, w_kc_kv, W_qr, W_kr, Wo):
        import jax, jax.numpy as jnp
        import numpy as np
        B, S, L = (2, 256, 256)
        DIM_Q, H, K, D_C, D_CQ, R = (512, 16, 128, 128, 384, 64)

        def _rope_tables(length, dim):
            inv = 1.0 / 10000.0 ** (jnp.arange(0, dim, 2, dtype=jnp.float32) / dim)
            f = jnp.arange(length, dtype=jnp.float32)[:, None] * inv[None, :]
            sin = jnp.repeat(jnp.sin(f), 2, axis=-1)
            cos = jnp.repeat(jnp.cos(f), 2, axis=-1)
            return (sin, cos)

        def _rotate_half(x):
            half = x.shape[-1] // 2
            return jnp.concatenate([-x[..., half:], x[..., :half]], axis=-1)

        def _apply_rope(x, sin, cos):
            return x * cos + _rotate_half(x) * sin
        Bv, Sv, _ = hidden_q.shape
        _, Lv, _ = kv_c.shape
        q_hk = (hidden_q @ Wq.T).reshape(Bv, Sv, H, K)
        q_big = jnp.einsum('bshk,hkq->bshq', q_hk, w_kc_q)
        sin_q, cos_q = _rope_tables(Sv, D_CQ)
        q_big = _apply_rope(q_big, sin_q[None, :, None, :], cos_q[None, :, None, :])
        sin_k, cos_k = _rope_tables(Lv, D_C)
        kv_r = _apply_rope(kv_c, sin_k[None], cos_k[None])
        q_r = jnp.einsum('bshq,hqr->bhsr', q_big, W_qr)
        k_r = jnp.einsum('bld,hdr->bhlr', kv_r, W_kr)
        scores = jnp.einsum('bhsr,bhlr->bhsl', q_r, k_r)
        attn = jax.nn.softmax(scores, axis=-1)
        ctx_c = jnp.einsum('bhsl,bld->bhsd', attn, kv_r)
        ctx_lat = jnp.einsum('bhsd,hkd->bhsk', ctx_c, w_kc_kv)
        ctx = ctx_lat.transpose(0, 2, 1, 3).reshape(Bv, Sv, H * K)
        return ctx @ Wo.T

    def _L3_ffn_ref(x, w_gate, w_up, w_down):
        import jax, jax.numpy as jnp
        import numpy as np
        DIM_IN = 512
        DIM_HIDDEN = 2048
        gate = jnp.einsum('bsd,hd->bsh', x, w_gate)
        up = jnp.einsum('bsd,hd->bsh', x, w_up)
        gated = jax.nn.silu(gate) * up
        return jnp.einsum('bsh,dh->bsd', gated, w_down)
    x = x + jnp.tanh(g_xattn[0]) * _L0_xattn_ref(ctx_512, _layernorm(x, axis=-1), L0_xattn_Wq, L0_xattn_Wk, L0_xattn_gamma_raw)
    x = x + jnp.tanh(g_ffn[0]) * _L0_ffn_ref(_layernorm(x, axis=-1), L0_ffn_W1, L0_ffn_W2, L0_ffn_W3)
    x = x + jnp.tanh(g_xattn[1]) * _L1_xattn_ref(_layernorm(x, axis=-1), ctx_512, L1_xattn_W_k, L1_xattn_b_k, L1_xattn_ln_gamma, L1_xattn_ln_beta)
    x = x + jnp.tanh(g_ffn[1]) * _L1_ffn_ref(_layernorm(x, axis=-1), L1_ffn_in_gamma, L1_ffn_in_beta, L1_ffn_agg_w, L1_ffn_agg_b, L1_ffn_pn_gamma, L1_ffn_pn_beta, L1_ffn_d1_w, L1_ffn_d1_b, L1_ffn_d2_w, L1_ffn_d2_b, L1_ffn_bc_w, L1_ffn_bc_b, L1_ffn_gate_w, L1_ffn_gate_b, L1_ffn_out_gamma, L1_ffn_out_beta)
    x = x + jnp.tanh(g_xattn[2]) * _L2_xattn_ref(_layernorm(x, axis=-1), ctx_512, ctx_512)
    x = x + jnp.tanh(g_ffn[2]) * _L2_ffn_ref(_layernorm(x, axis=-1), L2_ffn_router_w, L2_ffn_w1, L2_ffn_w2)
    x = x + jnp.tanh(g_xattn[3]) * _L3_xattn_ref(_layernorm(x, axis=-1), ctx_512, L3_xattn_Wq, L3_xattn_w_kc_q, L3_xattn_w_kc_kv, L3_xattn_W_qr, L3_xattn_W_kr, L3_xattn_Wo)
    x = x + jnp.tanh(g_ffn[3]) * _L3_ffn_ref(_layernorm(x, axis=-1), L3_ffn_w_gate, L3_ffn_w_up, L3_ffn_w_down)
    return x

_drawn_inputs = setup_inputs


def setup_inputs(seed=0):
    import zlib

    import numpy as np

    out = dict(_drawn_inputs(seed))
    spreads = {'L1_xattn_b_k': (0.0, 2.0),
     'L1_xattn_ln_gamma': (1.0, 0.6),
     'L1_xattn_ln_beta': (0.0, 0.8),
     'L1_ffn_in_gamma': (1.0, 0.6),
     'L1_ffn_in_beta': (0.0, 0.729),
     'L1_ffn_agg_b': (0.0, 0.36),
     'L1_ffn_pn_gamma': (1.0, 0.6),
     'L1_ffn_pn_beta': (0.0, 0.693),
     'L1_ffn_d1_b': (0.0, 0.324),
     'L1_ffn_d2_b': (0.0, 0.1),
     'L1_ffn_bc_b': (0.0, 0.343),
     'L1_ffn_gate_b': (0.0, 0.8),
     'L1_ffn_out_gamma': (1.0, 0.2),
     'L1_ffn_out_beta': (0.0, 0.1)}
    factors = {'g_ffn': 22.976,
     'L1_xattn_W_k': 8.0,
     'L2_ffn_router_w': 5.683,
     'L2_ffn_w1': 4.887,
     'L2_ffn_w2': 4.902,
     'L3_xattn_Wq': 2.72,
     'L3_xattn_w_kc_q': 2.726,
     'L3_xattn_W_qr': 2.732,
     'L3_xattn_W_kr': 2.727,
     'L3_ffn_w_gate': 2.925,
     'L3_ffn_w_up': 2.802,
     'L3_ffn_w_down': 2.807}
    for name, (base, spread) in spreads.items():
        noise = np.random.default_rng([zlib.crc32(name.encode()), seed]).standard_normal(out[name].shape)
        drawn = base * np.exp(spread * noise) if base else spread * noise
        out[name] = jnp.asarray(drawn.astype(out[name].dtype))
    for name, factor in factors.items():
        out[name] = (out[name] * factor).astype(out[name].dtype)
    return out
```

```python
from contextlib import ExitStack, contextmanager

import concourse.bass as bass
from concourse import mybir

ds = bass.ds
F32 = mybir.dt.float32
F32R = mybir.dt.float32r
I32 = mybir.dt.int32
ALU = mybir.AluOpType
ACT = mybir.ActivationFunctionType
AX = mybir.AxisListType

P = 128
B, S, D = 4, 512, 512
ST = S // P
KT = D // P
C = 128
TOPK = 153
TOP_ROUNDS = (TOPK - 1) // 8 + 1
L0_HEADS, L0_HEAD = 4, 32
HID = 2048
E, I = 8, 352
PAIR_TILES = 2 * B * ST + E - 1
NT = PAIR_TILES + 1
TW = NT + 2
EK = 3
QH, HD = 32, 16
KVH = 8
LH, LK, LQ, LR = 16, 128, 384, 64
EPS_BLOCK, EPS_INNER = 1e-5, 1e-6
K_STEPS = 4
UG = 4
AREA = 33200
FFN_AREA = AREA - 4 * 1536 - 2 * S - 4 * S


class Count:

    def __init__(self):
        self.base, self.k, self.odd, self.turn = 0, 0, 0, 0

    def bank(self):
        assert self.turn % 2 == 0, self.turn
        return (self.odd + self.k) % 2

    def now(self):
        return self.base + self.k

    def step(self, n=1):
        self.k += n
        return self.base + self.k


@contextmanager
def loop(eng, times, *counts):
    begun = [(c.base, c.k, c.odd, c.turn) for c, _ in counts]
    with eng.Fori(0, times) as i:
        for (c, n), (base, k, odd, _) in zip(counts, begun):
            c.base, c.k, c.odd, c.turn = i * n + (base + k), 0, (odd + k) % 2, n
        yield i
        for c, n in counts:
            assert c.k == n, (c.k, n)
    for (c, n), (base, k, odd, turn) in zip(counts, begun):
        c.base, c.k, c.odd, c.turn = base, k + times * n, odd, turn


class Ring:

    def __init__(self, banks, full, free):
        self.banks, self.full, self.free, self.depth = banks, full, free, banks.shape[1]


def flamingo(nc, x, ctx_n, ctx_t, gates, gamma_raw, ident, l0_wq, l0_wk, hadamard, l0_w13, l0_w2, l1_wk, l1_bk, l1_bk_row,
             l1_ln, l1_rows, l1_inrows, l1_cols, l1_agg, l1_d1, l1_d2, l1_bc, l1_gate, l2_router, l2_w12, l2_w2, moe_row, moe_tri, moe_token,
             l3_wq, l3_fold, rope_q, rope_k, l3_w13, l3_w2, out):
    ctx = ExitStack()
    with ctx:
        def sb(name, shape, dt=F32):
            return ctx.enter_context(nc.sbuf_tensor(name, shape, dt))

        def sem(name):
            return ctx.enter_context(nc.semaphore(name))

        X = sb("X", [P, B * ST, D])
        XN = sb("XN", [P, ST, D])
        XT = sb("XT", [P, 2, KT, S])
        ID = sb("ID", [P, P])
        STAT = sb("STAT", [P, ST, 6])
        MV = sb("MV", [P, ST, 2])
        VAR = sb("VAR", [P, ST])
        RSTD = sb("RSTD", [P, ST])
        HALF = sb("HALF", [P, ST])
        G = sb("G", [P, 8])
        GC = sb("GC", [P, 3])
        VAR1, RS1, NEGM1, SUM1 = [sb(n, [P, ST])[:, :] for n in ("VAR1", "RS1", "NEGM1", "SUM1")]
        AR = sb("AR", [P, AREA])

        def area(at=0):
            at = [at]

            def take(*shape):
                n = 1
                for s in shape:
                    n *= s
                v = AR[:, at[0]:at[0] + n]
                at[0] += n
                assert at[0] <= AREA, at[0]
                if len(shape) == 2:
                    v = v.rearrange("p (a b) -> p a b", b=shape[1])
                if len(shape) == 3:
                    v = v.rearrange("p (a b c) -> p a b c", b=shape[1], c=shape[2])
                return v
            take.here = lambda: at[0]
            return take

        BM = ctx.enter_context(nc.psum_tensor("BM", [P, 2, 512], F32))
        BR = ctx.enter_context(nc.psum_tensor("BR", [P, 2, 512], F32))
        BS = ctx.enter_context(nc.psum_tensor("BS", [P, 2, 512], F32))
        BT = ctx.enter_context(nc.psum_tensor("BT", [P, 2, 512], F32))

        def ring(banks, name):
            return Ring(banks, sem(name + "_full"), sem(name + "_free"))

        def rings(phase):
            return ring(BM, phase + "_m"), ring(BR, phase + "_r"), ring(BS, phase + "_s")

        turn = ring(BT, "turned")
        T_PE, T_ACT, T_V = Count(), Count(), Count()
        N_PE, N_V, N_P = Count(), Count(), Count()

        def start_job(pe, r, n):
            pe.wait_ge(r.free, n.now())
            bank = r.banks[:, n.bank() if r.depth == 2 else 0, :]
            n.step()
            return bank

        def full(eng, r, n):
            bank = r.banks[:, n.bank() if r.depth == 2 else 0, :]
            eng.wait_ge(r.full, n.step())
            return bank

        loaded = sem("loaded")
        consts = sem("consts")
        passed = sem("passed")
        g_ready = sem("g_ready")
        gc_ready = sem("gc_ready")
        vec = sem("vec")
        acts = sem("acts")
        V, A_ = Count(), Count()

        def hold(eng, s, value):
            eng.wait_ge(s, value)
            eng.sem_inc(passed, 1)

        def link(v, ins, alone=False):
            ins.then_inc(vec, 1)
            (hold if alone else lambda e, s, n: e.wait_ge(s, n))(v, vec, V.step())

        norm_stats, norm_aggr = sem("norm_stats"), sem("norm_aggr")
        norm_var, norm_rstd, xn_ready = sem("norm_var"), sem("norm_rstd"), sem("xn_ready")
        x_done = sem("x_done")

        def norm_vector(v, b):
            g = N_V.now()
            N_V.step()
            v.wait_ge(turn.free, T_V.now() + 1)
            for st in range(ST):
                last = nc.vector.bn_stats(STAT[:, st, :], X[:, ds(4 * b + st, 1), :])
            last.then_inc(norm_stats, 1)
            hold(v, norm_stats, g + 1)
            for st in range(ST):
                last = nc.vector.bn_aggr(MV[:, st, :], STAT[:, st, :])
            last.then_inc(norm_aggr, 1)
            v.wait_ge(norm_aggr, g + 1)
            nc.vector.tensor_scalar(VAR[:, :], MV[:, :, 1], EPS_BLOCK, None, ALU.add).then_inc(norm_var, 1)
            v.wait_ge(norm_rstd, g + 1)
            for st in range(ST):
                last = nc.vector.tensor_scalar(XN[:, st, :], X[:, ds(4 * b + st, 1), :].rearrange("p a n -> p (a n)"),
                                               MV[:, st, 0:1], RSTD[:, st:st + 1], ALU.subtract, ALU.mult)
            last.then_inc(xn_ready, 1)

        def norm_pool(pool):
            pool.wait_ge(norm_var, N_P.step())
            nc.gpsimd.tensor_tensor(RSTD[:, :], VAR[:, :], HALF[:, :], ALU.pow).then_inc(norm_rstd, 1)

        def norm_tensor(pe):
            pe.wait_ge(xn_ready, N_PE.step())
            for kt in range(KT):
                bank = start_job(pe, turn, T_PE)
                for st in range(ST):
                    last = nc.tensor.transpose(bank[:, st * P:(st + 1) * P], XN[:, st, kt * P:(kt + 1) * P], ID[:, :])
                last.then_inc(turn.full, 1)

        def norm_scalar(act, half):
            for kt in range(KT):
                bank = full(act, turn, T_ACT)
                nc.scalar.copy(XT[:, ds(half, 1), kt, :], bank.rearrange("p (a n) -> p a n", a=1)).then_inc(turn.free, 1)

        l0m, l0r, l0s = rings("l0")
        hadm = ring(BM, "had")
        HM_PE, HM_ACT = Count(), Count()
        a = area()
        WQ0, WK0 = a(C), a(C)
        QT0, KT0 = a(S), a(S)
        CT = a(B * S)
        SIM = a(ST, S)
        GRAPH = a(ST, S)
        WORK = a(2, S)
        TOP = a(ST, 8)
        HAD = a(P)
        WH = [a(HID // P, D), a(HID // P, D)]
        l0_w = sem("l0_w")
        graph_ready = sem("graph_ready")
        l0_had, butterflies = sem("l0_had"), sem("butterflies")
        wh_stored = sem("wh_stored")
        w2h = nc.dram_tensor("w2h", [HID // P // UG, P, UG * D], F32, kind="Internal").ap()

        def l0_tensor(pe):
            m, r, s = Count(), Count(), Count()
            pe.wait_ge(l0_w, 32)
            with loop(pe, B, (m, 2), (r, 4), (s, 4), (T_PE, KT), (N_PE, 1)) as b:
                for w in (WQ0, WK0):
                    nc.tensor.matmul(start_job(pe, l0m, m), w, CT[:, ds(b * S, S)], start=True, stop=True).then_inc(l0m.full, 1)
                pe.wait_ge(l0m.free, m.now() + 1)
                for st in range(ST):
                    nc.tensor.matmul(start_job(pe, l0s, s), QT0[:, st * P:(st + 1) * P], KT0, start=True, stop=True)\
                      .then_inc(l0s.full, 1)
                pe.wait_ge(graph_ready, b * ST + ST)
                for j in range(ST):
                    bank = start_job(pe, l0r, r)
                    for i in range(ST):
                        last = nc.tensor.transpose(bank[:, i * P:(i + 1) * P], GRAPH[:, i, j * P:(j + 1) * P], ID[:, :])
                    last.then_inc(l0r.full, 1)
                norm_tensor(pe)

        def had_tensor(pe):
            m = HM_PE
            pe.wait_ge(butterflies, 8)
            pe.wait_ge(l0_had, 32)
            for t in range(HID // P):
                nc.tensor.matmul(start_job(pe, hadm, m), HAD, WH[0][:, t, :], start=True, stop=True).then_inc(hadm.full, 1)

        def had_scalar(act):
            m = HM_ACT
            for t in range(HID // P):
                nc.scalar.activation(WH[1][:, t, :], full(act, hadm, m), ACT.Copy, scale=float(HID ** -0.5)).then_inc(hadm.free, 1)

        def had_pool(pool):
            pool.wait_ge(l0_had, 32)
            n = 0
            for stage in range(4):
                w = 1 << stage
                of, to = WH[stage % 2], WH[1 - stage % 2]
                of = of.rearrange("p (g two w) d -> p g two (w d)", two=2, w=w)
                to = to.rearrange("p (g two w) d -> p g two (w d)", two=2, w=w)
                if stage:
                    pool.wait_ge(butterflies, n)
                for half, op in ((0, ALU.add), (1, ALU.subtract)):
                    nc.gpsimd.tensor_tensor(to[:, :, half, :], of[:, :, 0, :], of[:, :, 1, :], op).then_inc(butterflies, 1)
                    n += 1

        def l0_scalar(act):
            m, s = Count(), Count()
            act.sem_inc(l0m.free, 1)
            act.sem_inc(l0s.free, 1)
            with loop(act, B, (m, 2), (s, 4), (T_ACT, KT)) as b:
                for dst in (QT0, KT0):
                    nc.scalar.copy(dst, full(act, l0m, m)).then_inc(l0m.free, 1)
                act.wait_ge(graph_ready, b * ST)
                for st in range(ST):
                    bank = full(act, l0s, s)
                    nc.scalar.activation(SIM[:, st, :], bank, ACT.Copy, scale=float(1.0 / (L0_HEAD ** 0.5 * L0_HEADS)))
                    nc.scalar.activation(GRAPH[:, st, :], bank, ACT.Sigmoid, scale=float(1.0 / (L0_HEAD ** 0.5 * L0_HEADS)))\
                      .then_inc(l0s.free, 1)
                norm_scalar(act, (b + 1) & 1)

        def l0_vector(v):
            r = Count()
            v.sem_inc(l0r.free, 1)
            v.wait_ge(gc_ready, 1)
            steps = 2 * TOP_ROUNDS - 1
            with loop(v, B, (r, 4), (V, ST + ST * steps + ST), (T_V, KT), (N_V, 1)) as b:
                xb = [X[:, ds(b * ST + st, 1), :].rearrange("p a n -> p (a n)") for st in range(ST)]
                v.wait_ge(xn_ready, b + 1)
                for st in range(ST):
                    last = nc.vector.scalar_tensor_tensor(out=xb[st], in0=XN[:, st, :], scalar=GC[:, 1:2], in1=xb[st],
                                                          op0=ALU.mult, op1=ALU.add)
                    last.then_inc(vec, 1)
                    V.step()
                for st in range(ST):
                    hold(v, l0s.free, b * ST + st + 2)
                    for t in range(TOP_ROUNDS):
                        link(v, nc.vector.max(TOP[:, st, :], SIM[:, st, :] if t == 0 else WORK[:, st % 2, :]), t < TOP_ROUNDS - 1)
                        if t < TOP_ROUNDS - 1:
                            link(v, nc.vector.match_replace(WORK[:, st % 2, :], TOP[:, st, :],
                                                            SIM[:, st, :] if t == 0 else WORK[:, st % 2, :], -3.0e38), True)
                    at = (TOPK - 1) % 8
                    nc.vector.scalar_tensor_tensor(out=GRAPH[:, st, :], in0=SIM[:, st, :], scalar=TOP[:, st, at:at + 1],
                                                   in1=GRAPH[:, st, :], op0=ALU.is_ge, op1=ALU.mult).then_inc(graph_ready, 1)
                v.wait_ge(graph_ready, b * ST + ST)
                for st in range(ST):
                    link(v, nc.vector.scalar_tensor_tensor(out=xb[st], in0=GRAPH[:, st, :], scalar=GC[:, 2:3], in1=xb[st],
                                                           op0=ALU.mult, op1=ALU.add))
                for st in range(ST):
                    bank = full(v, l0r, r)
                    nc.vector.scalar_tensor_tensor(out=xb[st], in0=bank, scalar=GC[:, 2:3], in1=xb[st],
                                                   op0=ALU.mult, op1=ALU.add).then_inc(l0r.free, 1)
                v.wait_ge(l0r.free, r.now() + 1)
                v.sem_inc(x_done, 1)
                norm_vector(v, (b + 1) & 3)
                T_V.step(KT)


        class Ffn:

            def __init__(self, name, phase, w13, w2, units, groups, per_turn, scale, after=()):
                self.phase, self.w13, self.w2, self.after = phase, w13, w2, after
                self.units, self.groups, self.per_turn, self.scale = units, groups, per_turn, scale
                self.m, self.r, self.s = rings(name)
                self.up_in = [sem(f"{name}_up_in{u}") for u in range(units)]
                self.down_in = sem(f"{name}_down_in")
                a = area(FFN_AREA)
                self.UP = a(units, 2 * KT * P)
                self.DOWN = a(units, D)
                self.SILU = a(2, S)
                self.HIDDEN = a(units, S)

        def ffn_sync(sp, f, begin):
            def up(u, n):
                sp.dma_start(f.UP[:, u, :], f.w13[ds(n, 1)].rearrange("a p n -> p (a n)")).then_inc(f.up_in[u], 16)

            def down(n):
                sp.dma_start(f.DOWN[:, :, :], f.w2[ds(n, 1)].rearrange("a p (u n) -> p (a u) n", u=f.units)).then_inc(f.down_in, 16)

            begin(sp)
            for u in range(f.units):
                up(u, u)
            for wait, n in f.after:
                sp.wait_ge(wait, n)
            down(0)
            with sp.Fori(1, B * f.groups) as g:
                for u in range(f.units):
                    sp.wait_ge(f.r.full, g * f.units - f.units + u + 1)
                    up(u, (g % f.groups) * f.units + u)
                sp.wait_ge(f.s.full, g * ST)
                down(g % f.groups)

        def ffn_tensor(pe, f):
            m, r, s, n_in = Count(), Count(), Count(), Count()
            with loop(pe, B, (m, f.groups * f.units), (r, f.groups * f.units), (s, f.groups * ST), (n_in, f.groups), (T_PE, KT), (N_PE, 1)) as b:
                hold(pe, turn.free, T_PE.now() + 1)
                with loop(pe, f.groups // f.per_turn, (m, f.units * f.per_turn), (r, f.units * f.per_turn),
                          (s, ST * f.per_turn), (n_in, f.per_turn)):
                    for _ in range(f.per_turn):
                        n_in.step()
                        hidden = r.now() + 2
                        for u in range(f.units):
                            pe.wait_ge(f.up_in[u], n_in.now() * 16)
                            w = f.UP[:, u, :].rearrange("p (k a n) -> p k a n", k=KT, a=2)
                            for a, (job, n) in enumerate(((f.m, m), (f.r, r))):
                                bank = start_job(pe, job, n)
                                for kt in range(KT):
                                    last = nc.tensor.matmul(bank.rearrange("p (a n) -> p a n", a=1), w[:, kt, a, :],
                                                            XT[:, ds(b & 1, 1), kt, :], start=kt == 0, stop=kt == KT - 1)
                                last.then_inc(job.full, 1)
                        pe.wait_ge(f.down_in, n_in.now() * 16)
                        for pair in range(ST // 2):
                            banks = [start_job(pe, f.s, s) for _ in range(2)]
                            for u in range(f.units):
                                if pair == 0:
                                    pe.wait_ge(f.r.free, hidden + u)
                                for j, bank in enumerate(banks):
                                    st = 2 * pair + j
                                    last = nc.tensor.matmul(bank, f.HIDDEN[:, u, st * P:(st + 1) * P], f.DOWN[:, u, :],
                                                            start=u == 0, stop=u == f.units - 1)
                                    if u == f.units - 1:
                                        last.then_inc(f.s.full, 1)
                norm_tensor(pe)

        def ffn_scalar(act, f):
            m, r = Count(), Count()
            act.sem_inc(f.m.free, 1)
            with loop(act, B, (m, f.groups * f.units), (r, f.groups * f.units), (T_ACT, KT)) as b:
                with loop(act, f.groups // f.per_turn, (m, f.units * f.per_turn), (r, f.units * f.per_turn)):
                    for _ in range(f.per_turn * f.units):
                        act.wait_ge(f.r.free, r.now())
                        bank = full(act, f.m, m)
                        nc.scalar.activation(f.SILU[:, r.bank(), :], bank, ACT.Silu).then_inc(f.m.free, 1)
                        r.step()
                norm_scalar(act, (b + 1) & 1)

        def ffn_vector(v, f):
            m, r, s = Count(), Count(), Count()
            v.sem_inc(f.r.free, 1)
            v.sem_inc(f.s.free, 1)
            with loop(v, B, (m, f.groups * f.units), (r, f.groups * f.units), (s, f.groups * ST), (T_V, KT), (N_V, 1)) as b:
                norm_vector(v, (b + 1) & 3)
                T_V.step(KT)
                with loop(v, f.groups // f.per_turn, (m, f.units * f.per_turn), (r, f.units * f.per_turn),
                          (s, ST * f.per_turn)) as turn_:
                    for q in range(f.per_turn):
                        for u in range(f.units):
                            v.wait_ge(f.m.free, m.step() + 1)
                            silu = f.SILU[:, r.bank(), :]
                            bank = full(v, f.r, r)
                            nc.vector.tensor_tensor(f.HIDDEN[:, u, :], silu, bank, ALU.mult).then_inc(f.r.free, 1)
                        for st in range(ST):
                            bank = full(v, f.s, s)
                            xb = X[:, ds(b * ST + st, 1), :].rearrange("p a n -> p (a n)")
                            nc.vector.scalar_tensor_tensor(out=xb, in0=bank, scalar=f.scale(b, turn_ * f.per_turn + q, st), in1=xb,
                                                           op0=ALU.mult, op1=ALU.add).then_inc(f.s.free, 1)
                v.wait_ge(f.s.free, s.now() + 1)
                v.sem_inc(x_done, 1)

        l0f = Ffn("l0f", 1, l0_w13, w2h, UG, HID // P // UG, 1, lambda b, g, st: G[:, 4:5], ((wh_stored, 16),))

        l1m, l1r, l1s = rings("l1")
        a = area(FFN_AREA)
        WK1, CTB, KVT1, OUT1 = a(C), a(S), a(S), a(S)
        CT1 = a(B * S)
        KV1 = a(ST, C)
        PROB1 = a(ST, S)
        ROWS1 = a(2, S)
        BKR, BK1 = a(C), a(1)
        l1_w, ctb_ready = sem("l1_w"), sem("ctb_ready")
        var1_ready, root1_ready, norm1_ready, exp1_done, prob1_used = [sem(n) for n in (
            "var1_ready", "root1_ready", "norm1_ready", "exp1_done", "prob1_used")]

        def l1_sync(sp):
            sp.wait_ge(x_done, 2 * B)
            sp.dma_start(WK1, l1_wk).then_inc(l1_w, 16)
            sp.dma_start(CT1, ctx_t).then_inc(l1_w, 16)
            sp.dma_start(BK1, l1_bk).then_inc(l1_w, 16)
            sp.dma_start(BKR, l1_bk_row.to_broadcast([P, C])).then_inc(l1_w, 16)
            sp.dma_start(ROWS1, l1_ln.rearrange("(o a) n -> o a n", o=1).to_broadcast([P, 2, S])).then_inc(l1_w, 16)

        def l1_tensor(pe):
            m, r, s = Count(), Count(), Count()
            pe.wait_ge(x_done, 2 * B)
            pe.wait_ge(l1_w, 80)
            with loop(pe, B, (m, 2), (r, 1 + 1), (s, ST), (T_PE, KT), (N_PE, 1)) as b:
                hold(pe, turn.free, T_PE.now() + 1)
                hold(pe, ctb_ready, b + 1)
                nc.tensor.matmul(start_job(pe, l1m, m), WK1, CTB, start=True, stop=True).then_inc(l1m.full, 1)
                for half in range(2):
                    bank = start_job(pe, l1r, r)
                    for j in range(2):
                        jt = 2 * half + j
                        last = nc.tensor.matmul(bank[:, j * C:(j + 1) * C], CTB[:, jt * P:(jt + 1) * P], WK1, start=True, stop=True)
                    last.then_inc(l1r.full, 1)
                hold(pe, l1r.free, r.now() + 1)
                bank = start_job(pe, l1m, m)
                for jt in range(ST):
                    last = nc.tensor.matmul(bank.rearrange("p (a n) -> p a n", a=1), KV1[:, jt, :], XT[:, ds(b & 1, 1), jt, :],
                                            start=jt == 0, stop=jt == ST - 1)
                last.then_inc(l1m.full, 1)
                pe.wait_ge(l1m.free, m.now() + 1)
                for st in range(ST):
                    nc.tensor.matmul(start_job(pe, l1s, s), OUT1[:, st * P:(st + 1) * P], KVT1, start=True, stop=True)\
                      .then_inc(l1s.full, 1)
                norm_tensor(pe)

        def l1_scalar(act):
            m, s = Count(), Count()
            act.sem_inc(l1m.free, 1)
            act.sem_inc(l1s.free, 1)
            with loop(act, B, (m, 2), (s, ST), (T_ACT, KT)) as b:
                nc.scalar.activation(KVT1, full(act, l1m, m), ACT.Identity, bias=BK1).then_inc(l1m.free, 1)
                nc.scalar.copy(OUT1, full(act, l1m, m)).then_inc(l1m.free, 1)
                act.wait_ge(prob1_used, b)
                for st in range(ST):
                    nc.scalar.copy(PROB1[:, st, :], full(act, l1s, s)).then_inc(l1s.free, 1)
                norm_scalar(act, (b + 1) & 1)
                act.wait_ge(norm1_ready, b + 1)
                for st in range(ST):
                    nc.scalar.activation(PROB1[:, st, :], PROB1[:, st, :], ACT.Exp, bias=NEGM1[:, st:st + 1],
                                         accum_out=SUM1[:, st:st + 1]).then_inc(exp1_done, 1)

        def l1_vector(v):
            r, s = Count(), Count()
            v.sem_inc(l1r.free, 1)
            v.wait_ge(l1_w, 80)
            scale = float(512 ** -0.5)
            with loop(v, B, (r, 2), (s, ST), (V, 2 * ST - 1 + 7), (T_V, KT), (N_V, 1)) as b:
                for half in range(2):
                    bank = full(v, l1r, r)
                    nc.vector.tensor_tensor(KV1[:, 2 * half:2 * half + 2, :], bank[:, 0:2 * C].rearrange("p (j c) -> p j c", j=2),
                                            BKR.rearrange("p (a c) -> p a c", a=1).to_broadcast([P, 2, C]), ALU.add)\
                      .then_inc(l1r.free, 1)
                norm_vector(v, (b + 1) & 3)
                T_V.step(KT)
                for st in range(ST):
                    s.step()
                    hold(v, l1s.free, s.now() + 1)
                    nc.vector.bn_stats(STAT[:, st, :], PROB1[:, st, :]).then_inc(vec, 1)
                    V.step()
                hold(v, vec, V.now())
                for st in range(ST):
                    last = nc.vector.bn_aggr(MV[:, st, :], STAT[:, st, :])
                link(v, last)
                nc.vector.tensor_scalar(VAR1, MV[:, :, 1], scale * scale, EPS_INNER, ALU.mult, ALU.add).then_inc(var1_ready, 1)
                v.wait_ge(root1_ready, b + 1)
                link(v, nc.vector.tensor_scalar(RS1, RS1, scale, None, ALU.mult))
                for st in range(ST):
                    last = nc.vector.tensor_scalar(PROB1[:, st, :], PROB1[:, st, :], MV[:, st, 0:1], RS1[:, st:st + 1],
                                                   ALU.subtract, ALU.mult)
                link(v, last)
                for row, op in ((0, ALU.mult), (1, ALU.add)):
                    link(v, nc.vector.tensor_tensor(PROB1, PROB1, ROWS1[:, row:row + 1, :].to_broadcast([P, ST, S]), op))
                nc.vector.tensor_reduce(NEGM1, PROB1, op=ALU.max, axis=AX.X, negate=True).then_inc(norm1_ready, 1)
                v.wait_ge(exp1_done, b * ST + ST)
                link(v, nc.vector.reciprocal(SUM1, SUM1))
                link(v, nc.vector.tensor_scalar(SUM1, SUM1, G[:, 1:2], None, ALU.mult))
                for st in range(ST):
                    xb = X[:, ds(b * ST + st, 1), :].rearrange("p a n -> p (a n)")
                    last = nc.vector.scalar_tensor_tensor(out=xb, in0=PROB1[:, st, :], scalar=SUM1[:, st:st + 1], in1=xb,
                                                          op0=ALU.mult, op1=ALU.add)
                    if st < ST - 1:
                        last.then_inc(vec, 1)
                        V.step()
                last.then_inc(prob1_used, 1)
                v.wait_ge(prob1_used, b + 1)
                v.sem_inc(x_done, 1)

        def l1_pool(pool):
            pool.wait_ge(l1_w, 80)
            with loop(pool, B, (N_P, 1)) as b:
                pool.wait_ge(l1r.full, b * 2)
                nc.gpsimd.tensor_copy(CTB, CT1[:, ds(b * S, S)]).then_inc(ctb_ready, 1)
                norm_pool(pool)
                pool.wait_ge(var1_ready, b + 1)
                nc.gpsimd.tensor_tensor(RS1, VAR1, HALF[:, :], ALU.pow).then_inc(root1_ready, 1)

        la, lr, ls = rings("l1f")
        a = area()
        AGG, D1, D2, BC, GATE = a(KT, D), a(KT, HID), a(HID // P, D), a(KT, D), a(KT, D)
        COLS = a(40)
        COL = {}
        for name, n in (("agg", 4), ("d1", 16), ("d2", 4), ("bc", 4), ("gate", 4), ("pn_g", 4), ("pn_b", 4)):
            COL[name] = COLS[:, sum(c[1] for c in COL.values()):sum(c[1] for c in COL.values()) + n], n
        COL = {k: c[0] for k, c in COL.items()}
        OROWS = a(2, D)
        TH, TC, TN, SQ, BCT, T0 = a(4 * B), a(4 * B), a(4 * B), a(4 * B), a(4 * B), a(4 * B)
        HP, GL = a(16 * B), a(16 * B)
        MU, VT, RT = a(B), a(B), a(B)
        MEAN = a(P)
        assert FFN_AREA >= 22528 + 40 + 1024 + 96 + 128 + 12 + P
        a = area(FFN_AREA)
        GT, OT, ON = a(KT, S), a(KT, S), a(ST, D)
        XL, INR = a(D), a(2, D)
        SL, ML, VL, RL = a(6), a(2), a(1), a(1)
        l1f_w, l1f_in, xl_in = sem("l1f_w"), sem("l1f_in"), sem("xl_in")
        th_ready, root_in, root_out = sem("th_ready"), sem("root_in"), sem("root_out")
        gelu_done, mix_done, out_norm = sem("gelu_done"), sem("mix_done"), sem("out_norm")
        t0_done = sem("t0_done")
        ROOTS = 2 + K_STEPS

        def l1f_sync_weights(sp):
            for dst, src in ((AGG, l1_agg), (D1, l1_d1), (D2, l1_d2), (BC, l1_bc), (GATE, l1_gate), (COLS, l1_cols)):
                sp.dma_start(dst, src).then_inc(l1f_w, 16)
            sp.dma_start(OROWS, l1_rows.rearrange("(o a) n -> o a n", o=1).to_broadcast([P, 2, D])).then_inc(l1f_w, 16)

        def l1f_sync(sp):
            sp.wait_ge(x_done, 3 * B)
            for b in range(B):
                sp.dma_start(XL[b:b + 1, :], X[P - 1:P, b * ST + ST - 1, :]).then_inc(xl_in, 16)
            sp.dma_start(INR[0:B, :, :], l1_inrows.rearrange("(o a) n -> o a n", o=1).to_broadcast([B, 2, D])).then_inc(xl_in, 16)

        def cols(t):
            return t.rearrange("p (m b) -> p m b", b=B)

        def over_b(col, n):
            return col.rearrange("p (m o) -> p m o", o=1).to_broadcast([P, n, B])

        def over_m(t):
            return t.rearrange("p (o b) -> p o b", o=1).to_broadcast([P, 4, B])

        def small_products(pe, n, w, of, tiles_in, tiles_out):
            bank = start_job(pe, lr, n)
            for mt in range(tiles_out):
                for kt in range(tiles_in):
                    last = nc.tensor.matmul(bank[:, mt * B:(mt + 1) * B], w[:, kt, mt * P:(mt + 1) * P], of[:, kt * B:(kt + 1) * B],
                                            start=kt == 0, stop=kt == tiles_in - 1)
            last.then_inc(lr.full, 1)

        def l1f_tensor(pe):
            m, r, s, th, gl = Count(), Count(), Count(), Count(), Count()
            pe.wait_ge(x_done, 3 * B)
            pe.wait_ge(l1f_w, 7 * 16)
            pe.wait_ge(th_ready, th.step())
            bank = start_job(pe, la, m)
            for kt in range(KT):
                last = nc.tensor.transpose(bank[:, kt * B:(kt + 1) * B], XL[0:B, kt * P:(kt + 1) * P], ID[0:B, 0:B])
            last.then_inc(la.full, 1)
            pe.wait_ge(la.free, m.now() + 1)
            small_products(pe, r, AGG, T0, KT, KT)
            pe.wait_ge(th_ready, th.step())
            with loop(pe, K_STEPS, (r, 4), (th, 3), (gl, 1)):
                nc.tensor.matmul(start_job(pe, lr, r)[:, 0:4 * B], MEAN, TH, start=True, stop=True).then_inc(lr.full, 1)
                hold(pe, th_ready, th.step())
                nc.tensor.matmul(start_job(pe, lr, r)[:, 0:4 * B], MEAN, SQ, start=True, stop=True).then_inc(lr.full, 1)
                hold(pe, th_ready, th.step())
                small_products(pe, r, D1, TN, KT, HID // P)
                hold(pe, gelu_done, gl.step())
                small_products(pe, r, D2, GL, HID // P, KT)
                hold(pe, th_ready, th.step())
            small_products(pe, r, BC, TH, KT, KT)
            m.step()
            bank = BM[:, 1, :]
            nc.tensor.matmul(bank[:, 0:P], ID[:, :], ID[:, :], start=True, stop=True).then_inc(la.full, 1)
            with loop(pe, B, (m, KT), (s, ST), (T_PE, KT), (N_PE, 1)) as b:
                hold(pe, turn.free, T_PE.now() + 1)
                for mt in range(KT):
                    bank = start_job(pe, la, m)
                    for kt in range(KT):
                        last = nc.tensor.matmul(bank.rearrange("p (a n) -> p a n", a=1), GATE[:, kt, mt * P:(mt + 1) * P],
                                                XT[:, ds(b & 1, 1), kt, :], start=kt == 0, stop=kt == KT - 1)
                    last.then_inc(la.full, 1)
                for st in range(ST):
                    if st == 0:
                        hold(pe, mix_done, b * KT + KT)
                    bank = start_job(pe, ls, s)
                    for mt in range(KT):
                        last = nc.tensor.transpose(bank[:, mt * P:(mt + 1) * P], OT[:, mt, st * P:(st + 1) * P], ID[:, :])
                    last.then_inc(ls.full, 1)
                norm_tensor(pe)

        def l1f_scalar(act):
            m, s = Count(), Count()
            act.sem_inc(la.free, 1)
            act.sem_inc(ls.free, 1)
            nc.scalar.copy(T0, full(act, la, m)[:, 0:4 * B]).then_inc(la.free, 1)
            with act.Fori(0, K_STEPS) as k:
                act.wait_ge(t0_done, k + 1)
                nc.scalar.activation(GL, HP, ACT.Gelu).then_inc(gelu_done, 1)
            nc.scalar.copy(T0[:, 0:1], full(act, la, m)[:, 0:1]).then_inc(la.free, 1)
            with loop(act, B, (m, KT), (s, ST), (T_ACT, KT)) as b:
                act.wait_ge(mix_done, b * KT)
                for mt in range(KT):
                    nc.scalar.activation(GT[:, mt, :], full(act, la, m), ACT.Sigmoid, bias=COL["gate"][:, mt:mt + 1]).then_inc(la.free, 1)
                act.wait_ge(out_norm, b * 2)
                for st in range(ST):
                    nc.scalar.copy(ON[:, st, :], full(act, ls, s)).then_inc(ls.free, 1)
                norm_scalar(act, (b + 1) & 1)

        def l1f_vector(v):
            m, r, s, t0, root = Count(), Count(), Count(), Count(), Count()
            v.sem_inc(lr.free, 1)
            v.wait_ge(l1f_w, 7 * 16)
            nc.vector.memset(MEAN, 1.0 / D).then_inc(vec, 1)
            V.step()
            link(v, nc.vector.tensor_scalar(OROWS, OROWS, G[:, 5:6], None, ALU.mult))
            v.wait_ge(xl_in, 5 * 16)
            for eps in (EPS_BLOCK, EPS_INNER):
                link(v, nc.vector.bn_stats(SL[0:B, :], XL[0:B, :]))
                link(v, nc.vector.bn_aggr(ML[0:B, :], SL[0:B, :]))
                nc.vector.tensor_scalar(VL[0:B, :], ML[0:B, 1:2], eps, None, ALU.add).then_inc(root_in, 1)
                v.wait_ge(root_out, root.step())
                link(v, nc.vector.tensor_scalar(XL[0:B, :], XL[0:B, :], ML[0:B, 0:1], RL[0:B, :], ALU.subtract, ALU.mult))
            link(v, nc.vector.tensor_tensor(XL[0:B, :], XL[0:B, :], INR[0:B, 0, :], ALU.mult))
            nc.vector.tensor_tensor(XL[0:B, :], XL[0:B, :], INR[0:B, 1, :], ALU.add).then_inc(th_ready, 1)
            bank = full(v, lr, r)
            nc.vector.tensor_tensor(cols(TH), cols(bank[:, 0:4 * B]), over_b(COL["agg"], 4), ALU.add).then_inc(lr.free, 1)
            v.wait_ge(lr.free, r.now() + 1)
            v.sem_inc(th_ready, 1)
            with loop(v, K_STEPS, (r, 4), (V, 7), (t0, 1), (root, 1)):
                bank = full(v, lr, r)
                link(v, nc.vector.tensor_reduce(MU, bank[:, 0:4 * B].rearrange("p (m b) -> p b m", b=B), op=ALU.add, axis=AX.X))
                link(v, nc.vector.tensor_tensor(cols(TC), cols(TH), over_m(MU), ALU.subtract))
                nc.vector.tensor_tensor(SQ, TC, TC, ALU.mult).then_inc(lr.free, 1)
                v.wait_ge(lr.free, r.now() + 1)
                v.sem_inc(th_ready, 1)
                bank = full(v, lr, r)
                link(v, nc.vector.tensor_reduce(MU, bank[:, 0:4 * B].rearrange("p (m b) -> p b m", b=B), op=ALU.add, axis=AX.X))
                nc.vector.tensor_scalar(VT, MU, EPS_INNER, None, ALU.add).then_inc(root_in, 1)
                v.wait_ge(root_out, root.step())
                link(v, nc.vector.tensor_tensor(cols(TC), cols(TC), over_m(RT), ALU.mult))
                link(v, nc.vector.tensor_tensor(cols(TC), cols(TC), over_b(COL["pn_g"], 4), ALU.mult))
                nc.vector.tensor_tensor(cols(TN), cols(TC), over_b(COL["pn_b"], 4), ALU.add).then_inc(lr.free, 1)
                v.wait_ge(lr.free, r.now() + 1)
                v.sem_inc(th_ready, 1)
                bank = full(v, lr, r)
                nc.vector.tensor_tensor(cols(HP), cols(bank[:, 0:16 * B]), over_b(COL["d1"], 16), ALU.add).then_inc(lr.free, 1)
                v.wait_ge(lr.free, r.now() + 1)
                v.sem_inc(t0_done, 1)
                t0.step()
                bank = full(v, lr, r)
                link(v, nc.vector.tensor_tensor(cols(TC), cols(bank[:, 0:4 * B]), over_b(COL["d2"], 4), ALU.add))
                nc.vector.tensor_tensor(TH, TH, TC, ALU.add).then_inc(lr.free, 1)
                v.wait_ge(lr.free, r.now() + 1)
                v.sem_inc(th_ready, 1)
                V.step()
                v.sem_inc(vec, 1)
            bank = full(v, lr, r)
            nc.vector.tensor_tensor(cols(BCT), cols(bank[:, 0:4 * B]), over_b(COL["bc"], 4), ALU.add).then_inc(lr.free, 1)
            v.wait_ge(lr.free, r.now() + 1)
            m.step(2)
            with loop(v, B, (m, KT), (s, ST), (V, ST + 1 + 1 + 2), (T_V, KT), (N_V, 1), (root, 1)) as b:
                norm_vector(v, (b + 1) & 3)
                T_V.step(KT)
                for mt in range(KT):
                    m.step()
                    v.wait_ge(la.free, m.now() + 1)
                    one = lambda t: t.rearrange("p (a n) -> p a n", a=1)
                    nc.vector.scalar_tensor_tensor(out=one(OT[:, mt, :]), in0=one(GT[:, mt, :]), scalar=BCT[:, ds(mt * B + b, 1)],
                                                   in1=XT[:, ds(b & 1, 1), mt, :], op0=ALU.mult, op1=ALU.add).then_inc(mix_done, 1)
                for st in range(ST):
                    s.step()
                    hold(v, ls.free, s.now() + 1)
                    nc.vector.bn_stats(STAT[:, st, :], ON[:, st, :]).then_inc(vec, 1)
                    V.step()
                hold(v, vec, V.now())
                for st in range(ST):
                    last = nc.vector.bn_aggr(MV[:, st, :], STAT[:, st, :])
                link(v, last)
                nc.vector.tensor_scalar(VAR1, MV[:, :, 1], EPS_INNER, None, ALU.add).then_inc(root_in, 1)
                v.wait_ge(root_out, root.step())
                for st in range(ST):
                    last = nc.vector.tensor_scalar(ON[:, st, :], ON[:, st, :], MV[:, st, 0:1], RS1[:, st:st + 1],
                                                   ALU.subtract, ALU.mult)
                link(v, last)
                link(v, nc.vector.tensor_tensor(ON, ON, OROWS[:, 0:1, :].to_broadcast([P, ST, D]), ALU.mult))
                nc.vector.tensor_tensor(ON, ON, OROWS[:, 1:2, :].to_broadcast([P, ST, D]), ALU.add).then_inc(out_norm, 1)
                v.wait_ge(out_norm, b * 2 + 1)
                xb = X[:, ds(b * ST, ST), :]
                nc.vector.tensor_tensor(xb, xb, ON, ALU.add).then_inc(out_norm, 1)
                v.wait_ge(out_norm, b * 2 + 2)
                v.sem_inc(x_done, 1)
                v.sem_inc(vec, 1)
                V.step()

        def l1f_pool(pool):
            for n in range(2):
                pool.wait_ge(root_in, n + 1)
                nc.gpsimd.tensor_tensor(RL[0:B, :], VL[0:B, :], HALF[0:B, 0:1], ALU.pow).then_inc(root_out, 1)
            with pool.Fori(0, K_STEPS) as k:
                pool.wait_ge(root_in, k + 3)
                nc.gpsimd.tensor_tensor(RT, VT, HALF[:, 0:B], ALU.pow).then_inc(root_out, 1)
            with loop(pool, B, (N_P, 1)) as b:
                norm_pool(pool)
                pool.wait_ge(root_in, b + ROOTS + 1)
                nc.gpsimd.tensor_tensor(RS1, VAR1, HALF[:, :], ALU.pow).then_inc(root_out, 1)

        ar, as_ = ring(BR, "l2_r"), ring(BS, "l2_s")
        aq = Ring(BM[:, 0:1, :], sem("l2_q_full"), sem("l2_q_free"))
        ao = Ring(BM[:, 1:2, :], sem("l2_out_full"), sem("l2_out_free"))
        a = area()
        CN2 = a(B * ST, C)
        KRAW = a(KVH, S)
        QHI, QLO = a(ST, D), a(ST, D)
        QST = a(2, ST, P)
        PROB2, PROBT2 = a(ST, S), a(ST, S)
        VWIN = a(2 * ST, 240)
        OUT2, TMP2 = a(S), a(S)
        SUM2, RS2, NEG2 = a(ST * 8), a(ST * 8), a(2 * ST)
        KPARTS = sb("KPARTS", [P, KVH, S], F32R)
        QPARTS = sb("QPARTS", [P, 2, S], F32R)
        HG = QH // 8
        zeroed, kraw_in, cn2_in, kparts_ready, q_cut = [sem(n) for n in ("zeroed", "kraw_in", "cn2_in", "kparts_ready", "q_cut")]
        q_staged, v_staged, max_done, sums_used = [sem(n) for n in ("q_staged", "v_staged", "max_done", "sums_used")]

        def l2_sync(sp):
            sp.wait_ge(x_done, 4 * B)
            sp.dma_start(CN2, ctx_n.rearrange("(n p) d -> p n d", p=P)).then_inc(cn2_in, 16)
            sp.wait_ge(zeroed, 3)
            with sp.Fori(0, B) as b:
                sp.wait_ge(kparts_ready, b)
                for q in range(4):
                    sp.dma_start(KRAW[32 * q:32 * q + HD, :, :],
                                 ctx_t[:, ds(b * S, S)].rearrange("(k d) t -> d k t", d=HD)).then_inc(kraw_in, 16)

        def l2_tensor(pe):
            r, s, q, o, vs = Count(), Count(), Count(), Count(), Count()
            pe.wait_ge(x_done, 4 * B)

            def turn_queries(j):
                hold(pe, q_staged, q.now() + 1)
                bank = start_job(pe, aq, q)
                for st in range(ST):
                    last = nc.tensor.transpose(bank[:, st * P:(st + 1) * P], QST[:, j % 2, st, :], ID[:, :])
                last.then_inc(aq.full, 1)

            def mix_values(j, bank):
                hold(pe, turn.free, T_PE.now() + 1)
                hold(pe, ar.free, r.now() + 1)
                for lt in range(ST):
                    last = nc.tensor.matmul(bank, VWIN[:, (j // 4) * ST + lt, 112 - HD * j:240 - HD * j], PROBT2[:, lt, :],
                                            start=j == 0 and lt == 0, stop=j == 7 and lt == ST - 1)
                return last

            with loop(pe, B, (r, 2 * QH), (s, ST * QH), (q, QH), (o, 2 * HG), (T_PE, 2 * QH + KT), (N_PE, 1), (vs, HG)) as b:
                hold(pe, kparts_ready, b + 1)
                with loop(pe, HG, (r, 16), (s, ST * 8), (q, 8), (o, 2), (T_PE, 16), (vs, 1)) as hg:
                    turn_queries(0)
                    for j in range(8):
                        hold(pe, aq.free, q.now())
                        for st in range(ST):
                            nc.tensor.matmul(start_job(pe, as_, s).rearrange("p (a n) -> p a n", a=1),
                                             QPARTS[:, j % 2, st * P:(st + 1) * P], KPARTS[:, ds(hg * 2 + j // 4, 1), :],
                                             start=True, stop=True).then_inc(as_.full, 1)
                        if j == 1:
                            hold(pe, v_staged, vs.step())
                            out_bank = start_job(pe, ao, o)
                        if j:
                            mix_values(j - 1, out_bank)
                        if j < 7:
                            turn_queries(j + 1)
                        hold(pe, as_.free, s.now() + 1)
                        for lt in range(ST):
                            job, n = (turn, T_PE) if lt % 2 == 0 else (ar, r)
                            bank = start_job(pe, job, n)
                            for st in range(ST):
                                last = nc.tensor.transpose(bank[:, st * P:(st + 1) * P], PROB2[:, st, lt * P:(lt + 1) * P], ID[:, :])
                            last.then_inc(job.full, 1)
                    mix_values(7, out_bank).then_inc(ao.full, 1)
                    bank = start_job(pe, ao, o)
                    for st in range(ST):
                        last = nc.tensor.transpose(bank[:, st * P:(st + 1) * P], OUT2[:, st * P:(st + 1) * P], ID[:, :])
                    last.then_inc(ao.full, 1)
                norm_tensor(pe)

        def l2_scalar(act):
            s, q, o, grp = Count(), Count(), Count(), Count()
            act.sem_inc(as_.free, 1)
            with loop(act, B, (s, ST * QH), (q, QH), (o, 2 * HG), (T_ACT, 2 * QH + KT), (grp, HG)) as b:
                with loop(act, HG, (s, ST * 8), (q, 8), (o, 2), (T_ACT, 16), (grp, 1)) as hg:
                    def queries(j):
                        nc.scalar.copy(QPARTS[:, j % 2, :], full(act, aq, q)).then_inc(aq.free, 1)
                    queries(0)
                    act.wait_ge(sums_used, grp.now())
                    grp.step()
                    for j in range(8):
                        for st in range(ST):
                            act.wait_ge(max_done, s.now() + 1)
                            bank = full(act, as_, s)
                            nc.scalar.activation(PROB2[:, st, :], bank, ACT.Exp, bias=NEG2[:, (j % 2) * ST + st:(j % 2) * ST + st + 1],
                                                 accum_out=SUM2[:, st * 8 + j:st * 8 + j + 1]).then_inc(as_.free, 1)
                        if j < 7:
                            queries(j + 1)
                        for lt in (0, 2):
                            nc.scalar.copy(PROBT2[:, lt, :], full(act, turn, T_ACT)).then_inc(turn.free, 1)
                    nc.scalar.copy(OUT2, full(act, ao, o)).then_inc(ao.free, 1)
                    o.step()
                norm_scalar(act, (b + 1) & 1)

        def l2_vector(v):
            r, s, o = Count(), Count(), Count()
            v.sem_inc(ar.free, 1)
            with loop(v, B, (r, 2 * QH), (s, ST * QH), (o, 2 * HG), (V, 2 + 3 * HG), (T_V, 2 * QH + KT), (N_V, 1)) as b:
                v.wait_ge(kraw_in, b * 64 + 64)
                nc.vector.tensor_copy(KPARTS[0:64, :, :], KRAW[0:64, :, :])
                link(v, nc.vector.tensor_copy(KPARTS[64:128, :, :], KRAW[64:128, :, :]))
                nc.vector.tensor_tensor(KPARTS[64:128, :, :], KRAW[64:128, :, :], KPARTS[64:128, :, :].bitcast(F32), ALU.subtract)\
                  .then_inc(kparts_ready, 1)
                link(v, nc.vector.tensor_scalar(QHI.bitcast(F32R), XN[:, :, :], HD ** -0.5, None, ALU.mult))
                nc.vector.scalar_tensor_tensor(out=QLO, in0=XN[:, :, :], scalar=HD ** -0.5, in1=QHI, op0=ALU.mult, op1=ALU.subtract)\
                  .then_inc(q_cut, 1)
                v.wait_ge(q_cut, b + 1)
                norm_vector(v, (b + 1) & 3)
                with loop(v, HG, (r, 16), (s, ST * 8), (o, 2), (V, 3), (T_V, 16)) as hg:
                    for j in range(8):
                        for st in range(ST):
                            bank = full(v, as_, s)
                            nc.vector.tensor_reduce(NEG2[:, (j % 2) * ST + st:(j % 2) * ST + st + 1], bank, op=ALU.max, axis=AX.X,
                                                    negate=True).then_inc(max_done, 1)
                        for lt in (1, 3):
                            nc.vector.tensor_copy(PROBT2[:, lt, :], full(v, ar, r)).then_inc(ar.free, 1)
                        T_V.step(2)
                    hold(v, as_.free, s.now() + 1)
                    nc.vector.reciprocal(RS2, SUM2).then_inc(sums_used, 1)
                    v.wait_ge(sums_used, b * HG + hg + 1)
                    link(v, nc.vector.tensor_scalar(RS2, RS2, G[:, 2:3], None, ALU.mult))
                    o.step()
                    bank = full(v, ao, o)
                    link(v, nc.vector.tensor_tensor(TMP2.rearrange("p (a d) -> p a d", d=HD), bank.rearrange("p (a d) -> p a d", d=HD),
                                                    RS2.rearrange("p (a o) -> p a o", o=1).to_broadcast([P, ST * 8, HD]), ALU.mult))
                    v.sem_inc(ao.free, 1)
                    xb = X[:, ds(b * ST, ST), ds(hg * 8 * HD, 8 * HD)]
                    link(v, nc.vector.tensor_tensor(xb, xb, TMP2.rearrange("p (s n) -> p s n", s=ST), ALU.add))
                T_V.step(KT)
                v.sem_inc(x_done, 1)

        def l2_pool(pool):
            q, o = Count(), Count()
            pool.wait_ge(x_done, 4 * B)
            for t in (KRAW, QST, VWIN):
                nc.gpsimd.memset(t, 0.0).then_inc(zeroed, 1)
            pool.wait_ge(zeroed, 3)
            pool.wait_ge(cn2_in, 16)
            with loop(pool, B, (q, QH), (o, 2 * HG), (N_P, 1)) as b:
                pool.wait_ge(q_cut, b + 1)
                norm_pool(pool)
                with loop(pool, HG, (q, 8), (o, 2)) as hg:
                    def stage(j):
                        to = QST[:, j % 2, :, :].rearrange("p s (a two w) -> p s a two w", two=2, w=32)
                        for part, of in ((0, QHI), (1, QLO)):
                            src = of[:, :, ds(hg * 8 * HD + j * HD, HD)].rearrange("p s (a d) -> p s a d", a=1)
                            last = nc.gpsimd.tensor_copy(to[:, :, :, part, 0:HD], src.to_broadcast([P, ST, 2, HD]))
                        last.then_inc(q_staged, 1)
                    pool.wait_ge(aq.full, q.now())
                    for j in (0, 1):
                        stage(j)
                    pool.wait_ge(ao.full, o.now())
                    for u in range(2):
                        last = nc.gpsimd.tensor_copy(VWIN[:, u * ST:(u + 1) * ST, 112:128], CN2[:, ds(b * ST, ST), ds((hg * 2 + u) * HD, HD)])
                    last.then_inc(v_staged, 1)
                    for j in range(2, 8):
                        q.step()
                        pool.wait_ge(aq.full, q.now())
                        stage(j)
                    q.step(2)
                    o.step(2)

        xnd = nc.dram_tensor("xnd", [B * S, D], F32, kind="Internal").ap()
        table = nc.dram_tensor("table", [P * TW, 1], I32, kind="Internal").ap()
        made = nc.dram_tensor("made", [NT * P, D], F32, kind="Internal").ap()
        em, er, es = rings("l2f")
        et = ring(BT, "l2f_t")
        a = area()
        EW1 = a(E * KT, 2 * I)
        EW2 = a(2, EK * D)
        XG, XGT = a(2, D), a(2, KT * P)
        EHT = a(2, EK * P)
        RW = a(KT, E)
        TRI, ONE = a(P), a(P)
        EC = a(E + 16 + TW)
        TOK = a(B * ST).bitcast(I32)
        n128 = B * ST * E
        MX0, MX1, MS, EX, WT0, WT1, POS0, POS1 = [a(B * ST) for _ in range(8)]
        IDX0, IDX1, YP0, YP1 = [a(B * ST).bitcast(I32) for _ in range(4)]
        NTL, END0, END1, START = a(E), a(E), a(E), a(E)
        EXF = a(TW)
        EXPERT, SLOTS = a(TW).bitcast(I32), a(TW).bitcast(I32)
        IX = [a(1).bitcast(I32) for _ in range(2)]
        here = a.here()
        a, a2 = area(here), area(here)
        LG, LG2, EQ, OH0, OH1, OHS, RANK, TOTAL, SCAN0, SCAN1 = [a(B * ST, E) for _ in range(10)]
        CMP, LT = a(TW, E), a(S)
        ESILU, EHID, YE = a2(2, I), a2(2, I), a2(2, D)
        YG = [XG[:, 0, :], XG[:, 1, :], XGT[:, 0, :], XGT[:, 1, :]]
        ew_in, xnd_in, router_in = sem("ew_in"), sem("xnd_in"), sem("router_in")
        pair_exp_in, pair_exp, ones_ready, routed = sem("pair_exp_in"), sem("pair_exp"), sem("ones_ready"), sem("routed")
        table_zero, table_in, slots_in = sem("table_zero"), sem("table_in"), sem("slots_in")
        ix_ready = sem("ix_ready")
        xg_in, ew2_in, y_stored = [[sem(f"{n}{u}") for u in range(2)] for n in ("xg_in", "ew2_in", "y_stored")]
        y_ready, yg_used, e_zero = sem("y_ready"), sem("yg_used"), sem("e_zero")
        yg_in = [sem(f"yg_in{k}") for k in range(4)]
        ZERO = sb("ZERO", [P, TW], I32)
        ROUTE_R = B + 2

        def moe_sync(sp):
            sp.wait_ge(x_done, 5 * B)
            for dst, src in ((RW, l2_router), (EC, moe_row.to_broadcast([P, E + 16 + TW])), (TRI, moe_tri), (TOK, moe_token)):
                sp.dma_start(dst, src).then_inc(router_in, 16)
            for e in range(E):
                sp.dma_start(EW1[:, e * KT:(e + 1) * KT, :], l2_w12[:, e * KT:(e + 1) * KT, :]).then_inc(ew_in, 16)
            for b in range(B):
                sp.wait_ge(xn_ready, 5 * B + b + 1)
                sp.dma_start(xnd[b * S:(b + 1) * S, :].rearrange("(s p) d -> p s d", p=P), XN[:, :, :]).then_inc(xnd_in, 16)
            sp.wait_ge(table_in, 2 * B * ST * 16)
            sp.dma_start(SLOTS, table.rearrange("(p n) o -> p (n o)", p=P)).then_inc(slots_in, 16)
            sp.wait_ge(routed, 1)
            sp.wait_ge(e_zero, 2)

            def down(u, t):
                e = sp.value_load(EXPERT[0:1, ds(t, 1)], min_val=0, max_val=E - 1)
                sp.dma_start(EW2[:, u, :].rearrange("p (a n) -> p a n", a=1), l2_w2[ds(e, 1)].rearrange("a p n -> p a n"))\
                  .then_inc(ew2_in[u], 16)
            down(0, 0)
            with sp.Fori(0, NT // 2) as i:
                for u in range(2):
                    sp.wait_ge(er.full, ROUTE_R + i * 4 + 2 * u + 2)
                    down(1 - u, i * 2 + u + 1)
                    sp.wait_ge(y_ready, i * 2 + u + 1)
                    sp.dma_start(made[ds((i * 2 + u) * P, P), :], YE[:, u, :]).then_inc(y_stored[u], 16)

        def moe_tensor(pe):
            m, r, s, t = Count(), Count(), Count(), Count()
            pe.wait_ge(x_done, 5 * B)
            pe.wait_ge(router_in, 64)
            for b in range(B):
                pe.wait_ge(turn.free, T_PE.now() + 1)
                bank = start_job(pe, em, m)
                for kt in range(KT):
                    last = nc.tensor.matmul(bank[0:E, :], RW[:, kt, :], XT[:, b % 2, kt, :], start=kt == 0, stop=kt == KT - 1)
                last.then_inc(em.full, 1)
                pe.wait_ge(em.free, m.now() + 1)
                bank = start_job(pe, er, r)
                for st in range(ST):
                    last = nc.tensor.transpose(bank[:, st * E:(st + 1) * E], LT[0:E, st * P:(st + 1) * P], ID[0:E, 0:E])
                last.then_inc(er.full, 1)
                if b < B - 1:
                    norm_tensor(pe)
            pe.wait_ge(ones_ready, 2)
            for w in (TRI, ONE):
                nc.tensor.matmul(start_job(pe, er, r)[:, 0:n128], w, OHS.rearrange("p t e -> p (t e)"), start=True, stop=True)\
                  .then_inc(er.full, 1)
            pe.wait_ge(turn.free, T_PE.now() + 1)
            pe.wait_ge(routed, 1)
            pe.wait_ge(ew_in, E * 16)
            pe.wait_ge(e_zero, 2)
            return m, r, s, t

        def moe_tensor_tiles(pe, m, r, s, t):
            def turn_tile(u, i):
                pe.wait_ge(xg_in[u], i * 16 + 16)
                bank = start_job(pe, et, t)
                for kt in range(KT):
                    last = nc.tensor.transpose(bank[:, kt * P:(kt + 1) * P], XG[:, u, kt * P:(kt + 1) * P], ID[:, :])
                last.then_inc(et.full, 1)

            turn_tile(0, 0)
            with loop(pe, NT // 2, (m, 2), (r, 4), (s, 2), (t, 2)) as i:
                for u in range(2):
                    e = pe.value_load(EXPERT[0:1, ds(i * 2 + u, 1)], min_val=0, max_val=E - 1)
                    hold(pe, et.free, t.now() + 1)
                    up_done = None
                    for job, n, c in ((em, m, 0), (er, r, I)):
                        bank = start_job(pe, job, n)
                        for kt in range(KT):
                            last = nc.tensor.matmul(bank[:, 0:I].rearrange("p (a n) -> p a n", a=1), XGT[:, u, kt * P:(kt + 1) * P],
                                                    EW1[:, ds(e * KT + kt, 1), c:c + I], start=kt == 0, stop=kt == KT - 1)
                        last.then_inc(job.full, 1)
                    up_done = r.now() + 1
                    turn_tile(1 - u, i + u)
                    hold(pe, es.free, s.now() + 1)
                    pe.wait_ge(ew2_in[1 - u], (i + u) * 16)
                    bank = start_job(pe, er, r)
                    for k in range(EK):
                        rows = min(P, I - k * P)
                        last = nc.tensor.matmul(bank, EHT[0:rows, 1 - u, k * P:(k + 1) * P], EW2[0:rows, 1 - u, k * D:(k + 1) * D],
                                                start=k == 0, stop=k == EK - 1)
                    last.then_inc(er.full, 1)
                    hold(pe, er.free, up_done)
                    bank = start_job(pe, es, s)
                    for k in range(EK):
                        rows = min(P, I - k * P)
                        last = nc.tensor.transpose(bank[0:rows, k * P:(k + 1) * P], EHID[:, u, k * P:k * P + rows], ID[:, :])
                    last.then_inc(es.full, 1)
            pe.wait_ge(et.free, t.now() + 1)
            norm_tensor(pe)

        def moe_scalar(act):
            m, s, t = Count(), Count(), Count()
            for q in (em, es, et):
                act.sem_inc(q.free, 1)
            for b in range(B):
                nc.scalar.copy(LT[0:E, :], full(act, em, m)[0:E, :]).then_inc(em.free, 1)
                if b < B - 1:
                    norm_scalar(act, (b + 1) & 1)
            act.wait_ge(pair_exp_in, 1)
            nc.scalar.activation(EX, EX, ACT.Exp).then_inc(pair_exp, 1)

            def rows(u):
                nc.scalar.copy(XGT[:, u, :], full(act, et, t)).then_inc(et.free, 1)
            rows(0)
            with loop(act, NT // 2, (m, 2), (s, 2), (t, 2)) as i:
                for u in range(2):
                    nc.scalar.activation(ESILU[:, u, :], full(act, em, m)[:, 0:I], ACT.Silu).then_inc(em.free, 1)
                    rows(1 - u)
                    bank = full(act, es, s)
                    nc.scalar.copy(EHT[:, u, 0:2 * P], bank[:, 0:2 * P])
                    nc.scalar.copy(EHT[0:I - 2 * P, u, 2 * P:], bank[0:I - 2 * P, 2 * P:EK * P]).then_inc(es.free, 1)
            norm_scalar(act, 0)

        def moe_vector(v):
            r, m = Count(), Count()
            one = lambda t, n: t.rearrange("p (t o) -> p t o", o=1).to_broadcast([P, B * ST, n])
            per_e = lambda t, n=B * ST: t.rearrange("p (o e) -> p o e", o=1).to_broadcast([P, n, E])
            tt = nc.vector.tensor_tensor
            v.sem_inc(er.free, 1)
            v.wait_ge(router_in, 64)
            nc.vector.memset(ONE, 1.0).then_inc(ones_ready, 1)
            for b in range(B):
                bank = full(v, er, r)
                nc.vector.tensor_copy(LG[:, b * ST:(b + 1) * ST, :], bank[:, 0:ST * E].rearrange("p (s e) -> p s e", e=E)).then_inc(er.free, 1)
                if b < B - 1:
                    v.wait_ge(xnd_in, 16 * (b + 1))
                    norm_vector(v, b + 1)
                    T_V.step(KT)
            v.wait_ge(er.free, r.now() + 1)
            for mx, lg, oh in ((MX0, LG, OH0), (MX1, LG2, OH1)):
                if oh is OH1:
                    link(v, nc.vector.tensor_scalar(LG2, OH0, -1.0e30, None, ALU.mult))
                    link(v, tt(LG2, LG2, LG, ALU.add))
                link(v, nc.vector.tensor_reduce(mx, lg, op=ALU.max, axis=AX.X))
                link(v, tt(EQ, lg, one(mx, E), ALU.is_ge))
                link(v, tt(EQ, EQ, per_e(EC[:, 0:E]), ALU.mult))
                link(v, nc.vector.tensor_reduce(MS, EQ, op=ALU.max, axis=AX.X))
                link(v, tt(oh, EQ, one(MS, E), ALU.is_equal))
            tt(OHS, OH0, OH1, ALU.add).then_inc(ones_ready, 1)
            tt(EX, MX1, MX0, ALU.subtract).then_inc(pair_exp_in, 1)
            v.wait_ge(pair_exp, 1)
            link(v, nc.vector.tensor_scalar(WT0, EX, 1.0, None, ALU.add))
            link(v, nc.vector.reciprocal(WT0, WT0))
            link(v, nc.vector.tensor_scalar(WT0, WT0, G[:, 6:7], None, ALU.mult))
            link(v, tt(WT1, EX, WT0, ALU.mult))
            nc.vector.tensor_copy(RANK, full(v, er, r)[:, 0:n128].rearrange("p (t e) -> p t e", e=E)).then_inc(er.free, 1)
            bank = full(v, er, r)[:, 0:n128].rearrange("p (t e) -> p t e", e=E)
            nc.vector.tensor_copy(TOTAL, bank)
            nc.vector.tensor_copy(SCAN0, bank).then_inc(er.free, 1)
            v.wait_ge(er.free, r.now() + 1)

            def scan(of, to, n, cut):
                w = 1
                while w < n:
                    nc.vector.tensor_copy(cut(to, 0, w), cut(of, 0, w)).then_inc(vec, 1)
                    V.step()
                    link(v, tt(cut(to, w, n), cut(of, w, n), cut(of, 0, n - w), ALU.add))
                    of, to, w = to, of, 2 * w
                return of
            incl = scan(SCAN0, SCAN1, B * ST, lambda t, i, j: t[:, i:j, :])
            link(v, tt(TOTAL, incl, TOTAL, ALU.subtract))
            link(v, tt(RANK, RANK, TOTAL, ALU.add))
            count = incl[:, B * ST - 1, :]
            c3 = CMP.rearrange("p a b -> p (a b)")[:, 0:E * 16].rearrange("p (e t) -> p e t", e=E)
            link(v, tt(c3, count.rearrange("p (e o) -> p e o", o=1).to_broadcast([P, E, 16]),
                       EC[:, E:E + 16].rearrange("p (o t) -> p o t", o=1).to_broadcast([P, E, 16]), ALU.is_gt))
            link(v, nc.vector.tensor_reduce(NTL, c3, op=ALU.add, axis=AX.X))
            link(v, nc.vector.tensor_copy(END0, NTL))
            end = scan(END0, END1, E, lambda t, i, j: t[:, i:j])
            link(v, tt(START, end, NTL, ALU.subtract))
            link(v, nc.vector.tensor_scalar(START, START, float(P), None, ALU.mult))
            link(v, tt(RANK, RANK, per_e(START), ALU.add))
            for oh, pos, idx, yp in ((OH0, POS0, IDX0, YP0), (OH1, POS1, IDX1, YP1)):
                link(v, tt(EQ, oh, RANK, ALU.mult))
                link(v, nc.vector.tensor_reduce(pos, EQ, op=ALU.add, axis=AX.X))
                link(v, nc.vector.tensor_scalar(yp, pos, float(P), None, ALU.add))
                link(v, nc.vector.tensor_copy(idx, pos))
                link(v, nc.vector.tensor_scalar(idx, idx, 7, None, ALU.arith_shift_right))
                link(v, nc.vector.tensor_copy(MS, idx))
                link(v, nc.vector.tensor_scalar(MS, MS, float(1 - P * TW), None, ALU.mult))
                link(v, nc.vector.scalar_tensor_tensor(out=MS, in0=pos, scalar=float(TW), in1=MS, op0=ALU.mult, op1=ALU.add))
                link(v, nc.vector.tensor_copy(idx, MS))
            link(v, tt(CMP, EC[:, E + 16:].rearrange("p (t o) -> p t o", o=1).to_broadcast([P, TW, E]), per_e(end, TW), ALU.is_ge))
            link(v, nc.vector.tensor_reduce(EXF, CMP, op=ALU.add, axis=AX.X))
            nc.vector.tensor_scalar(EXPERT, EXF, float(E - 1), None, ALU.min).then_inc(routed, 1)

            m.step(B)
            with loop(v, NT // 2, (m, 2), (r, 4)) as i:
                for u in range(2):
                    bank = full(v, er, r)
                    v.wait_ge(em.free, m.step() + 1)
                    tt(EHID[:, u, :], ESILU[:, u, :], bank[:, 0:I], ALU.mult).then_inc(er.free, 1)
                    v.wait_ge(y_stored[u], i * 16)
                    nc.vector.tensor_copy(YE[:, u, :], full(v, er, r)).then_inc(y_ready, 1)
                    v.wait_ge(y_ready, i * 2 + u + 1)
                    v.sem_inc(er.free, 1)
            for k in range(2 * B * ST):
                tile, j = divmod(k, 2)
                v.wait_ge(yg_in[k % 4], 16 * (k // 4) + 16)
                nc.vector.scalar_tensor_tensor(out=X[:, tile, :], in0=YG[k % 4], scalar=(WT0, WT1)[j][:, tile:tile + 1],
                                               in1=X[:, tile, :], op0=ALU.mult, op1=ALU.add).then_inc(yg_used, 1)
                v.wait_ge(yg_used, k + 1)
            v.sem_inc(x_done, B)
            norm_vector(v, 0)
            T_V.step(KT)

        def moe_pool(pool):
            t = Count()
            nc.gpsimd.memset(EHT, 0.0).then_inc(e_zero, 1)
            nc.gpsimd.memset(EW2[:, 1, :], 0.0).then_inc(e_zero, 1)
            for b in range(B - 1):
                norm_pool(pool)
            pool.wait_ge(routed, 1)
            pool.wait_ge(table_zero, 16)
            for tile in range(B * ST):
                for idx in (IDX0, IDX1):
                    nc.gpsimd.indirect_dma_start(out=table, out_offset=bass.IndirectOffsetOnAxis(ap=idx[:, tile:tile + 1], axis=0),
                                                 in_=TOK[:, tile:tile + 1], in_offset=None).then_inc(table_in, 16)
            pool.wait_ge(slots_in, 16)
            pool.wait_ge(xnd_in, B * 16)

            def gather(u, i, n):
                nc.gpsimd.tensor_copy(IX[u], SLOTS[:, ds(i, 1)]).then_inc(ix_ready, 1)
                hold(pool, ix_ready, n)
                nc.gpsimd.indirect_dma_start(out=XG[:, u, :], out_offset=None, in_=xnd,
                                             in_offset=bass.IndirectOffsetOnAxis(ap=IX[u], axis=0)).then_inc(xg_in[u], 16)
            gather(0, 0, 1)
            gather(1, 1, 2)
            with pool.Fori(0, NT // 2) as i:
                for u in range(2):
                    pool.wait_ge(et.full, i * 2 + u + 1)
                    gather(u, i * 2 + u + 2, i * 2 + u + 3)
            for u in range(2):
                pool.wait_ge(y_stored[u], NT // 2 * 16)
                pool.wait_ge(xg_in[u], (NT // 2 + 1) * 16)
            pool.wait_ge(er.full, ROUTE_R + 2 * NT)
            pool.wait_ge(et.free, NT + 2)
            for k in range(2 * B * ST):
                tile, j = divmod(k, 2)
                if k >= 4:
                    pool.wait_ge(yg_used, k - 3)
                nc.gpsimd.indirect_dma_start(out=YG[k % 4], out_offset=None, in_=made,
                                             in_offset=bass.IndirectOffsetOnAxis(ap=(YP0, YP1)[j][:, tile:tile + 1], axis=0))\
                  .then_inc(yg_in[k % 4], 16)
            norm_pool(pool)

        lm, lr3, ls3 = rings("l3")
        mh = nc.dram_tensor("mh", [LH, P, 3 * C], F32, kind="Internal").ap()
        WSN = KT * P + LQ + 3 * C
        FTN = C + D + LQ + C
        a = area()
        W3 = a(LH, D)
        ROPE = a(6, S)
        KVN, KVT = a(B * ST, C), a(B * S)
        KVC = a(ST, C)
        WS = a(2, WSN)
        QHK, QP, CC = a(S), a(S), a(S)
        QB, RQ = a(4, S), a(3, S)
        FT, MST = a(2, FTN), a(2, 3 * C)
        ROPEK = a(2 * ST, C)
        SUM3, RS3, NEG3 = a(2 * ST), a(2 * ST), a(2 * ST)
        KV_TMP = QB.rearrange("p a n -> p (a n)").rearrange("p (t c) -> p t c", c=C)
        PROB3 = KPARTS[:, 0:ST, :].bitcast(F32)
        PROBT3 = KPARTS[:, ST:2 * ST, :].bitcast(F32)
        l3_in, kv_ready, kvc_ready = sem("l3_in"), sem("kv_ready"), sem("kvc_ready")
        ft_in, ws_in, m_stored = [[sem(f"{n}{u}") for u in range(2)] for n in ("ft_in", "ws_in", "m_stored")]
        max3_done, rope_ab, rope_c, rope_steps = sem("max3_done"), sem("rope_ab"), sem("rope_c"), sem("rope_steps")
        FOLD_M = 2 * LH + ST
        HEAD_M = 6
        PRO_M = 5

        def l3_sync(sp):
            sp.wait_ge(x_done, 6 * B)
            for u in range(2):
                sp.wait_ge(ew2_in[u], (NT // 2 + 1 - u) * 16)

            def fold(u, h):
                sp.dma_start(FT[:, u, :].rearrange("p (a n) -> p a n", a=1), l3_fold[ds(h, 1)].rearrange("a p n -> p a n")).then_inc(ft_in[u], 16)

            def weights(u, h):
                ws = WS[:, u, :].rearrange("p (a n) -> p a n", a=1)
                sp.dma_start(ws[:, :, 0:KT * P + LQ], l3_wq[ds(h, 1)].rearrange("a p n -> p a n")).then_inc(ws_in[u], 16)
                sp.dma_start(ws[:, :, KT * P + LQ:], mh[ds(h, 1)].rearrange("a p n -> p a n")).then_inc(ws_in[u], 16)
            for u in range(2):
                fold(u, u)
            for dst, src in ((KVN, ctx_n.rearrange("(n p) d -> p n d", p=P)), (ROPEK, rope_k), (ROPE, rope_q)):
                sp.dma_start(dst, src).then_inc(l3_in, 16)
            with sp.Fori(0, LH // 2) as i:
                for u in range(2):
                    hold(sp, lm.full, i * 4 + 2 * u + 2)
                    fold(u, (i * 2 + u + 2) & (LH - 1))
                    hold(sp, lm.free, i * 4 + 2 * u + 3)
                    sp.dma_start(mh[ds(i * 2 + u, 1)].rearrange("a p n -> p a n"), MST[:, u, :].rearrange("p (a n) -> p a n", a=1))\
                      .then_inc(m_stored[u], 16)
            for u in range(2):
                sp.wait_ge(m_stored[u], LH // 2 * 16)
            for u in range(2):
                weights(u, u)
            with sp.Fori(0, B * LH // 2) as i:
                for u in range(2):
                    hold(sp, lm.full, i * 2 * HEAD_M + (2 + u) * HEAD_M + FOLD_M - 1)
                    weights(u, (i * 2 + u + 2) & (LH - 1))

        def l3_tensor(pe):
            m, r, s, w = Count(), Count(), Count(), Count()
            pe.wait_ge(x_done, 6 * B)
            one = lambda t: t.rearrange("p (a n) -> p a n", a=1)
            with loop(pe, LH // 2, (m, 4)) as i:
                for u in range(2):
                    pe.wait_ge(ft_in[u], i * 16 + 16)
                    bank = start_job(pe, lm, m)
                    nc.tensor.matmul(bank, FT[:, u, 0:C], FT[:, u, C:C + D], start=True, stop=True).then_inc(lm.full, 1)
                    bank = start_job(pe, lm, m)
                    for k in range(3):
                        last = nc.tensor.matmul(bank[:, k * C:(k + 1) * C], FT[:, u, C + D + k * P:C + D + (k + 1) * P],
                                                FT[:, u, C + D + LQ:], start=True, stop=True)
                    last.then_inc(lm.full, 1)
            pe.wait_ge(kv_ready, 1)
            for t in range(ST):
                bank = start_job(pe, lm, m)
                for k in range(ST):
                    last = nc.tensor.transpose(bank[:, k * P:(k + 1) * P], KVN[:, t * ST + k, :], ID[:, :])
                last.then_inc(lm.full, 1)

            def head_queries(u, half, n):
                pe.wait_ge(ws_in[u], n)
                bank = start_job(pe, lm, m)
                for kt in range(KT):
                    last = nc.tensor.matmul(one(bank), WS[:, u, kt * P:(kt + 1) * P], XT[:, ds(half, 1), kt, :],
                                            start=kt == 0, stop=kt == KT - 1)
                last.then_inc(lm.full, 1)

            def big_queries(u):
                hold(pe, lm.free, m.now() + 1)
                for k in range(3):
                    nc.tensor.matmul(start_job(pe, lm, m), WS[:, u, (KT + k) * P:(KT + k + 1) * P], QHK, start=True, stop=True)\
                      .then_inc(lm.full, 1)

            def score_queries(u):
                hold(pe, rope_ab, w.now() + 1)
                hold(pe, rope_c, w.step())
                bank = start_job(pe, lm, m)
                for k in range(3):
                    last = nc.tensor.matmul(bank, WS[:, u, KT * P + LQ + k * C:KT * P + LQ + (k + 1) * C], RQ[:, k, :],
                                            start=k == 0, stop=k == 2)
                last.then_inc(lm.full, 1)

            head_queries(0, 0, 32)
            big_queries(0)
            score_queries(0)
            with loop(pe, B, (m, HEAD_M * LH), (r, ST * LH), (s, ST * LH), (w, LH), (T_PE, KT + ST * LH), (N_PE, 1)) as b:
                norm_tensor(pe)
                with loop(pe, LH // 2, (m, 2 * HEAD_M), (r, 2 * ST), (s, 2 * ST), (w, 2), (T_PE, 2 * ST)) as hp:
                    for u in range(2):
                        hold(pe, lm.free, m.now() + 1)
                        for st in range(ST):
                            nc.tensor.matmul(start_job(pe, ls3, s), QP[:, st * P:(st + 1) * P], KVT[:, ds(b * S, S)], start=True, stop=True)\
                              .then_inc(ls3.full, 1)
                        if u == 0:
                            head_queries(1, b & 1, b * (16 * LH) + hp * 32 + 32)
                        else:
                            hold(pe, turn.free, T_PE.now())
                            head_queries(0, ((b * 8 + hp + 1) >> 3) & 1, b * (16 * LH) + hp * 32 + 64)
                        hold(pe, ls3.free, s.now() + 1)

                        def turn_probs(lts):
                            for lt in lts:
                                bank = start_job(pe, turn, T_PE)
                                for st in range(ST):
                                    last = nc.tensor.transpose(bank[:, st * P:(st + 1) * P], PROB3[:, st, lt * P:(lt + 1) * P], ID[:, :])
                                last.then_inc(turn.full, 1)
                        turn_probs((0, 1))
                        big_queries(1 - u)
                        turn_probs((2, 3))
                        hold(pe, turn.free, T_PE.now() + 1)
                        if u == 0:
                            hold(pe, kvc_ready, b + 1)
                        bank = start_job(pe, lm, m)
                        for lt in range(ST):
                            last = nc.tensor.matmul(bank, KVC[:, lt, :], PROBT3[:, lt, :], start=lt == 0, stop=lt == ST - 1)
                        last.then_inc(lm.full, 1)
                        score_queries(1 - u)
                        hold(pe, lm.free, m.now())
                        for st in range(ST):
                            nc.tensor.matmul(one(start_job(pe, lr3, r)), CC[:, st * P:(st + 1) * P], W3[:, ds(hp * 2 + u, 1), :],
                                             start=True, stop=True).then_inc(lr3.full, 1)
            pe.wait_ge(lm.free, m.now() + 1)

        def l3_scalar(act):
            m, s, w = Count(), Count(), Count()
            act.sem_inc(lm.free, 1)
            act.sem_inc(ls3.free, 1)
            with loop(act, LH // 2, (m, 4)) as i:
                for u in range(2):
                    nc.scalar.copy(W3[:, ds(i * 2 + u, 1), :], full(act, lm, m).rearrange("p (a n) -> p a n", a=1)).then_inc(lm.free, 1)
                    act.wait_ge(m_stored[u], i * 16)
                    nc.scalar.copy(MST[:, u, :], full(act, lm, m)[:, 0:3 * C]).then_inc(lm.free, 1)
            for t in range(ST):
                nc.scalar.copy(KVT[:, t * S:(t + 1) * S], full(act, lm, m)).then_inc(lm.free, 1)

            def big_queries(first=False):
                for k in range(3):
                    if k == 0 and not first:
                        act.wait_ge(rope_ab, w.now())
                    if k == 2 and not first:
                        act.wait_ge(rope_c, w.now())
                    bank = full(act, lm, m)
                    last = nc.scalar.copy(QB[:, k, :], bank)
                    if k == 2:
                        nc.scalar.copy(QB[64:128, 3, :], bank[0:64, :])
                        last = nc.scalar.copy(QB[0:64, 3, :], bank[64:128, :])
                    last.then_inc(lm.free, 1)
                w.step()
            nc.scalar.copy(QHK, full(act, lm, m)).then_inc(lm.free, 1)
            big_queries(True)
            nc.scalar.copy(QP, full(act, lm, m)).then_inc(lm.free, 1)
            with loop(act, B, (m, HEAD_M * LH), (s, ST * LH), (w, LH), (T_ACT, KT + ST * LH)) as b:
                norm_scalar(act, (b + 1) & 1)
                with loop(act, LH // 2, (m, 2 * HEAD_M), (s, 2 * ST), (w, 2), (T_ACT, 2 * ST)) as hp:
                    for u in range(2):
                        for st in range(ST):
                            act.wait_ge(max3_done, s.now() + 1)
                            bank = full(act, ls3, s)
                            nc.scalar.activation(PROB3[:, st, :], bank, ACT.Exp, bias=NEG3[:, u * ST + st:u * ST + st + 1],
                                                 accum_out=SUM3[:, u * ST + st:u * ST + st + 1]).then_inc(ls3.free, 1)
                        nc.scalar.copy(QHK, full(act, lm, m)).then_inc(lm.free, 1)
                        for lt in (0, 1):
                            nc.scalar.copy(PROBT3[:, lt, :], full(act, turn, T_ACT)).then_inc(turn.free, 1)
                        big_queries()
                        for lt in (2, 3):
                            nc.scalar.copy(PROBT3[:, lt, :], full(act, turn, T_ACT)).then_inc(turn.free, 1)
                        nc.scalar.copy(CC, full(act, lm, m)).then_inc(lm.free, 1)
                        nc.scalar.copy(QP, full(act, lm, m)).then_inc(lm.free, 1)

        def l3_vector(v):
            m, r, s, w = Count(), Count(), Count(), Count()
            tt = nc.vector.tensor_tensor
            v.sem_inc(lr3.free, 1)
            v.wait_ge(l3_in, 48)
            kv = lambda t, i, j: t[:, :, i:j].rearrange("p (b s) c -> p b s c", b=B)
            tab = lambda k, i, j: ROPEK[:, k * ST:(k + 1) * ST, i:j].rearrange("p (o s) c -> p o s c", o=1).to_broadcast([P, B, ST, j - i])
            tt(kv(KV_TMP, 0, 64), kv(KVN, 64, 128), tab(1, 0, 64), ALU.mult)
            link(v, tt(kv(KV_TMP, 64, 128), kv(KVN, 0, 64), tab(1, 64, 128), ALU.mult))
            link(v, tt(kv(KVN, 0, 128), kv(KVN, 0, 128), tab(0, 0, 128), ALU.mult))
            tt(KVN, KVN, KV_TMP, ALU.add).then_inc(kv_ready, 1)
            m.step(FOLD_M)

            def rotate():
                v.wait_ge(lm.free, m.now() + 4)
                tt(RQ[:, 0, :], QB[:, 0, :], ROPE[:, 0, :], ALU.mult)
                tt(RQ[:, 1, :], QB[:, 1, :], ROPE[:, 2, :], ALU.mult)
                tt(QB[:, 1, :], QB[:, 1, :], ROPE[:, 1, :], ALU.mult)
                link(v, tt(QB[:, 0, :], QB[:, 0, :], ROPE[:, 3, :], ALU.mult))
                tt(RQ[:, 0, :], RQ[:, 0, :], QB[:, 1, :], ALU.subtract)
                tt(RQ[:, 1, :], RQ[:, 1, :], QB[:, 0, :], ALU.add).then_inc(rope_ab, 1)
            rotate()
            m.step(PRO_M)
            with loop(v, B, (m, HEAD_M * LH), (r, ST * LH), (s, ST * LH), (V, 3 * LH), (T_V, KT + ST * LH), (N_V, 1)) as b:
                norm_vector(v, (b + 1) & 3)
                T_V.step(KT)
                with loop(v, LH // 2, (m, 2 * HEAD_M), (r, 2 * ST), (s, 2 * ST), (V, 6), (T_V, 2 * ST)) as hp:
                    for u in range(2):
                        for st in range(ST):
                            nc.vector.tensor_reduce(NEG3[:, u * ST + st:u * ST + st + 1], full(v, ls3, s), op=ALU.max, axis=AX.X,
                                                    negate=True).then_inc(max3_done, 1)
                        hold(v, ls3.free, s.now() + 1)
                        link(v, nc.vector.reciprocal(RS3[:, u * ST:(u + 1) * ST], SUM3[:, u * ST:(u + 1) * ST]))
                        link(v, nc.vector.tensor_scalar(RS3[:, u * ST:(u + 1) * ST], RS3[:, u * ST:(u + 1) * ST], G[:, 3:4], None, ALU.mult))
                        rotate()
                        m.step(HEAD_M)
                        for st in range(ST):
                            bank = full(v, lr3, r)
                            xb = X[:, ds(b * ST + st, 1), :].rearrange("p a n -> p (a n)")
                            nc.vector.scalar_tensor_tensor(out=xb, in0=bank, scalar=RS3[:, u * ST + st:u * ST + st + 1], in1=xb,
                                                           op0=ALU.mult, op1=ALU.add).then_inc(lr3.free, 1)
                        T_V.step(ST)
                v.wait_ge(lr3.free, r.now() + 1)
                v.sem_inc(x_done, 1)

        def l3_pool(pool):
            m, w = Count(), Count()
            tt = nc.gpsimd.tensor_tensor
            m.step(FOLD_M)

            def rotate():
                pool.wait_ge(lm.free, m.now() + 5)
                tt(RQ[:, 2, :], QB[:, 2, :], ROPE[:, 4, :], ALU.mult)
                tt(QB[:, 3, :], QB[:, 3, :], ROPE[:, 5, :], ALU.mult).then_inc(rope_steps, 1)
                pool.wait_ge(rope_steps, w.step())
                tt(RQ[:, 2, :], RQ[:, 2, :], QB[:, 3, :], ALU.add).then_inc(rope_c, 1)
            pool.wait_ge(l3_in, 48)
            rotate()
            m.step(PRO_M)
            with loop(pool, B, (m, HEAD_M * LH), (w, LH), (N_P, 1)) as b:
                hold(pool, lm.full, m.now())
                nc.gpsimd.tensor_copy(KVC, KVN[:, ds(b * ST, ST), :]).then_inc(kvc_ready, 1)
                norm_pool(pool)
                with loop(pool, LH // 2, (m, 2 * HEAD_M), (w, 2)) as hp:
                    for u in range(2):
                        rotate()
                        m.step(HEAD_M)

        l3f = Ffn("l3f", 7, l3_w13, l3_w2, UG, HID // P // UG, 1, lambda b, g, st: G[:, 7:8])

        def l3f_begin(sp):
            sp.wait_ge(x_done, 7 * B)
            for u in range(2):
                sp.wait_ge(ws_in[u], (B * LH + 2) * 16)

        block = ctx.enter_context(nc.Block())
        stored = sem("stored")
        zero_ready = sem("zero_ready")

        @block.sync
        def _(sp):
            sp.wait_ge(zero_ready, 1)
            sp.dma_start(table.rearrange("(p n) o -> p (n o)", p=P), ZERO[:, :]).then_inc(table_zero, 16)
            sp.dma_start(X[:, :, :], x.rearrange("(n p) d -> p n d", p=P)).then_inc(loaded, 16)
            sp.dma_start(CT, ctx_t).then_inc(loaded, 16)
            sp.dma_start(ID[:, :], ident).then_inc(loaded, 16)
            sp.dma_start(G[:, :], gates.rearrange("(a n) -> a n", a=1).to_broadcast([P, 8])).then_inc(loaded, 16)
            sp.dma_start(GC[:, 0:1], gamma_raw.rearrange("(a n) -> a n", a=1).to_broadcast([P, 1])).then_inc(loaded, 16)
            sp.dma_start(WQ0, l0_wq).then_inc(l0_w, 16)
            sp.dma_start(WK0, l0_wk).then_inc(l0_w, 16)
            sp.dma_start(HAD, hadamard).then_inc(l0_had, 16)
            sp.dma_start(WH[0], l0_w2).then_inc(l0_had, 16)
            sp.wait_ge(hadm.free, HID // P + 1)
            sp.dma_start(w2h.rearrange("g p n -> p g n"), WH[1].rearrange("p (g u) n -> p g (u n)", u=UG)).then_inc(wh_stored, 16)
            ffn_sync(sp, l0f, lambda sp: sp.wait_ge(wh_stored, 16))
            l1_sync(sp)
            l1f_sync_weights(sp)
            l1f_sync(sp)
            l2_sync(sp)
            moe_sync(sp)
            l3_sync(sp)
            ffn_sync(sp, l3f, l3f_begin)
            sp.wait_ge(x_done, 8 * B)
            sp.dma_start(out.rearrange("(n p) d -> p n d", p=P), X[:, :, :]).then_inc(stored, 16)
            sp.wait_ge(stored, 16)

        @block.tensor
        def _(pe):
            pe.wait_ge(loaded, 80)
            norm_tensor(pe)
            l0_tensor(pe)
            had_tensor(pe)
            ffn_tensor(pe, l0f)
            l1_tensor(pe)
            l1f_tensor(pe)
            l2_tensor(pe)
            moe_tensor_tiles(pe, *moe_tensor(pe))
            l3_tensor(pe)
            ffn_tensor(pe, l3f)

        @block.scalar
        def _(act):
            act.sem_inc(turn.free, 1)
            act.wait_ge(loaded, 80)
            nc.scalar.activation(G[:, :], G[:, :], ACT.Tanh).then_inc(g_ready, 1)
            nc.scalar.activation(GC[:, 0:1], GC[:, 0:1], ACT.Sigmoid).then_inc(g_ready, 1)
            act.sem_inc(hadm.free, 1)
            norm_scalar(act, 0)
            l0_scalar(act)
            had_scalar(act)
            ffn_scalar(act, l0f)
            l1_scalar(act)
            l1f_scalar(act)
            l2_scalar(act)
            moe_scalar(act)
            l3_scalar(act)
            ffn_scalar(act, l3f)

        @block.vector
        def _(v):
            v.wait_ge(loaded, 80)
            norm_vector(v, 0)
            T_V.step(KT)
            v.wait_ge(g_ready, 2)
            link(v, nc.vector.tensor_scalar(GC[:, 1:2], GC[:, 0:1], -1.0, 1.0, ALU.mult, ALU.add))
            link(v, nc.vector.tensor_scalar(GC[:, 1:2], GC[:, 1:2], G[:, 0:1], None, ALU.mult))
            nc.vector.tensor_scalar(GC[:, 2:3], GC[:, 0:1], G[:, 0:1], 0.5, ALU.mult, ALU.mult).then_inc(gc_ready, 1)
            l0_vector(v)
            ffn_vector(v, l0f)
            l1_vector(v)
            l1f_vector(v)
            l2_vector(v)
            moe_vector(v)
            l3_vector(v)
            ffn_vector(v, l3f)

        @block.gpsimd
        def _(pool):
            nc.gpsimd.memset(ZERO[:, :], 0).then_inc(zero_ready, 1)
            nc.gpsimd.memset(HALF[:, :], -0.5).then_inc(consts, 1)
            pool.wait_ge(consts, 1)
            norm_pool(pool)
            had_pool(pool)
            with loop(pool, 2 * B, (N_P, 1)):
                norm_pool(pool)
            l1_pool(pool)
            l1f_pool(pool)
            l2_pool(pool)
            pool.wait_ge(x_done, 5 * B)
            moe_pool(pool)
            l3_pool(pool)
            with loop(pool, B, (N_P, 1)):
                norm_pool(pool)


def layouts(inp):
    import numpy as np

    f = {k: np.asarray(v) for k, v in inp.items()}
    c = np.ascontiguousarray

    def up_tiles(wg, wu):
        n = wg.shape[0] // P
        w = np.stack([wg, wu]).reshape(2, n, P, KT, P)
        return c(w.transpose(1, 4, 3, 0, 2)).reshape(n, P, KT * 2 * P)

    def cut(w):
        return c(w.reshape(-1, P, w.shape[-1]).transpose(1, 0, 2))

    o = {}
    o["x"] = f["x"].reshape(B * S, D)
    ctx = f["ctx_512"].reshape(B * S, C)
    o["ctx_n"], o["ctx_t"] = ctx, c(ctx.T)
    o["gates"] = np.concatenate([f["g_xattn"], f["g_ffn"]])
    o["gamma_raw"] = f["L0_xattn_gamma_raw"].reshape(1)
    o["ident"] = np.eye(P, dtype=np.float32)
    had = np.ones((1, 1), np.float32)
    while len(had) < P:
        had = np.block([[had, had], [had, -had]])
    o["hadamard"] = had.astype(np.float32)
    o["l0_w13"] = up_tiles(f["L0_ffn_W1"], f["L0_ffn_W3"])
    o["l0_w2"] = cut(f["L0_ffn_W2"].T)
    row = lambda *n: np.stack([f["L1_" + k] for k in n])
    col = lambda k: f["L1_ffn_" + k].reshape(-1, P).T
    o["l1_wk"], o["l1_bk"] = c(f["L1_xattn_W_k"].T), f["L1_xattn_b_k"].reshape(P, 1)
    o["l1_bk_row"] = f["L1_xattn_b_k"].reshape(1, C)
    o["l1_ln"] = row("xattn_ln_gamma", "xattn_ln_beta")
    o["l1_rows"] = row("ffn_out_gamma", "ffn_out_beta")
    o["l1_inrows"] = row("ffn_in_gamma", "ffn_in_beta")
    o["l1_cols"] = c(np.concatenate([col(k) for k in ("agg_b", "d1_b", "d2_b", "bc_b", "gate_b", "pn_gamma", "pn_beta")], 1))
    for k, n in (("l1_agg", "agg_w"), ("l1_d1", "d1_w"), ("l1_d2", "d2_w"), ("l1_bc", "bc_w"), ("l1_gate", "gate_w")):
        o[k] = cut(f["L1_ffn_" + n])
    o["l2_router"] = cut(f["L2_ffn_router_w"].T)
    o["l2_w12"] = c(f["L2_ffn_w1"].reshape(E, 2 * I, KT, P).transpose(3, 0, 2, 1)).reshape(P, E * KT, 2 * I)
    w2 = np.zeros((E, EK * P, D), np.float32)
    w2[:, :I] = f["L2_ffn_w2"].transpose(0, 2, 1)
    o["l2_w2"] = c(w2.reshape(E, EK, P, D).transpose(0, 2, 1, 3)).reshape(E, P, EK * D)
    o["moe_row"] = np.concatenate([8.0 - np.arange(E), 128.0 * np.arange(16), np.arange(TW)]).astype(np.float32)[None]
    o["moe_tri"] = np.triu(np.ones((P, P), np.float32), 1)
    o["moe_token"] = (np.arange(B * ST)[None, :] * P + np.arange(P)[:, None]).astype(np.int32)
    order = np.concatenate([np.arange(128), np.arange(192, 320), np.arange(128, 192), np.arange(320, 384)])
    wq = f["L3_xattn_Wq"].reshape(LH, LK, KT, P).transpose(0, 3, 2, 1).reshape(LH, P, KT * LK)
    o["l3_wq"] = np.concatenate([wq, f["L3_xattn_w_kc_q"][:, :, order]], 2)
    wo = f["L3_xattn_Wo"].reshape(D, LH, LK).transpose(1, 2, 0)
    qr_kr = np.zeros((LH, P, LQ + C), np.float32)
    qr_kr[:, :LR, :LQ] = f["L3_xattn_W_qr"][:, order, :].transpose(0, 2, 1)
    qr_kr[:, :LR, LQ:] = f["L3_xattn_W_kr"].transpose(0, 2, 1)
    o["l3_fold"] = np.concatenate([f["L3_xattn_w_kc_kv"], wo, qr_kr], 2)

    def rope(dim):
        inv = (np.float32(1) / np.float32(10000) ** (np.arange(0, dim, 2, dtype=np.float32) / np.float32(dim))).astype(np.float32)
        at = np.repeat(np.arange(S, dtype=np.float32)[:, None] * inv, 2, axis=1).astype(np.float64)
        return np.cos(at).astype(np.float32), np.sin(at).astype(np.float32)
    cos, sin = rope(LQ)
    cos, sin = cos.T[order].reshape(3, P, S).copy(), sin.T[order].reshape(3, P, S).copy()
    sin[2, :64] *= -1
    o["rope_q"] = c(np.stack([cos, sin], 1).reshape(6, P, S).transpose(1, 0, 2))
    cos, sin = rope(C)
    sin[:, :C // 2] *= -1
    o["rope_k"] = c(np.stack([cos, sin]).reshape(2 * ST, P, C).transpose(1, 0, 2))
    o["l3_w13"] = up_tiles(f["L3_ffn_w_gate"], f["L3_ffn_w_up"])
    o["l3_w2"] = c(f["L3_ffn_w_down"].T.reshape(HID // P // UG, UG, P, D).transpose(0, 2, 1, 3)).reshape(HID // P // UG, P, UG * D)
    o["l0_wq"], o["l0_wk"] = c(f["L0_xattn_Wq"].T), c(f["L0_xattn_Wk"].T)
    return o


LOADED = """x ctx_n ctx_t gates gamma_raw ident l0_wq l0_wk hadamard l0_w13 l0_w2 l1_wk l1_bk l1_bk_row l1_ln l1_rows l1_inrows l1_cols l1_agg l1_d1 l1_d2 l1_bc l1_gate l2_router l2_w12 l2_w2 moe_row moe_tri moe_token l3_wq l3_fold rope_q rope_k l3_w13 l3_w2""".split()


def kernel(**inputs):
    import numpy as np
    import concourse.bacc as bacc
    from concourse.bass_utils import run_bass_kernel_spmd

    nc = bacc.Bacc("TRN2", target_bir_lowering=False, num_devices=1)
    laid = layouts(inputs)
    arrays = {f"{name}_dram": np.ascontiguousarray(laid[name]) for name in LOADED}
    args = [nc.dram_tensor(f"{name}_dram", arrays[f"{name}_dram"].shape, mybir.dt.from_np(arrays[f"{name}_dram"].dtype),
                           kind="ExternalInput").ap() for name in LOADED]
    out = nc.dram_tensor("out_dram", (B * S, D), F32, kind="ExternalOutput").ap()
    flamingo(nc, *args, out)
    return run_bass_kernel_spmd(nc, [arrays], core_ids=[0]).results[0]["out_dram"].reshape(B, S, D)
```

```python
from contextlib import ExitStack, contextmanager

import concourse.bass as bass
from concourse import mybir

ds = bass.ds
F32 = mybir.dt.float32
F32R = mybir.dt.float32r
I32 = mybir.dt.int32
ALU = mybir.AluOpType
ACT = mybir.ActivationFunctionType
AX = mybir.AxisListType

P = 128
B, S, D = 4, 512, 512
ST = S // P
KT = D // P
C = 128
TOPK = 153
TOP_ROUNDS = (TOPK - 1) // 8 + 1
L0_HEADS, L0_HEAD = 4, 32
HID = 2048
E, I = 8, 352
PAIR_TILES = 2 * B * ST + E - 1
NT = PAIR_TILES + 1
TW = NT + 2
EK = 3
QH, HD = 32, 16
KVH = 8
LH, LK, LQ, LR = 16, 128, 384, 64
EPS_BLOCK, EPS_INNER = 1e-5, 1e-6
K_STEPS = 4
UG = 4
AREA = 33200
FFN_AREA = AREA - 4 * 1536 - 2 * S - 4 * S


class Count:

    def __init__(self):
        self.base, self.k, self.odd, self.turn = 0, 0, 0, 0

    def bank(self):
        assert self.turn % 2 == 0, self.turn
        return (self.odd + self.k) % 2

    def now(self):
        return self.base + self.k

    def step(self, n=1):
        self.k += n
        return self.base + self.k


@contextmanager
def loop(eng, times, *counts):
    begun = [(c.base, c.k, c.odd, c.turn) for c, _ in counts]
    with eng.Fori(0, times) as i:
        for (c, n), (base, k, odd, _) in zip(counts, begun):
            c.base, c.k, c.odd, c.turn = i * n + (base + k), 0, (odd + k) % 2, n
        yield i
        for c, n in counts:
            assert c.k == n, (c.k, n)
    for (c, n), (base, k, odd, turn) in zip(counts, begun):
        c.base, c.k, c.odd, c.turn = base, k + times * n, odd, turn


class Ring:

    def __init__(self, banks, full, free):
        self.banks, self.full, self.free, self.depth = banks, full, free, banks.shape[1]


def flamingo(nc, x, ctx_n, ctx_t, gates, gamma_raw, ident, l0_wq, l0_wk, hadamard, l0_w13, l0_w2, l1_wk, l1_bk, l1_bk_row,
             l1_ln, l1_rows, l1_inrows, l1_cols, l1_agg, l1_d1, l1_d2, l1_bc, l1_gate, l2_router, l2_w12, l2_w2, moe_row, moe_tri, moe_token,
             l3_wq, l3_fold, rope_q, rope_k, l3_w13, l3_w2, out):
    ctx = ExitStack()
    with ctx:
        def sb(name, shape, dt=F32):
            return ctx.enter_context(nc.sbuf_tensor(name, shape, dt))

        def sem(name):
            return ctx.enter_context(nc.semaphore(name))

        X = sb("X", [P, B * ST, D])
        XN = sb("XN", [P, ST, D])
        XT = sb("XT", [P, 2, KT, S])
        ID = sb("ID", [P, P])
        STAT = sb("STAT", [P, ST, 6])
        MV = sb("MV", [P, ST, 2])
        VAR = sb("VAR", [P, ST])
        RSTD = sb("RSTD", [P, ST])
        HALF = sb("HALF", [P, ST])
        G = sb("G", [P, 8])
        GC = sb("GC", [P, 3])
        VAR1, RS1, NEGM1, SUM1 = [sb(n, [P, ST])[:, :] for n in ("VAR1", "RS1", "NEGM1", "SUM1")]
        AR = sb("AR", [P, AREA])

        def area(at=0):
            at = [at]

            def take(*shape):
                n = 1
                for s in shape:
                    n *= s
                v = AR[:, at[0]:at[0] + n]
                at[0] += n
                assert at[0] <= AREA, at[0]
                if len(shape) == 2:
                    v = v.rearrange("p (a b) -> p a b", b=shape[1])
                if len(shape) == 3:
                    v = v.rearrange("p (a b c) -> p a b c", b=shape[1], c=shape[2])
                return v
            take.here = lambda: at[0]
            return take

        BM = ctx.enter_context(nc.psum_tensor("BM", [P, 2, 512], F32))
        BR = ctx.enter_context(nc.psum_tensor("BR", [P, 2, 512], F32))
        BS = ctx.enter_context(nc.psum_tensor("BS", [P, 2, 512], F32))
        BT = ctx.enter_context(nc.psum_tensor("BT", [P, 2, 512], F32))

        def ring(banks, name):
            return Ring(banks, sem(name + "_full"), sem(name + "_free"))

        def rings(phase):
            return ring(BM, phase + "_m"), ring(BR, phase + "_r"), ring(BS, phase + "_s")

        turn = ring(BT, "turned")
        T_PE, T_ACT, T_V = Count(), Count(), Count()
        N_PE, N_V, N_P = Count(), Count(), Count()

        def start_job(pe, r, n):
            pe.wait_ge(r.free, n.now() + 1)
            bank = r.banks[:, n.bank() if r.depth == 2 else 0, :]
            n.step()
            return bank

        def full(eng, r, n):
            bank = r.banks[:, n.bank() if r.depth == 2 else 0, :]
            eng.wait_ge(r.full, n.step())
            return bank

        loaded = sem("loaded")
        consts = sem("consts")
        passed = sem("passed")
        g_ready = sem("g_ready")
        gc_ready = sem("gc_ready")
        vec = sem("vec")
        acts = sem("acts")
        V, A_ = Count(), Count()

        def hold(eng, s, value):
            eng.wait_ge(s, value)
            eng.sem_inc(passed, 1)

        def link(v, ins, alone=False):
            ins.then_inc(vec, 1)
            (hold if alone else lambda e, s, n: e.wait_ge(s, n))(v, vec, V.step())

        norm_stats, norm_aggr = sem("norm_stats"), sem("norm_aggr")
        norm_var, norm_rstd, xn_ready = sem("norm_var"), sem("norm_rstd"), sem("xn_ready")
        x_done = sem("x_done")

        def norm_vector(v, b):
            g = N_V.now()
            N_V.step()
            hold(v, turn.free, T_V.now() + 2)
            for st in range(ST):
                last = nc.vector.bn_stats(STAT[:, st, :], X[:, ds(4 * b + st, 1), :])
            last.then_inc(norm_stats, 1)
            hold(v, norm_stats, g + 1)
            for st in range(ST):
                last = nc.vector.bn_aggr(MV[:, st, :], STAT[:, st, :])
            last.then_inc(norm_aggr, 1)
            v.wait_ge(norm_aggr, g + 1)
            nc.vector.tensor_scalar(VAR[:, :], MV[:, :, 1], EPS_BLOCK, None, ALU.add).then_inc(norm_var, 1)
            v.wait_ge(norm_rstd, g + 1)
            for st in range(ST):
                last = nc.vector.tensor_scalar(XN[:, st, :], X[:, ds(4 * b + st, 1), :].rearrange("p a n -> p (a n)"),
                                               MV[:, st, 0:1], RSTD[:, st:st + 1], ALU.subtract, ALU.mult)
            last.then_inc(xn_ready, 1)

        def norm_pool(pool):
            pool.wait_ge(norm_var, N_P.step())
            nc.gpsimd.tensor_tensor(RSTD[:, :], VAR[:, :], HALF[:, :], ALU.pow).then_inc(norm_rstd, 1)

        def norm_tensor(pe):
            pe.wait_ge(xn_ready, N_PE.step())
            for kt in range(KT):
                bank = start_job(pe, turn, T_PE)
                for st in range(ST):
                    last = nc.tensor.transpose(bank[:, st * P:(st + 1) * P], XN[:, st, kt * P:(kt + 1) * P], ID[:, :])
                last.then_inc(turn.full, 1)

        def norm_scalar(act, half):
            for kt in range(KT):
                bank = full(act, turn, T_ACT)
                nc.scalar.copy(XT[:, ds(half, 1), kt, :], bank.rearrange("p (a n) -> p a n", a=1)).then_inc(turn.free, 1)

        a = area()
        WQ0, WK0 = a(C), a(C)
        QT0, KT0 = a(S), a(S)
        CT = a(B * S)
        SIM = a(ST, S)
        GRAPH = a(ST, S)
        WORK = a(S)
        TOP = a(8)
        HAD = a(P)
        WH = [a(HID // P, D), a(HID // P, D)]
        l0_w = sem("l0_w")
        graph_ready = sem("graph_ready")
        l0_had, butterflies = sem("l0_had"), sem("butterflies")
        wh_stored = sem("wh_stored")
        w2h = nc.dram_tensor("w2h", [HID // P // UG, P, UG * D], F32, kind="Internal").ap()

        def had_pool(pool):
            pool.wait_ge(l0_had, 32)
            n = 0
            for stage in range(4):
                w = 1 << stage
                of, to = WH[stage % 2], WH[1 - stage % 2]
                of = of.rearrange("p (g two w) d -> p g two (w d)", two=2, w=w)
                to = to.rearrange("p (g two w) d -> p g two (w d)", two=2, w=w)
                if stage:
                    pool.wait_ge(butterflies, n)
                for half, op in ((0, ALU.add), (1, ALU.subtract)):
                    nc.gpsimd.tensor_tensor(to[:, :, half, :], of[:, :, 0, :], of[:, :, 1, :], op).then_inc(butterflies, 1)
                    n += 1

        class Ffn:

            def __init__(self, name, phase, w13, w2, units, groups, per_turn, scale, after=(), before=0, between=0):
                self.before, self.between = before, between
                assert groups == 4
                self.phase, self.w13, self.w2, self.after = phase, w13, w2, after
                self.units, self.groups, self.per_turn, self.scale = units, groups, per_turn, scale
                self.m, self.r, self.s = rings(name)
                self.up_in = [sem(f"{name}_up_in{u}") for u in range(units)]
                self.down_in = sem(f"{name}_down_in")
                a = area(FFN_AREA)
                self.UP = a(units, 2 * KT * P)
                self.DOWN = a(units, D)
                self.SILU = a(2, S)
                self.HIDDEN = a(units, S)

        def ffn_sync(sp, f, begin):
            def up(u, n):
                sp.dma_start(f.UP[:, u, :], f.w13[ds(n, 1)].rearrange("a p n -> p (a n)")).then_inc(f.up_in[u], 16)

            def down(n):
                sp.dma_start(f.DOWN[:, :, :], f.w2[ds(n, 1)].rearrange("a p (u n) -> p (a u) n", u=f.units)).then_inc(f.down_in, 16)

            begin(sp)
            for u in range(f.units):
                up(u, u)
            for wait, n in f.after:
                sp.wait_ge(wait, n)
            down(0)
            with sp.Fori(1, B * f.groups) as g:
                for u in range(f.units):
                    sp.wait_ge(f.r.full, (g - 1) * f.units + (u + 1 + f.before) + (((g - 1) >> 2) * f.between if f.between else 0))
                    up(u, (g % f.groups) * f.units + u)
                sp.wait_ge(f.s.full, g * ST)
                down(g % f.groups)

        def ffn_tensor_batch(pe, f, m, r, s, n_in, b):
            with loop(pe, f.groups // f.per_turn, (m, f.units * f.per_turn), (r, f.units * f.per_turn),
                      (s, ST * f.per_turn), (n_in, f.per_turn)):
                for _ in range(f.per_turn):
                    n_in.step()
                    hidden = r.now() + 3
                    for u in range(f.units):
                        pe.wait_ge(f.up_in[u], n_in.now() * 16)
                        w = f.UP[:, u, :].rearrange("p (k a n) -> p k a n", k=KT, a=2)
                        for a, (job, n) in enumerate(((f.m, m), (f.r, r))):
                            bank = start_job(pe, job, n)
                            for kt in range(KT):
                                last = nc.tensor.matmul(bank.rearrange("p (a n) -> p a n", a=1), w[:, kt, a, :],
                                                        XT[:, ds(b & 1, 1), kt, :], start=kt == 0, stop=kt == KT - 1)
                            last.then_inc(job.full, 1)
                    pe.wait_ge(f.down_in, n_in.now() * 16)
                    for pair in range(ST // 2):
                        banks = [start_job(pe, f.s, s) for _ in range(2)]
                        for u in range(f.units):
                            if pair == 0:
                                pe.wait_ge(f.r.free, hidden + u)
                            for j, bank in enumerate(banks):
                                st = 2 * pair + j
                                last = nc.tensor.matmul(bank, f.HIDDEN[:, u, st * P:(st + 1) * P], f.DOWN[:, u, :],
                                                        start=u == 0, stop=u == f.units - 1)
                                if u == f.units - 1:
                                    last.then_inc(f.s.full, 1)

        def ffn_tensor(pe, f):
            m, r, s, n_in = Count(), Count(), Count(), Count()
            with loop(pe, B, (m, f.groups * f.units), (r, f.groups * f.units), (s, f.groups * ST), (n_in, f.groups), (T_PE, KT), (N_PE, 1)) as b:
                hold(pe, turn.free, T_PE.now() + 2)
                ffn_tensor_batch(pe, f, m, r, s, n_in, b)
                norm_tensor(pe)

        def ffn_scalar_batch(act, f, m, r):
            with loop(act, f.groups // f.per_turn, (m, f.units * f.per_turn), (r, f.units * f.per_turn)):
                for _ in range(f.per_turn * f.units):
                    act.wait_ge(f.r.free, r.now() + 1)
                    bank = full(act, f.m, m)
                    nc.scalar.activation(f.SILU[:, r.bank(), :], bank, ACT.Silu).then_inc(f.m.free, 1)
                    r.step()

        def ffn_scalar(act, f):
            m, r = Count(), Count()
            act.sem_inc(f.m.free, 2)
            with loop(act, B, (m, f.groups * f.units), (r, f.groups * f.units), (T_ACT, KT)) as b:
                ffn_scalar_batch(act, f, m, r)
                norm_scalar(act, (b + 1) & 1)

        def ffn_vector_batch(v, f, m, r, s, b, between=None, extra=()):
            with loop(v, f.groups // f.per_turn, (m, f.units * f.per_turn), (r, f.units * f.per_turn),
                      (s, ST * f.per_turn), *extra) as turn_:
                for q in range(f.per_turn):
                    for u in range(f.units):
                        v.wait_ge(f.m.free, m.step() + 2)
                        silu = f.SILU[:, r.bank(), :]
                        bank = full(v, f.r, r)
                        nc.vector.tensor_tensor(f.HIDDEN[:, u, :], silu, bank, ALU.mult).then_inc(f.r.free, 1)
                        if between:
                            between(turn_, u)
                    for st in range(ST):
                        if between and st % 2 == 0:
                            between(turn_, f.units + st // 2)
                        bank = full(v, f.s, s)
                        xb = X[:, ds(b * ST + st, 1), :].rearrange("p a n -> p (a n)")
                        nc.vector.scalar_tensor_tensor(out=xb, in0=bank, scalar=f.scale(b, turn_ * f.per_turn + q, st), in1=xb,
                                                       op0=ALU.mult, op1=ALU.add).then_inc(f.s.free, 1)
            v.wait_ge(f.s.free, s.now() + 2)
            v.sem_inc(x_done, 1)

        def ffn_vector(v, f):
            m, r, s = Count(), Count(), Count()
            v.sem_inc(f.r.free, 2)
            v.sem_inc(f.s.free, 2)
            with loop(v, B, (m, f.groups * f.units), (r, f.groups * f.units), (s, f.groups * ST), (T_V, KT), (N_V, 1)) as b:
                norm_vector(v, (b + 1) & 3)
                T_V.step(KT)
                ffn_vector_batch(v, f, m, r, s, b)

        l0f = Ffn("l0f", 1, l0_w13, w2h, UG, HID // P // UG, 1, lambda b, g, st: G[:, 4:5], ((wh_stored, 16),), ST, ST)
        assert l0f.groups == ST
        L0_M, L0_R = UG * ST + 2 + ST, UG * ST + ST
        HAD_M = HID // P

        def l0_tensor(pe):
            m, r, s, n_in = Count(), Count(), Count(), Count()

            def similarities(b):
                for w in (WQ0, WK0):
                    nc.tensor.matmul(start_job(pe, l0f.m, m), w, CT[:, ds(b * S, S)], start=True, stop=True).then_inc(l0f.m.full, 1)
                pe.wait_ge(l0f.m.free, m.now() + 2)
                for st in range(ST):
                    nc.tensor.matmul(start_job(pe, l0f.m, m), QT0[:, st * P:(st + 1) * P], KT0, start=True, stop=True)\
                      .then_inc(l0f.m.full, 1)

            def turn_graph(b):
                pe.wait_ge(graph_ready, b * ST + ST + 1)
                for j in range(ST):
                    bank = start_job(pe, l0f.r, r)
                    for i in range(ST):
                        last = nc.tensor.transpose(bank[:, i * P:(i + 1) * P], GRAPH[:, i, j * P:(j + 1) * P], ID[:, :])
                    last.then_inc(l0f.r.full, 1)

            pe.wait_ge(l0_w, 32)
            similarities(0)
            pe.wait_ge(butterflies, 8)
            for t in range(HAD_M):
                nc.tensor.matmul(start_job(pe, l0f.m, m), HAD, WH[0][:, t, :], start=True, stop=True).then_inc(l0f.m.full, 1)
            turn_graph(0)
            N_PE.step()
            norm_tensor(pe)
            with loop(pe, B - 1, (m, L0_M), (r, L0_R), (s, ST * ST), (n_in, ST), (T_PE, KT), (N_PE, 2)) as b:
                hold(pe, turn.free, T_PE.now() + 2)
                similarities(b + 1)
                ffn_tensor_batch(pe, l0f, m, r, s, n_in, b)
                turn_graph(b + 1)
                N_PE.step()
                norm_tensor(pe)
            pe.wait_ge(turn.free, T_PE.now() + 2)
            ffn_tensor_batch(pe, l0f, m, r, s, n_in, B - 1)
            norm_tensor(pe)

        def l0_scalar(act):
            m, r = Count(), Count()
            act.sem_inc(l0f.m.free, 2)

            def similarities(b):
                for dst in (QT0, KT0):
                    nc.scalar.copy(dst, full(act, l0f.m, m)).then_inc(l0f.m.free, 1)
                act.wait_ge(graph_ready, b * ST + 1)
                for st in range(ST):
                    bank = full(act, l0f.m, m)
                    nc.scalar.activation(SIM[:, st, :], bank, ACT.Copy, scale=float(1.0 / (L0_HEAD ** 0.5 * L0_HEADS)))
                    nc.scalar.activation(GRAPH[:, st, :], bank, ACT.Sigmoid, scale=float(1.0 / (L0_HEAD ** 0.5 * L0_HEADS)))\
                      .then_inc(l0f.m.free, 1)
            similarities(0)
            for t in range(HAD_M):
                nc.scalar.activation(WH[1][:, t, :], full(act, l0f.m, m), ACT.Copy, scale=float(HID ** -0.5)).then_inc(l0f.m.free, 1)
            r.step(ST)
            norm_scalar(act, 0)
            with loop(act, B - 1, (m, L0_M), (r, L0_R), (T_ACT, KT)) as b:
                similarities(b + 1)
                ffn_scalar_batch(act, l0f, m, r)
                r.step(ST)
                norm_scalar(act, (b + 1) & 1)
            ffn_scalar_batch(act, l0f, m, r)
            norm_scalar(act, 0)

        def l0_vector(v):
            m, r, s = Count(), Count(), Count()
            v.sem_inc(l0f.r.free, 2)
            v.sem_inc(l0f.s.free, 2)
            v.sem_inc(graph_ready, 1)
            v.wait_ge(gc_ready, 1)
            steps = 1 + 2 * TOP_ROUNDS - 1
            rows = lambda b, st: X[:, ds(b * ST + st, 1), :].rearrange("p a n -> p (a n)")

            def add_norm(b):
                v.wait_ge(xn_ready, N_V.now())
                for st in range(ST):
                    nc.vector.scalar_tensor_tensor(out=rows(b, st), in0=XN[:, st, :], scalar=GC[:, 1:2], in1=rows(b, st),
                                                   op0=ALU.mult, op1=ALU.add).then_inc(vec, 1)
                    V.step()

            def search(t0, t1, st):
                if t0 == 0:
                    link(v, nc.vector.tensor_copy(WORK.rearrange("p (a n) -> p a n", a=1), SIM[:, ds(st, 1), :]), True)
                for t in range(t0, t1):
                    link(v, nc.vector.max(TOP, WORK), t < TOP_ROUNDS - 1)
                    if t < TOP_ROUNDS - 1:
                        link(v, nc.vector.match_replace(WORK, TOP, WORK, -3.0e38), True)
                if t1 == TOP_ROUNDS:
                    at = (TOPK - 1) % 8
                    one = lambda t: t[:, ds(st, 1), :].rearrange("p a n -> p (a n)")
                    nc.vector.scalar_tensor_tensor(out=one(GRAPH), in0=one(SIM), scalar=TOP[:, at:at + 1],
                                                   in1=one(GRAPH), op0=ALU.is_ge, op1=ALU.mult).then_inc(graph_ready, 1)

            def add_graph(b):
                v.wait_ge(graph_ready, b * ST + ST + 1)
                for st in range(ST):
                    link(v, nc.vector.scalar_tensor_tensor(out=rows(b, st), in0=GRAPH[:, st, :], scalar=GC[:, 2:3], in1=rows(b, st),
                                                           op0=ALU.mult, op1=ALU.add))
                for st in range(ST):
                    nc.vector.scalar_tensor_tensor(out=rows(b, st), in0=full(v, l0f.r, r), scalar=GC[:, 2:3], in1=rows(b, st),
                                                   op0=ALU.mult, op1=ALU.add).then_inc(l0f.r.free, 1)
                v.wait_ge(l0f.r.free, r.now() + 2)
                v.sem_inc(x_done, 1)

            places = [TOP_ROUNDS * k // (UG + 2) for k in range(UG + 3)]
            add_norm(0)
            m.step(2 + ST)
            v.wait_ge(l0f.m.free, m.now() + 2)
            with loop(v, ST, (V, steps)) as st:
                search(0, TOP_ROUNDS, st)
            add_graph(0)
            m.step(HAD_M)
            norm_vector(v, 0)
            T_V.step(KT)
            with loop(v, B - 1, (m, L0_M), (r, L0_R), (s, ST * ST), (V, ST + ST * steps + ST), (T_V, KT), (N_V, 2)) as b:
                norm_vector(v, b + 1)
                add_norm(b + 1)
                m.step(2 + ST)
                hold(v, l0f.m.free, m.now() + 2)
                ffn_vector_batch(v, l0f, m, r, s, b, lambda g, k: search(places[k], places[k + 1], g), ((V, steps),))
                add_graph(b + 1)
                norm_vector(v, b + 1)
                T_V.step(KT)
            norm_vector(v, 0)
            T_V.step(KT)
            ffn_vector_batch(v, l0f, m, r, s, B - 1)

        l1m, l1r, l1s = rings("l1")
        a = area(FFN_AREA)
        WK1, CTB, KVT1, OUT1 = a(C), a(S), a(S), a(S)
        CT1 = a(B * S)
        KV1 = a(ST, C)
        PROB1 = a(ST, S)
        ROWS1 = a(2, S)
        BKR, BK1 = a(C), a(1)
        l1_w, ctb_ready = sem("l1_w"), sem("ctb_ready")
        var1_ready, root1_ready, norm1_ready, exp1_done, prob1_used = [sem(n) for n in (
            "var1_ready", "root1_ready", "norm1_ready", "exp1_done", "prob1_used")]

        def l1_sync(sp):
            sp.wait_ge(x_done, 2 * B)
            sp.dma_start(WK1, l1_wk).then_inc(l1_w, 16)
            sp.dma_start(CT1, ctx_t).then_inc(l1_w, 16)
            sp.dma_start(BK1, l1_bk).then_inc(l1_w, 16)
            sp.dma_start(BKR, l1_bk_row.to_broadcast([P, C])).then_inc(l1_w, 16)
            sp.dma_start(ROWS1, l1_ln.rearrange("(o a) n -> o a n", o=1).to_broadcast([P, 2, S])).then_inc(l1_w, 16)

        def l1_tensor(pe):
            m, r, s = Count(), Count(), Count()
            pe.wait_ge(x_done, 2 * B)
            pe.wait_ge(l1_w, 80)
            with loop(pe, B, (m, 2), (r, 1 + 1), (s, ST), (T_PE, KT), (N_PE, 1)) as b:
                hold(pe, turn.free, T_PE.now() + 2)
                hold(pe, ctb_ready, b + 1)
                nc.tensor.matmul(start_job(pe, l1m, m), WK1, CTB, start=True, stop=True).then_inc(l1m.full, 1)
                for half in range(2):
                    bank = start_job(pe, l1r, r)
                    for j in range(2):
                        jt = 2 * half + j
                        last = nc.tensor.matmul(bank[:, j * C:(j + 1) * C], CTB[:, jt * P:(jt + 1) * P], WK1, start=True, stop=True)
                    last.then_inc(l1r.full, 1)
                hold(pe, l1r.free, r.now() + 2)
                bank = start_job(pe, l1m, m)
                for jt in range(ST):
                    last = nc.tensor.matmul(bank.rearrange("p (a n) -> p a n", a=1), KV1[:, jt, :], XT[:, ds(b & 1, 1), jt, :],
                                            start=jt == 0, stop=jt == ST - 1)
                last.then_inc(l1m.full, 1)
                pe.wait_ge(l1m.free, m.now() + 2)
                for st in range(ST):
                    nc.tensor.matmul(start_job(pe, l1s, s), OUT1[:, st * P:(st + 1) * P], KVT1, start=True, stop=True)\
                      .then_inc(l1s.full, 1)
                norm_tensor(pe)

        def l1_scalar(act):
            m, s = Count(), Count()
            act.sem_inc(l1m.free, 2)
            act.sem_inc(l1s.free, 2)
            with loop(act, B, (m, 2), (s, ST), (T_ACT, KT)) as b:
                nc.scalar.activation(KVT1, full(act, l1m, m), ACT.Identity, bias=BK1).then_inc(l1m.free, 1)
                nc.scalar.copy(OUT1, full(act, l1m, m)).then_inc(l1m.free, 1)
                act.wait_ge(prob1_used, b + 1)
                for st in range(ST):
                    nc.scalar.copy(PROB1[:, st, :], full(act, l1s, s)).then_inc(l1s.free, 1)
                norm_scalar(act, (b + 1) & 1)
                act.wait_ge(norm1_ready, b + 1)
                for st in range(ST):
                    nc.scalar.activation(PROB1[:, st, :], PROB1[:, st, :], ACT.Exp, bias=NEGM1[:, st:st + 1],
                                         accum_out=SUM1[:, st:st + 1]).then_inc(exp1_done, 1)

        def l1_vector(v):
            r, s = Count(), Count()
            v.sem_inc(l1r.free, 2)
            v.sem_inc(prob1_used, 1)
            v.wait_ge(l1_w, 80)
            scale = float(512 ** -0.5)
            with loop(v, B, (r, 2), (s, ST), (V, 2 * ST - 1 + 7), (T_V, KT), (N_V, 1)) as b:
                for half in range(2):
                    bank = full(v, l1r, r)
                    nc.vector.tensor_tensor(KV1[:, 2 * half:2 * half + 2, :], bank[:, 0:2 * C].rearrange("p (j c) -> p j c", j=2),
                                            BKR.rearrange("p (a c) -> p a c", a=1).to_broadcast([P, 2, C]), ALU.add)\
                      .then_inc(l1r.free, 1)
                norm_vector(v, (b + 1) & 3)
                T_V.step(KT)
                for st in range(ST):
                    s.step()
                    hold(v, l1s.free, s.now() + 2)
                    nc.vector.bn_stats(STAT[:, st, :], PROB1[:, st, :]).then_inc(vec, 1)
                    V.step()
                hold(v, vec, V.now())
                for st in range(ST):
                    last = nc.vector.bn_aggr(MV[:, st, :], STAT[:, st, :])
                link(v, last)
                nc.vector.tensor_scalar(VAR1, MV[:, :, 1], scale * scale, EPS_INNER, ALU.mult, ALU.add).then_inc(var1_ready, 1)
                v.wait_ge(root1_ready, b + 1)
                link(v, nc.vector.tensor_scalar(RS1, RS1, scale, None, ALU.mult))
                for st in range(ST):
                    last = nc.vector.tensor_scalar(PROB1[:, st, :], PROB1[:, st, :], MV[:, st, 0:1], RS1[:, st:st + 1],
                                                   ALU.subtract, ALU.mult)
                link(v, last)
                for row, op in ((0, ALU.mult), (1, ALU.add)):
                    link(v, nc.vector.tensor_tensor(PROB1, PROB1, ROWS1[:, row:row + 1, :].to_broadcast([P, ST, S]), op))
                nc.vector.tensor_reduce(NEGM1, PROB1, op=ALU.max, axis=AX.X, negate=True).then_inc(norm1_ready, 1)
                v.wait_ge(exp1_done, b * ST + ST)
                link(v, nc.vector.reciprocal(SUM1, SUM1))
                link(v, nc.vector.tensor_scalar(SUM1, SUM1, G[:, 1:2], None, ALU.mult))
                for st in range(ST):
                    xb = X[:, ds(b * ST + st, 1), :].rearrange("p a n -> p (a n)")
                    last = nc.vector.scalar_tensor_tensor(out=xb, in0=PROB1[:, st, :], scalar=SUM1[:, st:st + 1], in1=xb,
                                                          op0=ALU.mult, op1=ALU.add)
                    if st < ST - 1:
                        last.then_inc(vec, 1)
                        V.step()
                last.then_inc(prob1_used, 1)
                v.wait_ge(prob1_used, b + 2)
                v.sem_inc(x_done, 1)

        def l1_pool(pool):
            pool.wait_ge(l1_w, 80)
            with loop(pool, B, (N_P, 1)) as b:
                pool.wait_ge(l1r.free, b * 2 + 2)
                nc.gpsimd.tensor_copy(CTB, CT1[:, ds(b * S, S)]).then_inc(ctb_ready, 1)
                norm_pool(pool)
                pool.wait_ge(var1_ready, b + 1)
                nc.gpsimd.tensor_tensor(RS1, VAR1, HALF[:, :], ALU.pow).then_inc(root1_ready, 1)

        la, lr, ls = rings("l1f")
        a = area()
        AGG, D1, D2, BC, GATE = a(KT, D), a(KT, HID), a(HID // P, D), a(KT, D), a(KT, D)
        COLS = a(40)
        COL = {}
        for name, n in (("agg", 4), ("d1", 16), ("d2", 4), ("bc", 4), ("gate", 4), ("pn_g", 4), ("pn_b", 4)):
            COL[name] = COLS[:, sum(c[1] for c in COL.values()):sum(c[1] for c in COL.values()) + n], n
        COL = {k: c[0] for k, c in COL.items()}
        OROWS = a(2, D)
        TH, TC, TN, SQ, BCT, T0 = a(4 * B), a(4 * B), a(4 * B), a(4 * B), a(4 * B), a(4 * B)
        HP, GL = a(16 * B), a(16 * B)
        MU, VT, RT = a(B), a(B), a(B)
        MEAN = a(P)
        assert FFN_AREA >= 22528 + 40 + 1024 + 96 + 128 + 12 + P
        a = area(FFN_AREA)
        GT, OT, ON = a(KT, S), a(KT, S), a(ST, D)
        XL, INR = a(D), a(2, D)
        SL, ML, VL, RL = a(6), a(2), a(1), a(1)
        l1f_w, l1f_in, xl_in = sem("l1f_w"), sem("l1f_in"), sem("xl_in")
        th_ready, root_in, root_out = sem("th_ready"), sem("root_in"), sem("root_out")
        gelu_done, mix_done, out_norm = sem("gelu_done"), sem("mix_done"), sem("out_norm")
        t0_done = sem("t0_done")
        ROOTS = 2 + K_STEPS

        def l1f_sync_weights(sp):
            for dst, src in ((AGG, l1_agg), (D1, l1_d1), (D2, l1_d2), (BC, l1_bc), (GATE, l1_gate), (COLS, l1_cols)):
                sp.dma_start(dst, src).then_inc(l1f_w, 16)
            sp.dma_start(OROWS, l1_rows.rearrange("(o a) n -> o a n", o=1).to_broadcast([P, 2, D])).then_inc(l1f_w, 16)

        def l1f_sync(sp):
            sp.wait_ge(x_done, 3 * B)
            for b in range(B):
                sp.dma_start(XL[b:b + 1, :], X[P - 1:P, b * ST + ST - 1, :]).then_inc(xl_in, 16)
            sp.dma_start(INR[0:B, :, :], l1_inrows.rearrange("(o a) n -> o a n", o=1).to_broadcast([B, 2, D])).then_inc(xl_in, 16)

        def cols(t):
            return t.rearrange("p (m b) -> p m b", b=B)

        def over_b(col, n):
            return col.rearrange("p (m o) -> p m o", o=1).to_broadcast([P, n, B])

        def over_m(t):
            return t.rearrange("p (o b) -> p o b", o=1).to_broadcast([P, 4, B])

        def small_products(pe, n, w, of, tiles_in, tiles_out):
            bank = start_job(pe, lr, n)
            for mt in range(tiles_out):
                for kt in range(tiles_in):
                    last = nc.tensor.matmul(bank[:, mt * B:(mt + 1) * B], w[:, kt, mt * P:(mt + 1) * P], of[:, kt * B:(kt + 1) * B],
                                            start=kt == 0, stop=kt == tiles_in - 1)
            last.then_inc(lr.full, 1)

        def l1f_tensor(pe):
            m, r, s, th, gl = Count(), Count(), Count(), Count(), Count()
            pe.wait_ge(x_done, 3 * B)
            pe.wait_ge(l1f_w, 7 * 16)
            pe.wait_ge(th_ready, th.step())
            bank = start_job(pe, la, m)
            for kt in range(KT):
                last = nc.tensor.transpose(bank[:, kt * B:(kt + 1) * B], XL[0:B, kt * P:(kt + 1) * P], ID[0:B, 0:B])
            last.then_inc(la.full, 1)
            pe.wait_ge(la.free, m.now() + 2)
            small_products(pe, r, AGG, T0, KT, KT)
            pe.wait_ge(th_ready, th.step())
            with loop(pe, K_STEPS, (r, 4), (th, 3), (gl, 1)):
                nc.tensor.matmul(start_job(pe, lr, r)[:, 0:4 * B], MEAN, TH, start=True, stop=True).then_inc(lr.full, 1)
                hold(pe, th_ready, th.step())
                nc.tensor.matmul(start_job(pe, lr, r)[:, 0:4 * B], MEAN, SQ, start=True, stop=True).then_inc(lr.full, 1)
                hold(pe, th_ready, th.step())
                small_products(pe, r, D1, TN, KT, HID // P)
                hold(pe, gelu_done, gl.step())
                small_products(pe, r, D2, GL, HID // P, KT)
                hold(pe, th_ready, th.step())
            small_products(pe, r, BC, TH, KT, KT)
            m.step()
            bank = BM[:, 1, :]
            nc.tensor.matmul(bank[:, 0:P], ID[:, :], ID[:, :], start=True, stop=True).then_inc(la.full, 1)
            with loop(pe, B, (m, KT), (s, ST), (T_PE, KT), (N_PE, 1)) as b:
                hold(pe, turn.free, T_PE.now() + 2)
                for mt in range(KT):
                    bank = start_job(pe, la, m)
                    for kt in range(KT):
                        last = nc.tensor.matmul(bank.rearrange("p (a n) -> p a n", a=1), GATE[:, kt, mt * P:(mt + 1) * P],
                                                XT[:, ds(b & 1, 1), kt, :], start=kt == 0, stop=kt == KT - 1)
                    last.then_inc(la.full, 1)
                for st in range(ST):
                    if st == 0:
                        hold(pe, mix_done, b * KT + KT + 1)
                    bank = start_job(pe, ls, s)
                    for mt in range(KT):
                        last = nc.tensor.transpose(bank[:, mt * P:(mt + 1) * P], OT[:, mt, st * P:(st + 1) * P], ID[:, :])
                    last.then_inc(ls.full, 1)
                norm_tensor(pe)

        def l1f_scalar(act):
            m, s = Count(), Count()
            act.sem_inc(la.free, 2)
            act.sem_inc(ls.free, 2)
            nc.scalar.copy(T0, full(act, la, m)[:, 0:4 * B]).then_inc(la.free, 1)
            with act.Fori(0, K_STEPS) as k:
                act.wait_ge(t0_done, k + 1)
                nc.scalar.activation(GL, HP, ACT.Gelu).then_inc(gelu_done, 1)
            nc.scalar.copy(T0[:, 0:1], full(act, la, m)[:, 0:1]).then_inc(la.free, 1)
            with loop(act, B, (m, KT), (s, ST), (T_ACT, KT)) as b:
                act.wait_ge(mix_done, b * KT + 1)
                for mt in range(KT):
                    nc.scalar.activation(GT[:, mt, :], full(act, la, m), ACT.Sigmoid, bias=COL["gate"][:, mt:mt + 1]).then_inc(la.free, 1)
                act.wait_ge(out_norm, b * 2 + 1)
                for st in range(ST):
                    nc.scalar.copy(ON[:, st, :], full(act, ls, s)).then_inc(ls.free, 1)
                norm_scalar(act, (b + 1) & 1)

        def l1f_vector(v):
            m, r, s, t0, root = Count(), Count(), Count(), Count(), Count()
            for q in (lr.free, mix_done, out_norm):
                v.sem_inc(q, 2 if q is lr.free else 1)
            v.wait_ge(l1f_w, 7 * 16)
            nc.vector.memset(MEAN, 1.0 / D).then_inc(vec, 1)
            V.step()
            link(v, nc.vector.tensor_scalar(OROWS, OROWS, G[:, 5:6], None, ALU.mult))
            v.wait_ge(xl_in, 5 * 16)
            for eps in (EPS_BLOCK, EPS_INNER):
                link(v, nc.vector.bn_stats(SL[0:B, :], XL[0:B, :]))
                link(v, nc.vector.bn_aggr(ML[0:B, :], SL[0:B, :]))
                nc.vector.tensor_scalar(VL[0:B, :], ML[0:B, 1:2], eps, None, ALU.add).then_inc(root_in, 1)
                v.wait_ge(root_out, root.step())
                link(v, nc.vector.tensor_scalar(XL[0:B, :], XL[0:B, :], ML[0:B, 0:1], RL[0:B, :], ALU.subtract, ALU.mult))
            link(v, nc.vector.tensor_tensor(XL[0:B, :], XL[0:B, :], INR[0:B, 0, :], ALU.mult))
            nc.vector.tensor_tensor(XL[0:B, :], XL[0:B, :], INR[0:B, 1, :], ALU.add).then_inc(th_ready, 1)
            bank = full(v, lr, r)
            nc.vector.tensor_tensor(cols(TH), cols(bank[:, 0:4 * B]), over_b(COL["agg"], 4), ALU.add).then_inc(lr.free, 1)
            v.wait_ge(lr.free, r.now() + 2)
            v.sem_inc(th_ready, 1)
            with loop(v, K_STEPS, (r, 4), (V, 7), (t0, 1), (root, 1)):
                bank = full(v, lr, r)
                link(v, nc.vector.tensor_reduce(MU, bank[:, 0:4 * B].rearrange("p (m b) -> p b m", b=B), op=ALU.add, axis=AX.X))
                link(v, nc.vector.tensor_tensor(cols(TC), cols(TH), over_m(MU), ALU.subtract))
                nc.vector.tensor_tensor(SQ, TC, TC, ALU.mult).then_inc(lr.free, 1)
                v.wait_ge(lr.free, r.now() + 2)
                v.sem_inc(th_ready, 1)
                bank = full(v, lr, r)
                link(v, nc.vector.tensor_reduce(MU, bank[:, 0:4 * B].rearrange("p (m b) -> p b m", b=B), op=ALU.add, axis=AX.X))
                nc.vector.tensor_scalar(VT, MU, EPS_INNER, None, ALU.add).then_inc(root_in, 1)
                v.wait_ge(root_out, root.step())
                link(v, nc.vector.tensor_tensor(cols(TC), cols(TC), over_m(RT), ALU.mult))
                link(v, nc.vector.tensor_tensor(cols(TC), cols(TC), over_b(COL["pn_g"], 4), ALU.mult))
                nc.vector.tensor_tensor(cols(TN), cols(TC), over_b(COL["pn_b"], 4), ALU.add).then_inc(lr.free, 1)
                v.wait_ge(lr.free, r.now() + 2)
                v.sem_inc(th_ready, 1)
                bank = full(v, lr, r)
                nc.vector.tensor_tensor(cols(HP), cols(bank[:, 0:16 * B]), over_b(COL["d1"], 16), ALU.add).then_inc(lr.free, 1)
                v.wait_ge(lr.free, r.now() + 2)
                v.sem_inc(t0_done, 1)
                t0.step()
                bank = full(v, lr, r)
                link(v, nc.vector.tensor_tensor(cols(TC), cols(bank[:, 0:4 * B]), over_b(COL["d2"], 4), ALU.add))
                nc.vector.tensor_tensor(TH, TH, TC, ALU.add).then_inc(lr.free, 1)
                v.wait_ge(lr.free, r.now() + 2)
                v.sem_inc(th_ready, 1)
                V.step()
                v.sem_inc(vec, 1)
            bank = full(v, lr, r)
            nc.vector.tensor_tensor(cols(BCT), cols(bank[:, 0:4 * B]), over_b(COL["bc"], 4), ALU.add).then_inc(lr.free, 1)
            v.wait_ge(lr.free, r.now() + 2)
            m.step(2)
            with loop(v, B, (m, KT), (s, ST), (V, ST + 1 + 1 + 2), (T_V, KT), (N_V, 1), (root, 1)) as b:
                norm_vector(v, (b + 1) & 3)
                T_V.step(KT)
                for mt in range(KT):
                    m.step()
                    v.wait_ge(la.free, m.now() + 2)
                    one = lambda t: t.rearrange("p (a n) -> p a n", a=1)
                    nc.vector.scalar_tensor_tensor(out=one(OT[:, mt, :]), in0=one(GT[:, mt, :]), scalar=BCT[:, ds(mt * B + b, 1)],
                                                   in1=XT[:, ds(b & 1, 1), mt, :], op0=ALU.mult, op1=ALU.add).then_inc(mix_done, 1)
                for st in range(ST):
                    s.step()
                    hold(v, ls.free, s.now() + 2)
                    nc.vector.bn_stats(STAT[:, st, :], ON[:, st, :]).then_inc(vec, 1)
                    V.step()
                hold(v, vec, V.now())
                for st in range(ST):
                    last = nc.vector.bn_aggr(MV[:, st, :], STAT[:, st, :])
                link(v, last)
                nc.vector.tensor_scalar(VAR1, MV[:, :, 1], EPS_INNER, None, ALU.add).then_inc(root_in, 1)
                v.wait_ge(root_out, root.step())
                for st in range(ST):
                    last = nc.vector.tensor_scalar(ON[:, st, :], ON[:, st, :], MV[:, st, 0:1], RS1[:, st:st + 1],
                                                   ALU.subtract, ALU.mult)
                link(v, last)
                link(v, nc.vector.tensor_tensor(ON, ON, OROWS[:, 0:1, :].to_broadcast([P, ST, D]), ALU.mult))
                nc.vector.tensor_tensor(ON, ON, OROWS[:, 1:2, :].to_broadcast([P, ST, D]), ALU.add).then_inc(out_norm, 1)
                v.wait_ge(out_norm, b * 2 + 2)
                xb = X[:, ds(b * ST, ST), :]
                nc.vector.tensor_tensor(xb, xb, ON, ALU.add).then_inc(out_norm, 1)
                v.wait_ge(out_norm, b * 2 + 3)
                v.sem_inc(x_done, 1)
                v.sem_inc(vec, 1)
                V.step()

        def l1f_pool(pool):
            for n in range(2):
                pool.wait_ge(root_in, n + 1)
                nc.gpsimd.tensor_tensor(RL[0:B, :], VL[0:B, :], HALF[0:B, 0:1], ALU.pow).then_inc(root_out, 1)
            with pool.Fori(0, K_STEPS) as k:
                pool.wait_ge(root_in, k + 3)
                nc.gpsimd.tensor_tensor(RT, VT, HALF[:, 0:B], ALU.pow).then_inc(root_out, 1)
            with loop(pool, B, (N_P, 1)) as b:
                norm_pool(pool)
                pool.wait_ge(root_in, b + ROOTS + 1)
                nc.gpsimd.tensor_tensor(RS1, VAR1, HALF[:, :], ALU.pow).then_inc(root_out, 1)

        ar, as_ = ring(BR, "l2_r"), ring(BS, "l2_s")
        aq = Ring(BM[:, 0:1, :], sem("l2_q_full"), sem("l2_q_free"))
        ao = Ring(BM[:, 1:2, :], sem("l2_out_full"), sem("l2_out_free"))
        a = area()
        CN2 = a(B * ST, C)
        KRAW = a(KVH, S)
        QHI, QLO = a(ST, D), a(ST, D)
        QST = a(2, ST, P)
        PROB2, PROBT2 = a(2 * ST, S), a(ST, S)
        VWIN = a(2 * ST, 240)
        OUT2, TMP2 = a(S), a(S)
        SUM2, RS2, NEG2 = a(2 * ST), a(ST * 8), a(2 * ST)
        KPARTS = sb("KPARTS", [P, KVH, S], F32R)
        QPARTS = sb("QPARTS", [P, 2, S], F32R)
        HG = QH // 8
        zeroed, kraw_in, cn2_in, kparts_ready, q_cut = [sem(n) for n in ("zeroed", "kraw_in", "cn2_in", "kparts_ready", "q_cut")]
        q_staged, v_staged, max_done, mixed = [sem(n) for n in ("q_staged", "v_staged", "max_done", "mixed")]

        def l2_sync(sp):
            sp.wait_ge(x_done, 4 * B)
            sp.dma_start(CN2, ctx_n.rearrange("(n p) d -> p n d", p=P)).then_inc(cn2_in, 16)
            sp.wait_ge(zeroed, 3)
            with sp.Fori(0, B) as b:
                sp.wait_ge(kparts_ready, b + 1)
                for q in range(4):
                    sp.dma_start(KRAW[32 * q:32 * q + HD, :, :],
                                 ctx_t[:, ds(b * S, S)].rearrange("(k d) t -> d k t", d=HD)).then_inc(kraw_in, 16)

        def l2_tensor(pe):
            r, s, q, o, vs = Count(), Count(), Count(), Count(), Count()
            pe.wait_ge(x_done, 4 * B)

            def turn_queries(j):
                hold(pe, q_staged, q.now() + 1)
                bank = start_job(pe, aq, q)
                for st in range(ST):
                    last = nc.tensor.transpose(bank[:, st * P:(st + 1) * P], QST[:, j % 2, st, :], ID[:, :])
                last.then_inc(aq.full, 1)

            def scores(j, st, key):
                nc.tensor.matmul(start_job(pe, as_, s).rearrange("p (a n) -> p a n", a=1),
                                 QPARTS[:, j % 2, st * P:(st + 1) * P], KPARTS[:, ds(key, 1), :],
                                 start=True, stop=True).then_inc(as_.full, 1)

            def mix_values(j, lt, bank, copied):
                pe.wait_ge(*copied)
                return nc.tensor.matmul(bank, VWIN[:, (j // 4) * ST + lt, 112 - HD * j:240 - HD * j], PROBT2[:, lt, :],
                                        start=j == 0 and lt == 0, stop=j == 7 and lt == ST - 1)

            with loop(pe, B, (r, 2 * QH + 2 * HG), (s, ST * QH + ST), (q, QH + 2), (o, HG), (T_PE, 2 * QH + KT), (N_PE, 1), (vs, 2 * HG)) as b:
                hold(pe, kparts_ready, b + 2)
                turn_queries(0)
                turn_queries(1)
                hold(pe, aq.free, q.now())
                for st in range(ST):
                    scores(0, st, 0)
                with loop(pe, HG, (r, 18), (s, ST * 8), (q, 8), (o, 1), (T_PE, 16), (vs, 2)) as hg:
                    for j in range(8):
                        copied = [None] * ST
                        hold(pe, aq.free, q.now() + 1)
                        hold(pe, as_.free, s.now() + 2)
                        for k in range(ST):
                            scores(j + 1, k, (hg * 2 + (j + 1) // 4) & (KVH - 1))
                            job, n = (turn, T_PE) if k % 2 == 0 else (ar, r)
                            bank = start_job(pe, job, n)
                            for st in range(ST):
                                last = nc.tensor.transpose(bank[:, st * P:(st + 1) * P], PROB2[:, (j % 2) * ST + st, k * P:(k + 1) * P], ID[:, :])
                            last.then_inc(job.full, 1)
                            copied[k] = job.free, n.now() + 2
                            if k == 1 and j == 0:
                                out_bank = start_job(pe, ao, o)
                            if k == 1 and j % 4 == 0:
                                hold(pe, v_staged, vs.step())
                            if k:
                                mix_values(j, k - 1, out_bank, copied[k - 1])
                        turn_queries(j)
                        last = mix_values(j, ST - 1, out_bank, copied[ST - 1])
                        last.then_inc(mixed, 1)
                    hold(pe, mixed, b * QH + hg * 8 + 9)
                    pe.sem_inc(ao.full, 1)
                    hold(pe, ao.free, o.now() + 1)
                    for half in range(2):
                        bank = start_job(pe, ar, r)
                        for st in range(2):
                            at = (2 * half + st) * P
                            last = nc.tensor.transpose(bank[:, st * P:(st + 1) * P], OUT2[:, at:at + P], ID[:, :])
                        last.then_inc(ar.full, 1)
                norm_tensor(pe)

        def l2_scalar(act):
            s, q, o = Count(), Count(), Count()
            act.sem_inc(as_.free, 2)
            act.sem_inc(aq.free, 1)
            act.sem_inc(ao.free, 1)
            act.sem_inc(mixed, 1)

            def queries(j):
                nc.scalar.copy(QPARTS[:, j % 2, :], full(act, aq, q)).then_inc(aq.free, 1)

            def exps(j, st):
                act.wait_ge(max_done, s.now() + 1)
                bank = full(act, as_, s)
                nc.scalar.activation(PROB2[:, (j % 2) * ST + st, :], bank, ACT.Exp, bias=NEG2[:, (j % 2) * ST + st:(j % 2) * ST + st + 1],
                                     accum_out=SUM2[:, (j % 2) * ST + st:(j % 2) * ST + st + 1]).then_inc(as_.free, 1)

            with loop(act, B, (s, ST * QH + ST), (q, QH + 2), (o, HG), (T_ACT, 2 * QH + KT)) as b:
                queries(0)
                queries(1)
                for st in range(ST):
                    exps(0, st)
                with loop(act, HG, (s, ST * 8), (q, 8), (o, 1), (T_ACT, 16)) as hg:
                    for j in range(8):
                        for st in range(ST):
                            if st % 2 == 0:
                                nc.scalar.copy(PROBT2[:, st, :], full(act, turn, T_ACT)).then_inc(turn.free, 1)
                            exps(j + 1, st)
                        queries(j)
                    nc.scalar.copy(OUT2, full(act, ao, o)).then_inc(ao.free, 1)
                norm_scalar(act, (b + 1) & 1)

        def l2_vector(v):
            r, s, q = Count(), Count(), Count()
            v.sem_inc(ar.free, 2)
            v.sem_inc(kparts_ready, 1)

            def maximum(j, st):
                at = (j % 2) * ST + st
                nc.vector.tensor_reduce(NEG2[:, at:at + 1], full(v, as_, s), op=ALU.max, axis=AX.X, negate=True).then_inc(max_done, 1)

            with loop(v, B, (r, 2 * QH + 2 * HG), (s, ST * QH + ST), (q, QH + 2), (V, 2 + (8 + 3) * HG), (T_V, 2 * QH + KT), (N_V, 1)) as b:
                v.wait_ge(kraw_in, b * 64 + 64)
                nc.vector.tensor_copy(KPARTS[0:64, :, :], KRAW[0:64, :, :])
                link(v, nc.vector.tensor_copy(KPARTS[64:128, :, :], KRAW[64:128, :, :]))
                nc.vector.tensor_tensor(KPARTS[64:128, :, :], KRAW[64:128, :, :], KPARTS[64:128, :, :].bitcast(F32), ALU.subtract)\
                  .then_inc(kparts_ready, 1)
                v.wait_ge(aq.free, q.now() + 1)
                q.step(QH + 2)
                link(v, nc.vector.tensor_scalar(QHI.bitcast(F32R), XN[:, :, :], HD ** -0.5, None, ALU.mult))
                nc.vector.scalar_tensor_tensor(out=QLO, in0=XN[:, :, :], scalar=HD ** -0.5, in1=QHI, op0=ALU.mult, op1=ALU.subtract)\
                  .then_inc(q_cut, 1)
                v.wait_ge(q_cut, b + 1)
                for st in range(ST):
                    maximum(0, st)
                norm_vector(v, (b + 1) & 3)
                with loop(v, HG, (r, 18), (s, ST * 8), (V, 11), (T_V, 16)) as hg:
                    for j in range(8):
                        hold(v, as_.free, s.now() + 2)
                        nc.vector.reciprocal(RS2.rearrange("p (s e) -> p s e", e=8)[:, :, j:j + 1],
                                             SUM2[:, (j % 2) * ST:(j % 2) * ST + ST].rearrange("p (s o) -> p s o", o=1)).then_inc(vec, 1)
                        V.step()
                        for st in range(ST):
                            maximum(j + 1, st)
                            if st % 2 == 1:
                                nc.vector.tensor_copy(PROBT2[:, st, :], full(v, ar, r)).then_inc(ar.free, 1)
                        T_V.step(2)
                    v.wait_ge(vec, V.now())
                    link(v, nc.vector.tensor_scalar(RS2, RS2, G[:, 2:3], None, ALU.mult))
                    for half in range(2):
                        bank = full(v, ar, r)
                        last = nc.vector.tensor_tensor(TMP2[:, half * 2 * P:(half + 1) * 2 * P].rearrange("p (a d) -> p a d", d=HD),
                                                       bank[:, 0:2 * P].rearrange("p (a d) -> p a d", d=HD),
                                                       RS2[:, half * 16:(half + 1) * 16].rearrange("p (a o) -> p a o", o=1).to_broadcast([P, 16, HD]), ALU.mult)
                        last.then_inc(ar.free, 1)
                    v.wait_ge(ar.free, r.now() + 2)
                    xb = X[:, ds(b * ST, ST), ds(hg * 8 * HD, 8 * HD)]
                    link(v, nc.vector.tensor_tensor(xb, xb, TMP2.rearrange("p (s n) -> p s n", s=ST), ALU.add))
                    v.sem_inc(vec, 1)
                    V.step()
                T_V.step(KT)
                v.sem_inc(x_done, 1)

        def l2_pool(pool):
            q = Count()
            pool.wait_ge(x_done, 4 * B)
            for t in (KRAW, QST, VWIN):
                nc.gpsimd.memset(t, 0.0).then_inc(zeroed, 1)
            pool.wait_ge(zeroed, 3)
            pool.wait_ge(cn2_in, 16)

            def stage_queries(j, head):
                to = QST[:, j % 2, :, :].rearrange("p s (a two w) -> p s a two w", two=2, w=32)
                for part, of in ((0, QHI), (1, QLO)):
                    src = of[:, :, ds(head * HD, HD)].rearrange("p s (a d) -> p s a d", a=1)
                    last = nc.gpsimd.tensor_copy(to[:, :, :, part, 0:HD], src.to_broadcast([P, ST, 2, HD]))
                last.then_inc(q_staged, 1)

            def stage_values(u, group):
                nc.gpsimd.tensor_copy(VWIN[:, u * ST:(u + 1) * ST, 112:128],
                                      CN2[:, ds(((group >> 2) & 3) * ST, ST), ds(((group & 3) * 2 + u) * HD, HD)]).then_inc(v_staged, 1)
            nc.gpsimd.tensor_copy(VWIN[:, 0:ST, 112:128], CN2[:, 0:ST, 0:HD]).then_inc(v_staged, 1)
            with loop(pool, B, (q, QH + 2), (N_P, 1)) as b:
                hold(pool, q_cut, b + 1)
                hold(pool, aq.free, q.now() + 1)
                for j in range(2):
                    stage_queries(j, b * 0 + j)
                    q.step()
                norm_pool(pool)
                with loop(pool, HG, (q, 8)) as hg:
                    hold(pool, mixed, b * QH + hg * 8 + 1)
                    stage_values(1, b * HG + hg)
                    for j in range(8):
                        hold(pool, aq.free, q.now())
                        stage_queries(j, (hg * 8 + j + 2) & (QH - 1))
                        q.step()
                        if j == 5:
                            hold(pool, mixed, b * QH + hg * 8 + 5)
                            stage_values(0, b * HG + hg + 1)

        xnd = nc.dram_tensor("xnd", [B * S, D], F32, kind="Internal").ap()
        table = nc.dram_tensor("table", [P * TW, 1], I32, kind="Internal").ap()
        made = nc.dram_tensor("made", [NT * P, D], F32, kind="Internal").ap()
        em, er, es = rings("l2f")
        et = ring(BT, "l2f_t")
        a = area()
        EW1 = a(E * KT, 2 * I)
        EW2 = a(2, EK * D)
        XG, XGT = a(2, D), a(2, KT * P)
        EHT = a(2, EK * P)
        RW = a(KT, E)
        TRI, ONE = a(P), a(P)
        EC = a(E + 16 + TW)
        TOK = a(B * ST).bitcast(I32)
        n128 = B * ST * E
        MX0, MX1, MS, EX, WT0, WT1, POS0, POS1 = [a(B * ST) for _ in range(8)]
        IDX0, IDX1, YP0, YP1 = [a(B * ST).bitcast(I32) for _ in range(4)]
        NTL, END0, END1, START = a(E), a(E), a(E), a(E)
        EXF = a(TW)
        EXPERT, SLOTS = a(TW).bitcast(I32), a(TW).bitcast(I32)
        IX = [a(1).bitcast(I32) for _ in range(2)]
        here = a.here()
        a, a2 = area(here), area(here)
        LG, LG2, EQ, OH0, OH1, OHS, RANK, TOTAL, SCAN0, SCAN1 = [a(B * ST, E) for _ in range(10)]
        CMP, LT = a(TW, E), a(S)
        ESILU, EHID, YE = a2(2, I), a2(2, I), a2(2, D)
        YG = [XG[:, 0, :], XG[:, 1, :], XGT[:, 0, :], XGT[:, 1, :]]
        ew_in, xnd_in, router_in = sem("ew_in"), sem("xnd_in"), sem("router_in")
        pair_exp_in, pair_exp, ones_ready, routed = sem("pair_exp_in"), sem("pair_exp"), sem("ones_ready"), sem("routed")
        table_zero, table_in, slots_in = sem("table_zero"), sem("table_in"), sem("slots_in")
        ix_ready = sem("ix_ready")
        xg_in, ew2_in, y_stored = [[sem(f"{n}{u}") for u in range(2)] for n in ("xg_in", "ew2_in", "y_stored")]
        y_ready, yg_used, e_zero = sem("y_ready"), sem("yg_used"), sem("e_zero")
        yg_in = [sem(f"yg_in{k}") for k in range(4)]
        ZERO = sb("ZERO", [P, TW], I32)
        ROUTE_R = B + 2

        def moe_sync(sp):
            sp.wait_ge(x_done, 5 * B)
            for dst, src in ((RW, l2_router), (EC, moe_row.to_broadcast([P, E + 16 + TW])), (TRI, moe_tri), (TOK, moe_token)):
                sp.dma_start(dst, src).then_inc(router_in, 16)
            for e in range(E):
                sp.dma_start(EW1[:, e * KT:(e + 1) * KT, :], l2_w12[:, e * KT:(e + 1) * KT, :]).then_inc(ew_in, 16)
            for b in range(B):
                sp.wait_ge(xn_ready, 5 * B + b + 1)
                sp.dma_start(xnd[b * S:(b + 1) * S, :].rearrange("(s p) d -> p s d", p=P), XN[:, :, :]).then_inc(xnd_in, 16)
            sp.wait_ge(table_in, 2 * B * ST * 16)
            sp.dma_start(SLOTS, table.rearrange("(p n) o -> p (n o)", p=P)).then_inc(slots_in, 16)
            sp.wait_ge(routed, 1)

            def down(u, t):
                e = sp.value_load(EXPERT[0:1, ds(t, 1)], min_val=0, max_val=E - 1)
                sp.dma_start(EW2[:, u, :].rearrange("p (a n) -> p a n", a=1), l2_w2[ds(e, 1)].rearrange("a p n -> p a n"))\
                  .then_inc(ew2_in[u], 16)
            down(1, 0)
            down(0, 0)
            with sp.Fori(0, NT // 2) as i:
                for u in range(2):
                    sp.wait_ge(er.full, ROUTE_R + i * 4 + 2 * u + 2)
                    down(1 - u, i * 2 + u + 1)
                    sp.wait_ge(y_ready, i * 2 + u + 1)
                    sp.dma_start(made[ds((i * 2 + u) * P, P), :], YE[:, u, :]).then_inc(y_stored[u], 16)

        def moe_tensor(pe):
            m, r, s, t = Count(), Count(), Count(), Count()
            pe.wait_ge(x_done, 5 * B)
            pe.wait_ge(router_in, 64)
            for b in range(B):
                pe.wait_ge(turn.free, T_PE.now() + 2)
                bank = start_job(pe, em, m)
                for kt in range(KT):
                    last = nc.tensor.matmul(bank[0:E, :], RW[:, kt, :], XT[:, b % 2, kt, :], start=kt == 0, stop=kt == KT - 1)
                last.then_inc(em.full, 1)
                pe.wait_ge(em.free, m.now() + 2)
                bank = start_job(pe, er, r)
                for st in range(ST):
                    last = nc.tensor.transpose(bank[:, st * E:(st + 1) * E], LT[0:E, st * P:(st + 1) * P], ID[0:E, 0:E])
                last.then_inc(er.full, 1)
                if b < B - 1:
                    norm_tensor(pe)
            pe.wait_ge(ones_ready, 2)
            for w in (TRI, ONE):
                nc.tensor.matmul(start_job(pe, er, r)[:, 0:n128], w, OHS.rearrange("p t e -> p (t e)"), start=True, stop=True)\
                  .then_inc(er.full, 1)
            pe.wait_ge(turn.free, T_PE.now() + 2)
            pe.wait_ge(routed, 1)
            pe.wait_ge(ew_in, E * 16)
            pe.wait_ge(e_zero, 1)
            return m, r, s, t

        def moe_tensor_tiles(pe, m, r, s, t):
            def turn_tile(u, i):
                pe.wait_ge(xg_in[u], i * 16 + 16)
                bank = start_job(pe, et, t)
                for kt in range(KT):
                    last = nc.tensor.transpose(bank[:, kt * P:(kt + 1) * P], XG[:, u, kt * P:(kt + 1) * P], ID[:, :])
                last.then_inc(et.full, 1)

            turn_tile(0, 0)
            with loop(pe, NT // 2, (m, 2), (r, 4), (s, 2), (t, 2)) as i:
                for u in range(2):
                    e = pe.value_load(EXPERT[0:1, ds(i * 2 + u, 1)], min_val=0, max_val=E - 1)
                    hold(pe, et.free, t.now() + 2)
                    up_done = None
                    for job, n, c in ((em, m, 0), (er, r, I)):
                        bank = start_job(pe, job, n)
                        for kt in range(KT):
                            last = nc.tensor.matmul(bank[:, 0:I].rearrange("p (a n) -> p a n", a=1), XGT[:, u, kt * P:(kt + 1) * P],
                                                    EW1[:, ds(e * KT + kt, 1), c:c + I], start=kt == 0, stop=kt == KT - 1)
                        last.then_inc(job.full, 1)
                    up_done = r.now() + 2
                    turn_tile(1 - u, i + u)
                    hold(pe, es.free, s.now() + 2)
                    pe.wait_ge(ew2_in[1 - u], (i + 1) * 16)
                    bank = start_job(pe, er, r)
                    for k in range(EK):
                        rows = min(P, I - k * P)
                        last = nc.tensor.matmul(bank, EHT[0:rows, 1 - u, k * P:(k + 1) * P], EW2[0:rows, 1 - u, k * D:(k + 1) * D],
                                                start=k == 0, stop=k == EK - 1)
                    last.then_inc(er.full, 1)
                    hold(pe, er.free, up_done)
                    bank = start_job(pe, es, s)
                    for k in range(EK):
                        rows = min(P, I - k * P)
                        last = nc.tensor.transpose(bank[0:rows, k * P:(k + 1) * P], EHID[:, u, k * P:k * P + rows], ID[:, :])
                    last.then_inc(es.full, 1)
            pe.wait_ge(et.free, t.now() + 2)
            norm_tensor(pe)

        def moe_scalar(act):
            m, s, t = Count(), Count(), Count()
            for q in (em, es, et):
                act.sem_inc(q.free, 2)
            for b in range(B):
                nc.scalar.copy(LT[0:E, :], full(act, em, m)[0:E, :]).then_inc(em.free, 1)
                if b < B - 1:
                    norm_scalar(act, (b + 1) & 1)
            act.wait_ge(pair_exp_in, 1)
            nc.scalar.activation(EX, EX, ACT.Exp).then_inc(pair_exp, 1)

            def rows(u):
                nc.scalar.copy(XGT[:, u, :], full(act, et, t)).then_inc(et.free, 1)
            rows(0)
            with loop(act, NT // 2, (m, 2), (s, 2), (t, 2)) as i:
                for u in range(2):
                    nc.scalar.activation(ESILU[:, u, :], full(act, em, m)[:, 0:I], ACT.Silu).then_inc(em.free, 1)
                    rows(1 - u)
                    bank = full(act, es, s)
                    nc.scalar.copy(EHT[:, u, 0:2 * P], bank[:, 0:2 * P])
                    nc.scalar.copy(EHT[0:I - 2 * P, u, 2 * P:], bank[0:I - 2 * P, 2 * P:EK * P]).then_inc(es.free, 1)
            norm_scalar(act, 0)

        def moe_vector(v):
            r, m = Count(), Count()
            one = lambda t, n: t.rearrange("p (t o) -> p t o", o=1).to_broadcast([P, B * ST, n])
            per_e = lambda t, n=B * ST: t.rearrange("p (o e) -> p o e", o=1).to_broadcast([P, n, E])
            tt = nc.vector.tensor_tensor
            v.sem_inc(er.free, 2)
            for u in range(2):
                v.sem_inc(y_stored[u], 16)
            v.wait_ge(router_in, 64)
            nc.vector.memset(ONE, 1.0).then_inc(ones_ready, 1)
            for b in range(B):
                bank = full(v, er, r)
                nc.vector.tensor_copy(LG[:, b * ST:(b + 1) * ST, :], bank[:, 0:ST * E].rearrange("p (s e) -> p s e", e=E)).then_inc(er.free, 1)
                if b < B - 1:
                    v.wait_ge(xnd_in, 16 * (b + 1))
                    norm_vector(v, b + 1)
                    T_V.step(KT)
            v.wait_ge(er.free, r.now() + 2)
            for mx, lg, oh in ((MX0, LG, OH0), (MX1, LG2, OH1)):
                if oh is OH1:
                    link(v, nc.vector.tensor_scalar(LG2, OH0, -1.0e30, None, ALU.mult))
                    link(v, tt(LG2, LG2, LG, ALU.add))
                link(v, nc.vector.tensor_reduce(mx, lg, op=ALU.max, axis=AX.X))
                link(v, tt(EQ, lg, one(mx, E), ALU.is_ge))
                link(v, tt(EQ, EQ, per_e(EC[:, 0:E]), ALU.mult))
                link(v, nc.vector.tensor_reduce(MS, EQ, op=ALU.max, axis=AX.X))
                link(v, tt(oh, EQ, one(MS, E), ALU.is_equal))
            tt(OHS, OH0, OH1, ALU.add).then_inc(ones_ready, 1)
            tt(EX, MX1, MX0, ALU.subtract).then_inc(pair_exp_in, 1)
            v.wait_ge(pair_exp, 1)
            link(v, nc.vector.tensor_scalar(WT0, EX, 1.0, None, ALU.add))
            link(v, nc.vector.reciprocal(WT0, WT0))
            link(v, nc.vector.tensor_scalar(WT0, WT0, G[:, 6:7], None, ALU.mult))
            link(v, tt(WT1, EX, WT0, ALU.mult))
            nc.vector.tensor_copy(RANK, full(v, er, r)[:, 0:n128].rearrange("p (t e) -> p t e", e=E)).then_inc(er.free, 1)
            bank = full(v, er, r)[:, 0:n128].rearrange("p (t e) -> p t e", e=E)
            nc.vector.tensor_copy(TOTAL, bank)
            nc.vector.tensor_copy(SCAN0, bank).then_inc(er.free, 1)
            v.wait_ge(er.free, r.now() + 2)

            def scan(of, to, n, cut):
                w = 1
                while w < n:
                    nc.vector.tensor_copy(cut(to, 0, w), cut(of, 0, w)).then_inc(vec, 1)
                    V.step()
                    link(v, tt(cut(to, w, n), cut(of, w, n), cut(of, 0, n - w), ALU.add))
                    of, to, w = to, of, 2 * w
                return of
            incl = scan(SCAN0, SCAN1, B * ST, lambda t, i, j: t[:, i:j, :])
            link(v, tt(TOTAL, incl, TOTAL, ALU.subtract))
            link(v, tt(RANK, RANK, TOTAL, ALU.add))
            count = incl[:, B * ST - 1, :]
            c3 = CMP.rearrange("p a b -> p (a b)")[:, 0:E * 16].rearrange("p (e t) -> p e t", e=E)
            link(v, tt(c3, count.rearrange("p (e o) -> p e o", o=1).to_broadcast([P, E, 16]),
                       EC[:, E:E + 16].rearrange("p (o t) -> p o t", o=1).to_broadcast([P, E, 16]), ALU.is_gt))
            link(v, nc.vector.tensor_reduce(NTL, c3, op=ALU.add, axis=AX.X))
            link(v, nc.vector.tensor_copy(END0, NTL))
            end = scan(END0, END1, E, lambda t, i, j: t[:, i:j])
            link(v, tt(START, end, NTL, ALU.subtract))
            link(v, nc.vector.tensor_scalar(START, START, float(P), None, ALU.mult))
            link(v, tt(RANK, RANK, per_e(START), ALU.add))
            for oh, pos, idx, yp in ((OH0, POS0, IDX0, YP0), (OH1, POS1, IDX1, YP1)):
                link(v, tt(EQ, oh, RANK, ALU.mult))
                link(v, nc.vector.tensor_reduce(pos, EQ, op=ALU.add, axis=AX.X))
                link(v, nc.vector.tensor_scalar(yp, pos, float(P), None, ALU.add))
                link(v, nc.vector.tensor_copy(idx, pos))
                link(v, nc.vector.tensor_scalar(idx, idx, 7, None, ALU.arith_shift_right))
                link(v, nc.vector.tensor_copy(MS, idx))
                link(v, nc.vector.tensor_scalar(MS, MS, float(1 - P * TW), None, ALU.mult))
                link(v, nc.vector.scalar_tensor_tensor(out=MS, in0=pos, scalar=float(TW), in1=MS, op0=ALU.mult, op1=ALU.add))
                link(v, nc.vector.tensor_copy(idx, MS))
            link(v, tt(CMP, EC[:, E + 16:].rearrange("p (t o) -> p t o", o=1).to_broadcast([P, TW, E]), per_e(end, TW), ALU.is_ge))
            link(v, nc.vector.tensor_reduce(EXF, CMP, op=ALU.add, axis=AX.X))
            nc.vector.tensor_scalar(EXPERT, EXF, float(E - 1), None, ALU.min).then_inc(routed, 1)

            m.step(B)
            with loop(v, NT // 2, (m, 2), (r, 4)) as i:
                for u in range(2):
                    bank = full(v, er, r)
                    v.wait_ge(em.free, m.step() + 2)
                    tt(EHID[:, u, :], ESILU[:, u, :], bank[:, 0:I], ALU.mult).then_inc(er.free, 1)
                    v.wait_ge(y_stored[u], i * 16 + 16)
                    nc.vector.tensor_copy(YE[:, u, :], full(v, er, r)).then_inc(y_ready, 1)
                    v.wait_ge(y_ready, i * 2 + u + 1)
                    v.sem_inc(er.free, 1)
            for k in range(2 * B * ST):
                tile, j = divmod(k, 2)
                v.wait_ge(yg_in[k % 4], 16 * (k // 4) + 16)
                nc.vector.scalar_tensor_tensor(out=X[:, tile, :], in0=YG[k % 4], scalar=(WT0, WT1)[j][:, tile:tile + 1],
                                               in1=X[:, tile, :], op0=ALU.mult, op1=ALU.add).then_inc(yg_used, 1)
                v.wait_ge(yg_used, k + 1)
            v.sem_inc(x_done, B)
            norm_vector(v, 0)
            T_V.step(KT)

        def moe_pool(pool):
            t = Count()
            nc.gpsimd.memset(EHT, 0.0).then_inc(e_zero, 1)
            for b in range(B - 1):
                norm_pool(pool)
            pool.wait_ge(routed, 1)
            pool.wait_ge(table_zero, 16)
            for tile in range(B * ST):
                for idx in (IDX0, IDX1):
                    nc.gpsimd.indirect_dma_start(out=table, out_offset=bass.IndirectOffsetOnAxis(ap=idx[:, tile:tile + 1], axis=0),
                                                 in_=TOK[:, tile:tile + 1], in_offset=None).then_inc(table_in, 16)
            pool.wait_ge(slots_in, 16)
            pool.wait_ge(xnd_in, B * 16)

            def gather(u, i, n):
                nc.gpsimd.tensor_copy(IX[u], SLOTS[:, ds(i, 1)]).then_inc(ix_ready, 1)
                hold(pool, ix_ready, n)
                nc.gpsimd.indirect_dma_start(out=XG[:, u, :], out_offset=None, in_=xnd,
                                             in_offset=bass.IndirectOffsetOnAxis(ap=IX[u], axis=0)).then_inc(xg_in[u], 16)
            gather(0, 0, 1)
            gather(1, 1, 2)
            with pool.Fori(0, NT // 2) as i:
                for u in range(2):
                    pool.wait_ge(et.full, i * 2 + u + 1)
                    gather(u, i * 2 + u + 2, i * 2 + u + 3)
            for u in range(2):
                pool.wait_ge(y_stored[u], (NT // 2 + 1) * 16)
                pool.wait_ge(xg_in[u], (NT // 2 + 1) * 16)
            pool.wait_ge(er.full, ROUTE_R + 2 * NT)
            pool.wait_ge(et.free, NT + 3)
            for k in range(2 * B * ST):
                tile, j = divmod(k, 2)
                if k >= 4:
                    pool.wait_ge(yg_used, k - 3)
                nc.gpsimd.indirect_dma_start(out=YG[k % 4], out_offset=None, in_=made,
                                             in_offset=bass.IndirectOffsetOnAxis(ap=(YP0, YP1)[j][:, tile:tile + 1], axis=0))\
                  .then_inc(yg_in[k % 4], 16)
            norm_pool(pool)

        lm, lr3, ls3 = rings("l3")
        mh = nc.dram_tensor("mh", [LH, P, 3 * C], F32, kind="Internal").ap()
        WSN = KT * P + LQ + 3 * C
        FTN = C + D + LQ + C
        a = area()
        W3 = a(LH, D)
        ROPE = a(6, S)
        KVN, KVT = a(B * ST, C), a(B * S)
        KVC = a(ST, C)
        WS = a(2, WSN)
        QHK, QP, CC = a(S), a(S), a(S)
        QB, RQ = a(4, S), a(3, S)
        FT, MST = a(2, FTN), a(2, 3 * C)
        ROPEK = a(2 * ST, C)
        SUM3, RS3, NEG3 = a(2 * ST), a(2 * ST), a(2 * ST)
        KV_TMP = QB.rearrange("p a n -> p (a n)").rearrange("p (t c) -> p t c", c=C)
        PROB3, PROBT3 = a(ST, S), a(ST, S)
        l3_in, kv_ready, kvc_ready = sem("l3_in"), sem("kv_ready"), sem("kvc_ready")
        ft_in, ws_in, m_stored = [[sem(f"{n}{u}") for u in range(2)] for n in ("ft_in", "ws_in", "m_stored")]
        max3_done, rope_ab, rope_c, rope_steps = sem("max3_done"), sem("rope_ab"), sem("rope_c"), sem("rope_steps")
        FOLD_M = 2 * LH + ST
        HEAD_M = 6
        PRO_M = 5

        def l3_sync(sp):
            sp.wait_ge(x_done, 6 * B)
            for u in range(2):
                sp.wait_ge(ew2_in[u], (NT // 2 + 1) * 16)

            def fold(u, h):
                sp.dma_start(FT[:, u, :].rearrange("p (a n) -> p a n", a=1), l3_fold[ds(h, 1)].rearrange("a p n -> p a n")).then_inc(ft_in[u], 16)

            def weights(u, h):
                ws = WS[:, u, :].rearrange("p (a n) -> p a n", a=1)
                sp.dma_start(ws[:, :, 0:KT * P + LQ], l3_wq[ds(h, 1)].rearrange("a p n -> p a n")).then_inc(ws_in[u], 16)
                sp.dma_start(ws[:, :, KT * P + LQ:], mh[ds(h, 1)].rearrange("a p n -> p a n")).then_inc(ws_in[u], 16)
            for u in range(2):
                fold(u, u)
            for dst, src in ((KVN, ctx_n.rearrange("(n p) d -> p n d", p=P)), (ROPEK, rope_k), (ROPE, rope_q)):
                sp.dma_start(dst, src).then_inc(l3_in, 16)
            with sp.Fori(0, LH // 2) as i:
                for u in range(2):
                    hold(sp, lm.full, i * 4 + 2 * u + 2)
                    fold(u, (i * 2 + u + 2) & (LH - 1))
                    hold(sp, lm.free, i * 4 + 2 * u + 4)
                    sp.dma_start(mh[ds(i * 2 + u, 1)].rearrange("a p n -> p a n"), MST[:, u, :].rearrange("p (a n) -> p a n", a=1))\
                      .then_inc(m_stored[u], 16)
            for u in range(2):
                sp.wait_ge(m_stored[u], (LH // 2 + 1) * 16)
            for u in range(2):
                weights(u, u)
            with sp.Fori(0, B * LH // 2) as i:
                for u in range(2):
                    hold(sp, lm.full, i * 2 * HEAD_M + (2 + u) * HEAD_M + FOLD_M - 1)
                    weights(u, (i * 2 + u + 2) & (LH - 1))

        def l3_tensor(pe):
            m, r, s, w = Count(), Count(), Count(), Count()
            pe.wait_ge(x_done, 6 * B)
            one = lambda t: t.rearrange("p (a n) -> p a n", a=1)
            with loop(pe, LH // 2, (m, 4)) as i:
                for u in range(2):
                    pe.wait_ge(ft_in[u], i * 16 + 16)
                    bank = start_job(pe, lm, m)
                    nc.tensor.matmul(bank, FT[:, u, 0:C], FT[:, u, C:C + D], start=True, stop=True).then_inc(lm.full, 1)
                    bank = start_job(pe, lm, m)
                    for k in range(3):
                        last = nc.tensor.matmul(bank[:, k * C:(k + 1) * C], FT[:, u, C + D + k * P:C + D + (k + 1) * P],
                                                FT[:, u, C + D + LQ:], start=True, stop=True)
                    last.then_inc(lm.full, 1)
            pe.wait_ge(kv_ready, 1)
            for t in range(ST):
                bank = start_job(pe, lm, m)
                for k in range(ST):
                    last = nc.tensor.transpose(bank[:, k * P:(k + 1) * P], KVN[:, t * ST + k, :], ID[:, :])
                last.then_inc(lm.full, 1)

            def head_queries(u, half, n):
                pe.wait_ge(ws_in[u], n)
                bank = start_job(pe, lm, m)
                for kt in range(KT):
                    last = nc.tensor.matmul(one(bank), WS[:, u, kt * P:(kt + 1) * P], XT[:, ds(half, 1), kt, :],
                                            start=kt == 0, stop=kt == KT - 1)
                last.then_inc(lm.full, 1)

            def big_queries(u):
                hold(pe, lm.free, m.now() + 2)
                for k in range(3):
                    nc.tensor.matmul(start_job(pe, lm, m), WS[:, u, (KT + k) * P:(KT + k + 1) * P], QHK, start=True, stop=True)\
                      .then_inc(lm.full, 1)

            def score_queries(u):
                hold(pe, rope_ab, w.now() + 1)
                hold(pe, rope_c, w.step())
                bank = start_job(pe, lm, m)
                for k in range(3):
                    last = nc.tensor.matmul(bank, WS[:, u, KT * P + LQ + k * C:KT * P + LQ + (k + 1) * C], RQ[:, k, :],
                                            start=k == 0, stop=k == 2)
                last.then_inc(lm.full, 1)

            head_queries(0, 0, 32)
            big_queries(0)
            score_queries(0)
            with loop(pe, B, (m, HEAD_M * LH), (r, ST * LH), (s, ST * LH), (w, LH), (T_PE, KT + ST * LH), (N_PE, 1)) as b:
                norm_tensor(pe)
                with loop(pe, LH // 2, (m, 2 * HEAD_M), (r, 2 * ST), (s, 2 * ST), (w, 2), (T_PE, 2 * ST)) as hp:
                    for u in range(2):
                        hold(pe, lm.free, m.now() + 2)
                        for st in range(ST):
                            nc.tensor.matmul(start_job(pe, ls3, s), QP[:, st * P:(st + 1) * P], KVT[:, ds(b * S, S)], start=True, stop=True)\
                              .then_inc(ls3.full, 1)
                        if u == 0:
                            head_queries(1, b & 1, b * (16 * LH) + hp * 32 + 32)
                        else:
                            hold(pe, turn.free, T_PE.now() + 1)
                            head_queries(0, ((b * 8 + hp + 1) >> 3) & 1, b * (16 * LH) + hp * 32 + 64)
                        hold(pe, ls3.free, s.now() + 2)

                        def turn_probs(lts):
                            for lt in lts:
                                bank = start_job(pe, turn, T_PE)
                                for st in range(ST):
                                    last = nc.tensor.transpose(bank[:, st * P:(st + 1) * P], PROB3[:, st, lt * P:(lt + 1) * P], ID[:, :])
                                last.then_inc(turn.full, 1)
                        turn_probs((0, 1))
                        big_queries(1 - u)
                        turn_probs((2, 3))
                        hold(pe, turn.free, T_PE.now() + 2)
                        if u == 0:
                            hold(pe, kvc_ready, b + 1)
                        bank = start_job(pe, lm, m)
                        for lt in range(ST):
                            last = nc.tensor.matmul(bank, KVC[:, lt, :], PROBT3[:, lt, :], start=lt == 0, stop=lt == ST - 1)
                        last.then_inc(lm.full, 1)
                        score_queries(1 - u)
                        hold(pe, lm.free, m.now() + 1)
                        for st in range(ST):
                            nc.tensor.matmul(one(start_job(pe, lr3, r)), CC[:, st * P:(st + 1) * P], W3[:, ds(hp * 2 + u, 1), :],
                                             start=True, stop=True).then_inc(lr3.full, 1)
            pe.wait_ge(lm.free, m.now() + 2)

        def l3_scalar(act):
            m, s, w = Count(), Count(), Count()
            act.sem_inc(lm.free, 2)
            act.sem_inc(ls3.free, 2)
            for u in range(2):
                act.sem_inc(m_stored[u], 16)
            with loop(act, LH // 2, (m, 4)) as i:
                for u in range(2):
                    nc.scalar.copy(W3[:, ds(i * 2 + u, 1), :], full(act, lm, m).rearrange("p (a n) -> p a n", a=1)).then_inc(lm.free, 1)
                    act.wait_ge(m_stored[u], i * 16 + 16)
                    nc.scalar.copy(MST[:, u, :], full(act, lm, m)[:, 0:3 * C]).then_inc(lm.free, 1)
            for t in range(ST):
                nc.scalar.copy(KVT[:, t * S:(t + 1) * S], full(act, lm, m)).then_inc(lm.free, 1)

            def big_queries(first=False):
                for k in range(3):
                    if k == 0 and not first:
                        act.wait_ge(rope_ab, w.now())
                    if k == 2 and not first:
                        act.wait_ge(rope_c, w.now())
                    bank = full(act, lm, m)
                    last = nc.scalar.copy(QB[:, k, :], bank)
                    if k == 2:
                        nc.scalar.copy(QB[64:128, 3, :], bank[0:64, :])
                        last = nc.scalar.copy(QB[0:64, 3, :], bank[64:128, :])
                    last.then_inc(lm.free, 1)
                w.step()
            nc.scalar.copy(QHK, full(act, lm, m)).then_inc(lm.free, 1)
            big_queries(True)
            nc.scalar.copy(QP, full(act, lm, m)).then_inc(lm.free, 1)
            with loop(act, B, (m, HEAD_M * LH), (s, ST * LH), (w, LH), (T_ACT, KT + ST * LH)) as b:
                norm_scalar(act, (b + 1) & 1)
                with loop(act, LH // 2, (m, 2 * HEAD_M), (s, 2 * ST), (w, 2), (T_ACT, 2 * ST)) as hp:
                    for u in range(2):
                        for st in range(ST):
                            act.wait_ge(max3_done, s.now() + 1)
                            bank = full(act, ls3, s)
                            nc.scalar.activation(PROB3[:, st, :], bank, ACT.Exp, bias=NEG3[:, u * ST + st:u * ST + st + 1],
                                                 accum_out=SUM3[:, u * ST + st:u * ST + st + 1]).then_inc(ls3.free, 1)
                        nc.scalar.copy(QHK, full(act, lm, m)).then_inc(lm.free, 1)
                        for lt in (0, 1):
                            nc.scalar.copy(PROBT3[:, lt, :], full(act, turn, T_ACT)).then_inc(turn.free, 1)
                        big_queries()
                        for lt in (2, 3):
                            nc.scalar.copy(PROBT3[:, lt, :], full(act, turn, T_ACT)).then_inc(turn.free, 1)
                        nc.scalar.copy(CC, full(act, lm, m)).then_inc(lm.free, 1)
                        nc.scalar.copy(QP, full(act, lm, m)).then_inc(lm.free, 1)

        def l3_vector(v):
            m, r, s, w = Count(), Count(), Count(), Count()
            tt = nc.vector.tensor_tensor
            v.sem_inc(lr3.free, 2)
            v.wait_ge(l3_in, 48)
            kv = lambda t, i, j: t[:, :, i:j].rearrange("p (b s) c -> p b s c", b=B)
            tab = lambda k, i, j: ROPEK[:, k * ST:(k + 1) * ST, i:j].rearrange("p (o s) c -> p o s c", o=1).to_broadcast([P, B, ST, j - i])
            tt(kv(KV_TMP, 0, 64), kv(KVN, 64, 128), tab(1, 0, 64), ALU.mult)
            link(v, tt(kv(KV_TMP, 64, 128), kv(KVN, 0, 64), tab(1, 64, 128), ALU.mult))
            link(v, tt(kv(KVN, 0, 128), kv(KVN, 0, 128), tab(0, 0, 128), ALU.mult))
            tt(KVN, KVN, KV_TMP, ALU.add).then_inc(kv_ready, 1)
            m.step(FOLD_M)

            def rotate():
                v.wait_ge(lm.free, m.now() + 5)
                tt(RQ[:, 0, :], QB[:, 0, :], ROPE[:, 0, :], ALU.mult)
                tt(RQ[:, 1, :], QB[:, 1, :], ROPE[:, 2, :], ALU.mult)
                tt(QB[:, 1, :], QB[:, 1, :], ROPE[:, 1, :], ALU.mult)
                link(v, tt(QB[:, 0, :], QB[:, 0, :], ROPE[:, 3, :], ALU.mult))
                tt(RQ[:, 0, :], RQ[:, 0, :], QB[:, 1, :], ALU.subtract)
                tt(RQ[:, 1, :], RQ[:, 1, :], QB[:, 0, :], ALU.add).then_inc(rope_ab, 1)
            rotate()
            m.step(PRO_M)
            with loop(v, B, (m, HEAD_M * LH), (r, ST * LH), (s, ST * LH), (V, 3 * LH), (T_V, KT + ST * LH), (N_V, 1)) as b:
                norm_vector(v, (b + 1) & 3)
                T_V.step(KT)
                with loop(v, LH // 2, (m, 2 * HEAD_M), (r, 2 * ST), (s, 2 * ST), (V, 6), (T_V, 2 * ST)) as hp:
                    for u in range(2):
                        for st in range(ST):
                            nc.vector.tensor_reduce(NEG3[:, u * ST + st:u * ST + st + 1], full(v, ls3, s), op=ALU.max, axis=AX.X,
                                                    negate=True).then_inc(max3_done, 1)
                        hold(v, ls3.free, s.now() + 2)
                        link(v, nc.vector.reciprocal(RS3[:, u * ST:(u + 1) * ST], SUM3[:, u * ST:(u + 1) * ST]))
                        link(v, nc.vector.tensor_scalar(RS3[:, u * ST:(u + 1) * ST], RS3[:, u * ST:(u + 1) * ST], G[:, 3:4], None, ALU.mult))
                        rotate()
                        m.step(HEAD_M)
                        for st in range(ST):
                            bank = full(v, lr3, r)
                            xb = X[:, ds(b * ST + st, 1), :].rearrange("p a n -> p (a n)")
                            nc.vector.scalar_tensor_tensor(out=xb, in0=bank, scalar=RS3[:, u * ST + st:u * ST + st + 1], in1=xb,
                                                           op0=ALU.mult, op1=ALU.add).then_inc(lr3.free, 1)
                        T_V.step(ST)
                v.wait_ge(lr3.free, r.now() + 2)
                v.sem_inc(x_done, 1)

        def l3_pool(pool):
            m, w = Count(), Count()
            tt = nc.gpsimd.tensor_tensor
            m.step(FOLD_M)

            def rotate():
                pool.wait_ge(lm.free, m.now() + 6)
                tt(RQ[:, 2, :], QB[:, 2, :], ROPE[:, 4, :], ALU.mult)
                tt(QB[:, 3, :], QB[:, 3, :], ROPE[:, 5, :], ALU.mult).then_inc(rope_steps, 1)
                pool.wait_ge(rope_steps, w.step())
                tt(RQ[:, 2, :], RQ[:, 2, :], QB[:, 3, :], ALU.add).then_inc(rope_c, 1)
            pool.wait_ge(l3_in, 48)
            rotate()
            m.step(PRO_M)
            with loop(pool, B, (m, HEAD_M * LH), (w, LH), (N_P, 1)) as b:
                hold(pool, lm.full, m.now())
                nc.gpsimd.tensor_copy(KVC, KVN[:, ds(b * ST, ST), :]).then_inc(kvc_ready, 1)
                norm_pool(pool)
                with loop(pool, LH // 2, (m, 2 * HEAD_M), (w, 2)) as hp:
                    for u in range(2):
                        rotate()
                        m.step(HEAD_M)

        l3f = Ffn("l3f", 7, l3_w13, l3_w2, UG, HID // P // UG, 1, lambda b, g, st: G[:, 7:8])

        def l3f_begin(sp):
            sp.wait_ge(x_done, 7 * B)
            for u in range(2):
                sp.wait_ge(ws_in[u], (B * LH + 2) * 16)

        block = ctx.enter_context(nc.Block())
        stored = sem("stored")
        zero_ready = sem("zero_ready")

        @block.sync
        def _(sp):
            sp.wait_ge(zero_ready, 1)
            sp.dma_start(table.rearrange("(p n) o -> p (n o)", p=P), ZERO[:, :]).then_inc(table_zero, 16)
            sp.dma_start(X[:, :, :], x.rearrange("(n p) d -> p n d", p=P)).then_inc(loaded, 16)
            sp.dma_start(CT, ctx_t).then_inc(loaded, 16)
            sp.dma_start(ID[:, :], ident).then_inc(loaded, 16)
            sp.dma_start(G[:, :], gates.rearrange("(a n) -> a n", a=1).to_broadcast([P, 8])).then_inc(loaded, 16)
            sp.dma_start(GC[:, 0:1], gamma_raw.rearrange("(a n) -> a n", a=1).to_broadcast([P, 1])).then_inc(loaded, 16)
            sp.dma_start(WQ0, l0_wq).then_inc(l0_w, 16)
            sp.dma_start(WK0, l0_wk).then_inc(l0_w, 16)
            sp.dma_start(HAD, hadamard).then_inc(l0_had, 16)
            sp.dma_start(WH[0], l0_w2).then_inc(l0_had, 16)
            sp.wait_ge(l0f.m.free, 2 + ST + HAD_M + 2)
            sp.dma_start(w2h.rearrange("g p n -> p g n"), WH[1].rearrange("p (g u) n -> p g (u n)", u=UG)).then_inc(wh_stored, 16)
            ffn_sync(sp, l0f, lambda sp: sp.wait_ge(wh_stored, 16))
            l1_sync(sp)
            l1f_sync_weights(sp)
            l1f_sync(sp)
            l2_sync(sp)
            moe_sync(sp)
            l3_sync(sp)
            ffn_sync(sp, l3f, l3f_begin)
            sp.wait_ge(x_done, 8 * B)
            sp.dma_start(out.rearrange("(n p) d -> p n d", p=P), X[:, :, :]).then_inc(stored, 16)
            sp.wait_ge(stored, 16)

        @block.tensor
        def _(pe):
            pe.wait_ge(loaded, 80)
            l0_tensor(pe)
            l1_tensor(pe)
            l1f_tensor(pe)
            l2_tensor(pe)
            moe_tensor_tiles(pe, *moe_tensor(pe))
            l3_tensor(pe)
            ffn_tensor(pe, l3f)

        @block.scalar
        def _(act):
            act.sem_inc(turn.free, 2)
            act.wait_ge(loaded, 80)
            nc.scalar.activation(G[:, :], G[:, :], ACT.Tanh).then_inc(g_ready, 1)
            nc.scalar.activation(GC[:, 0:1], GC[:, 0:1], ACT.Sigmoid).then_inc(g_ready, 1)
            l0_scalar(act)
            l1_scalar(act)
            l1f_scalar(act)
            l2_scalar(act)
            moe_scalar(act)
            l3_scalar(act)
            ffn_scalar(act, l3f)

        @block.vector
        def _(v):
            v.wait_ge(loaded, 80)
            norm_vector(v, 0)
            v.wait_ge(g_ready, 2)
            link(v, nc.vector.tensor_scalar(GC[:, 1:2], GC[:, 0:1], -1.0, 1.0, ALU.mult, ALU.add))
            link(v, nc.vector.tensor_scalar(GC[:, 1:2], GC[:, 1:2], G[:, 0:1], None, ALU.mult))
            nc.vector.tensor_scalar(GC[:, 2:3], GC[:, 0:1], G[:, 0:1], 0.5, ALU.mult, ALU.mult).then_inc(gc_ready, 1)
            l0_vector(v)
            l1_vector(v)
            l1f_vector(v)
            l2_vector(v)
            moe_vector(v)
            l3_vector(v)
            ffn_vector(v, l3f)

        @block.gpsimd
        def _(pool):
            nc.gpsimd.memset(ZERO[:, :], 0).then_inc(zero_ready, 1)
            nc.gpsimd.memset(HALF[:, :], -0.5).then_inc(consts, 1)
            pool.wait_ge(consts, 1)
            norm_pool(pool)
            had_pool(pool)
            with loop(pool, 2 * B, (N_P, 1)):
                norm_pool(pool)
            l1_pool(pool)
            l1f_pool(pool)
            l2_pool(pool)
            pool.wait_ge(x_done, 5 * B)
            moe_pool(pool)
            l3_pool(pool)
            with loop(pool, B, (N_P, 1)):
                norm_pool(pool)


def layouts(inp):
    import numpy as np

    f = {k: np.asarray(v) for k, v in inp.items()}
    c = np.ascontiguousarray

    def up_tiles(wg, wu):
        n = wg.shape[0] // P
        w = np.stack([wg, wu]).reshape(2, n, P, KT, P)
        return c(w.transpose(1, 4, 3, 0, 2)).reshape(n, P, KT * 2 * P)

    def cut(w):
        return c(w.reshape(-1, P, w.shape[-1]).transpose(1, 0, 2))

    o = {}
    o["x"] = f["x"].reshape(B * S, D)
    ctx = f["ctx_512"].reshape(B * S, C)
    o["ctx_n"], o["ctx_t"] = ctx, c(ctx.T)
    o["gates"] = np.concatenate([f["g_xattn"], f["g_ffn"]])
    o["gamma_raw"] = f["L0_xattn_gamma_raw"].reshape(1)
    o["ident"] = np.eye(P, dtype=np.float32)
    had = np.ones((1, 1), np.float32)
    while len(had) < P:
        had = np.block([[had, had], [had, -had]])
    o["hadamard"] = had.astype(np.float32)
    o["l0_w13"] = up_tiles(f["L0_ffn_W1"], f["L0_ffn_W3"])
    o["l0_w2"] = cut(f["L0_ffn_W2"].T)
    row = lambda *n: np.stack([f["L1_" + k] for k in n])
    col = lambda k: f["L1_ffn_" + k].reshape(-1, P).T
    o["l1_wk"], o["l1_bk"] = c(f["L1_xattn_W_k"].T), f["L1_xattn_b_k"].reshape(P, 1)
    o["l1_bk_row"] = f["L1_xattn_b_k"].reshape(1, C)
    o["l1_ln"] = row("xattn_ln_gamma", "xattn_ln_beta")
    o["l1_rows"] = row("ffn_out_gamma", "ffn_out_beta")
    o["l1_inrows"] = row("ffn_in_gamma", "ffn_in_beta")
    o["l1_cols"] = c(np.concatenate([col(k) for k in ("agg_b", "d1_b", "d2_b", "bc_b", "gate_b", "pn_gamma", "pn_beta")], 1))
    for k, n in (("l1_agg", "agg_w"), ("l1_d1", "d1_w"), ("l1_d2", "d2_w"), ("l1_bc", "bc_w"), ("l1_gate", "gate_w")):
        o[k] = cut(f["L1_ffn_" + n])
    o["l2_router"] = cut(f["L2_ffn_router_w"].T)
    o["l2_w12"] = c(f["L2_ffn_w1"].reshape(E, 2 * I, KT, P).transpose(3, 0, 2, 1)).reshape(P, E * KT, 2 * I)
    w2 = np.zeros((E, EK * P, D), np.float32)
    w2[:, :I] = f["L2_ffn_w2"].transpose(0, 2, 1)
    o["l2_w2"] = c(w2.reshape(E, EK, P, D).transpose(0, 2, 1, 3)).reshape(E, P, EK * D)
    o["moe_row"] = np.concatenate([8.0 - np.arange(E), 128.0 * np.arange(16), np.arange(TW)]).astype(np.float32)[None]
    o["moe_tri"] = np.triu(np.ones((P, P), np.float32), 1)
    o["moe_token"] = (np.arange(B * ST)[None, :] * P + np.arange(P)[:, None]).astype(np.int32)
    order = np.concatenate([np.arange(128), np.arange(192, 320), np.arange(128, 192), np.arange(320, 384)])
    wq = f["L3_xattn_Wq"].reshape(LH, LK, KT, P).transpose(0, 3, 2, 1).reshape(LH, P, KT * LK)
    o["l3_wq"] = np.concatenate([wq, f["L3_xattn_w_kc_q"][:, :, order]], 2)
    wo = f["L3_xattn_Wo"].reshape(D, LH, LK).transpose(1, 2, 0)
    qr_kr = np.zeros((LH, P, LQ + C), np.float32)
    qr_kr[:, :LR, :LQ] = f["L3_xattn_W_qr"][:, order, :].transpose(0, 2, 1)
    qr_kr[:, :LR, LQ:] = f["L3_xattn_W_kr"].transpose(0, 2, 1)
    o["l3_fold"] = np.concatenate([f["L3_xattn_w_kc_kv"], wo, qr_kr], 2)

    def rope(dim):
        inv = (np.float32(1) / np.float32(10000) ** (np.arange(0, dim, 2, dtype=np.float32) / np.float32(dim))).astype(np.float32)
        at = np.repeat(np.arange(S, dtype=np.float32)[:, None] * inv, 2, axis=1).astype(np.float64)
        return np.cos(at).astype(np.float32), np.sin(at).astype(np.float32)
    cos, sin = rope(LQ)
    cos, sin = cos.T[order].reshape(3, P, S).copy(), sin.T[order].reshape(3, P, S).copy()
    sin[2, :64] *= -1
    o["rope_q"] = c(np.stack([cos, sin], 1).reshape(6, P, S).transpose(1, 0, 2))
    cos, sin = rope(C)
    sin[:, :C // 2] *= -1
    o["rope_k"] = c(np.stack([cos, sin]).reshape(2 * ST, P, C).transpose(1, 0, 2))
    o["l3_w13"] = up_tiles(f["L3_ffn_w_gate"], f["L3_ffn_w_up"])
    o["l3_w2"] = c(f["L3_ffn_w_down"].T.reshape(HID // P // UG, UG, P, D).transpose(0, 2, 1, 3)).reshape(HID // P // UG, P, UG * D)
    o["l0_wq"], o["l0_wk"] = c(f["L0_xattn_Wq"].T), c(f["L0_xattn_Wk"].T)
    return o


LOADED = """x ctx_n ctx_t gates gamma_raw ident l0_wq l0_wk hadamard l0_w13 l0_w2 l1_wk l1_bk l1_bk_row l1_ln l1_rows l1_inrows l1_cols l1_agg l1_d1 l1_d2 l1_bc l1_gate l2_router l2_w12 l2_w2 moe_row moe_tri moe_token l3_wq l3_fold rope_q rope_k l3_w13 l3_w2""".split()


def kernel(**inputs):
    import numpy as np
    import concourse.bacc as bacc
    from concourse.bass_utils import run_bass_kernel_spmd

    nc = bacc.Bacc("TRN2", target_bir_lowering=False, num_devices=1)
    laid = layouts(inputs)
    arrays = {f"{name}_dram": np.ascontiguousarray(laid[name]) for name in LOADED}
    args = [nc.dram_tensor(f"{name}_dram", arrays[f"{name}_dram"].shape, mybir.dt.from_np(arrays[f"{name}_dram"].dtype),
                           kind="ExternalInput").ap() for name in LOADED]
    out = nc.dram_tensor("out_dram", (B * S, D), F32, kind="ExternalOutput").ap()
    flamingo(nc, *args, out)
    return run_bass_kernel_spmd(nc, [arrays], core_ids=[0]).results[0]["out_dram"].reshape(B, S, D)
```

```python
from contextlib import ExitStack, contextmanager

import concourse.bass as bass
from concourse import mybir

ds = bass.ds
F32 = mybir.dt.float32
F32R = mybir.dt.float32r
I32 = mybir.dt.int32
ALU = mybir.AluOpType
ACT = mybir.ActivationFunctionType
AX = mybir.AxisListType

P = 128
B, S, D = 4, 512, 512
ST = S // P
KT = D // P
C = 128
TOPK = 153
TOP_ROUNDS = (TOPK - 1) // 8 + 1
L0_HEADS, L0_HEAD = 4, 32
HID = 2048
E, I = 8, 352
PAIR_TILES = 2 * B * ST + E - 1
NT = PAIR_TILES + 1
TW = NT + 2
EK = 3
QH, HD = 32, 16
KVH = 8
LH, LK, LQ, LR = 16, 128, 384, 64
EPS_BLOCK, EPS_INNER = 1e-5, 1e-6
K_STEPS = 4
UG = 4
AREA = 33200
FFN_AREA = AREA - 4 * 1536 - 2 * S - 4 * S


class Count:

    def __init__(self):
        self.base, self.k, self.odd, self.turn = 0, 0, 0, 0

    def bank(self):
        assert self.turn % 2 == 0, self.turn
        return (self.odd + self.k) % 2

    def now(self):
        return self.base + self.k

    def step(self, n=1):
        self.k += n
        return self.base + self.k


@contextmanager
def loop(eng, times, *counts):
    begun = [(c.base, c.k, c.odd, c.turn) for c, _ in counts]
    with eng.Fori(0, times) as i:
        for (c, n), (base, k, odd, _) in zip(counts, begun):
            c.base, c.k, c.odd, c.turn = i * n + (base + k), 0, (odd + k) % 2, n
        yield i
        for c, n in counts:
            assert c.k == n, (c.k, n)
    for (c, n), (base, k, odd, turn) in zip(counts, begun):
        c.base, c.k, c.odd, c.turn = base, k + times * n, odd, turn


class Ring:

    def __init__(self, banks, full, free):
        self.banks, self.full, self.free, self.depth = banks, full, free, banks.shape[1]


def flamingo(nc, x, ctx_n, ctx_t, gates, gamma_raw, ident, l0_wq, l0_wk, hadamard, l0_w13, l0_w2, l1_wk, l1_bk, l1_bk_row,
             l1_ln, l1_rows, l1_inrows, l1_cols, l1_trows, l1_d1row, l1_agg, l1_d1, l1_d2, l1_bc, l1_gate, sum4, l2_router, l2_w12, l2_w2, moe_row, moe_tri, moe_token,
             l3_wq, l3_fold, rope_q, rope_k, l3_w13, l3_w2, out):
    ctx = ExitStack()
    with ctx:
        def sb(name, shape, dt=F32):
            return ctx.enter_context(nc.sbuf_tensor(name, shape, dt))

        def sem(name):
            return ctx.enter_context(nc.semaphore(name))

        X = sb("X", [P, B * ST, D])
        XN = sb("XN", [P, ST, D])
        XT = sb("XT", [P, 2, KT, S])
        ID = sb("ID", [P, P])
        STAT = sb("STAT", [P, ST, 6])
        MV = sb("MV", [P, ST, 2])
        VAR = sb("VAR", [P, ST])
        RSTD = sb("RSTD", [P, ST])
        HALF = sb("HALF", [P, ST])
        G = sb("G", [P, 8])
        GC = sb("GC", [P, 3])
        VAR1, RS1, NEGM1, SUM1 = [sb(n, [P, ST])[:, :] for n in ("VAR1", "RS1", "NEGM1", "SUM1")]
        AR = sb("AR", [P, AREA])

        def area(at=0):
            at = [at]

            def take(*shape):
                n = 1
                for s in shape:
                    n *= s
                v = AR[:, at[0]:at[0] + n]
                at[0] += n
                assert at[0] <= AREA, at[0]
                if len(shape) == 2:
                    v = v.rearrange("p (a b) -> p a b", b=shape[1])
                if len(shape) == 3:
                    v = v.rearrange("p (a b c) -> p a b c", b=shape[1], c=shape[2])
                return v
            take.here = lambda: at[0]
            return take

        BM = ctx.enter_context(nc.psum_tensor("BM", [P, 2, 512], F32))
        BR = ctx.enter_context(nc.psum_tensor("BR", [P, 2, 512], F32))
        BS = ctx.enter_context(nc.psum_tensor("BS", [P, 2, 512], F32))
        BT = ctx.enter_context(nc.psum_tensor("BT", [P, 2, 512], F32))

        def ring(banks, name):
            return Ring(banks, sem(name + "_full"), sem(name + "_free"))

        def rings(phase):
            return ring(BM, phase + "_m"), ring(BR, phase + "_r"), ring(BS, phase + "_s")

        turn = ring(BT, "turned")
        T_PE, T_ACT, T_V = Count(), Count(), Count()
        N_PE, N_V, N_P = Count(), Count(), Count()

        def start_job(pe, r, n, waited=False):
            if not waited:
                pe.wait_ge(r.free, n.now() + 1)
            bank = r.banks[:, n.bank() if r.depth == 2 else 0, :]
            n.step()
            return bank

        def full(eng, r, n):
            bank = r.banks[:, n.bank() if r.depth == 2 else 0, :]
            eng.wait_ge(r.full, n.step())
            return bank

        loaded = sem("loaded")
        x_rest = sem("x_rest")
        consts = sem("consts")
        passed = sem("passed")
        g_ready = sem("g_ready")
        gc_ready = sem("gc_ready")
        vec = sem("vec")
        V = Count()

        def hold(eng, s, value):
            eng.wait_ge(s, value)
            eng.sem_inc(passed, 1)

        def link(v, ins, alone=False):
            ins.then_inc(vec, 1)
            (hold if alone else lambda e, s, n: e.wait_ge(s, n))(v, vec, V.step())

        norm_stats, norm_aggr = sem("norm_stats"), sem("norm_aggr")
        norm_var, norm_rstd, xn_ready = sem("norm_var"), sem("norm_rstd"), sem("xn_ready")
        x_done = sem("x_done")

        def norm_vector(v, b):
            g = N_V.now()
            N_V.step()
            hold(v, turn.free, T_V.now() + 2)
            for st in range(ST):
                last = nc.vector.bn_stats(STAT[:, st, :], X[:, ds(4 * b + st, 1), :])
            last.then_inc(norm_stats, 1)
            hold(v, norm_stats, g + 1)
            for st in range(ST):
                last = nc.vector.bn_aggr(MV[:, st, :], STAT[:, st, :])
            last.then_inc(norm_aggr, 1)
            v.wait_ge(norm_aggr, g + 1)
            nc.vector.tensor_scalar(VAR[:, :], MV[:, :, 1], EPS_BLOCK, None, ALU.add).then_inc(norm_var, 1)
            v.wait_ge(norm_rstd, g + 1)
            for st in range(ST):
                last = nc.vector.tensor_scalar(XN[:, st, :], X[:, ds(4 * b + st, 1), :].rearrange("p a n -> p (a n)"),
                                               MV[:, st, 0:1], RSTD[:, st:st + 1], ALU.subtract, ALU.mult)
            last.then_inc(xn_ready, 1)

        def norm_pool(pool):
            pool.wait_ge(norm_var, N_P.step())
            nc.gpsimd.tensor_tensor(RSTD[:, :], VAR[:, :], HALF[:, :], ALU.pow).then_inc(norm_rstd, 1)

        def norm_tensor(pe):
            pe.wait_ge(xn_ready, N_PE.step())
            for kt in range(KT):
                bank = start_job(pe, turn, T_PE)
                for st in range(ST):
                    last = nc.tensor.transpose(bank[:, st * P:(st + 1) * P], XN[:, st, kt * P:(kt + 1) * P], ID[:, :])
                last.then_inc(turn.full, 1)

        def norm_scalar(act, half):
            for kt in range(KT):
                bank = full(act, turn, T_ACT)
                nc.scalar.copy(XT[:, ds(half, 1), kt, :], bank.rearrange("p (a n) -> p a n", a=1)).then_inc(turn.free, 1)

        a = area()
        WQ0, WK0 = a(C), a(C)
        QT0, KT0 = a(S), a(S)
        CT = a(B * S)
        SIM = a(ST, S)
        GRAPH = a(ST, S)
        WORK = a(S)
        TOP = a(8)
        HAD = a(P)
        WH = [a(HID // P, D), a(HID // P, D)]
        l0_w = sem("l0_w")
        graph_ready = sem("graph_ready")
        l0_had, butterflies = sem("l0_had"), sem("butterflies")
        wh_stored = sem("wh_stored")
        w2h = nc.dram_tensor("w2h", [HID // P // UG, P, UG * D], F32, kind="Internal").ap()

        def had_pool(pool):
            pool.wait_ge(l0_had, 32)
            n = 0
            for stage in range(4):
                w = 1 << stage
                of, to = WH[stage % 2], WH[1 - stage % 2]
                of = of.rearrange("p (g two w) d -> p g two (w d)", two=2, w=w)
                to = to.rearrange("p (g two w) d -> p g two (w d)", two=2, w=w)
                if stage:
                    pool.wait_ge(butterflies, n)
                for half, op in ((0, ALU.add), (1, ALU.subtract)):
                    nc.gpsimd.tensor_tensor(to[:, :, half, :], of[:, :, 0, :], of[:, :, 1, :], op).then_inc(butterflies, 1)
                    n += 1

        class Ffn:

            def __init__(self, name, phase, w13, w2, units, groups, per_turn, scale, after=(), before=0, between=0):
                self.before, self.between = before, between
                assert groups == 4
                self.phase, self.w13, self.w2, self.after = phase, w13, w2, after
                self.units, self.groups, self.per_turn, self.scale = units, groups, per_turn, scale
                self.m, self.r, self.s = rings(name)
                self.up_in = [sem(f"{name}_up_in{u}") for u in range(units)]
                self.down_in = sem(f"{name}_down_in")
                a = area(FFN_AREA)
                self.UP = a(units, 2 * KT * P)
                self.DOWN = a(units, D)
                self.SILU = a(2, S)
                self.HIDDEN = a(units, S)

        def ffn_sync(sp, f, begin):
            def up(u, n):
                sp.dma_start(f.UP[:, u, :], f.w13[ds(n, 1)].rearrange("a p n -> p (a n)")).then_inc(f.up_in[u], 16)

            def down(n):
                sp.dma_start(f.DOWN[:, :, :], f.w2[ds(n, 1)].rearrange("a p (u n) -> p (a u) n", u=f.units)).then_inc(f.down_in, 16)

            begin(sp)
            for u in range(f.units):
                up(u, u)
            for wait, n in f.after:
                sp.wait_ge(wait, n)
            down(0)
            with sp.Fori(1, B * f.groups) as g:
                for u in range(f.units):
                    sp.wait_ge(f.r.full, (g - 1) * f.units + (u + 1 + f.before) + (((g - 1) >> 2) * f.between if f.between else 0))
                    up(u, (g % f.groups) * f.units + u)
                sp.wait_ge(f.s.full, g * ST)
                down(g % f.groups)

        def ffn_tensor_batch(pe, f, m, r, s, n_in, b):
            with loop(pe, f.groups // f.per_turn, (m, f.units * f.per_turn), (r, f.units * f.per_turn),
                      (s, ST * f.per_turn), (n_in, f.per_turn)):
                for _ in range(f.per_turn):
                    n_in.step()
                    hidden = r.now() + 3
                    for u in range(f.units):
                        pe.wait_ge(f.up_in[u], n_in.now() * 16)
                        w = f.UP[:, u, :].rearrange("p (k a n) -> p k a n", k=KT, a=2)
                        for a, (job, n) in enumerate(((f.m, m), (f.r, r))):
                            bank = start_job(pe, job, n)
                            for kt in range(KT):
                                last = nc.tensor.matmul(bank.rearrange("p (a n) -> p a n", a=1), w[:, kt, a, :],
                                                        XT[:, ds(b & 1, 1), kt, :], start=kt == 0, stop=kt == KT - 1)
                            last.then_inc(job.full, 1)
                    pe.wait_ge(f.down_in, n_in.now() * 16)
                    for pair in range(ST // 2):
                        banks = [start_job(pe, f.s, s) for _ in range(2)]
                        for u in range(f.units):
                            if pair == 0:
                                pe.wait_ge(f.r.free, hidden + u)
                            for j, bank in enumerate(banks):
                                st = 2 * pair + j
                                last = nc.tensor.matmul(bank, f.HIDDEN[:, u, st * P:(st + 1) * P], f.DOWN[:, u, :],
                                                        start=u == 0, stop=u == f.units - 1)
                                if u == f.units - 1:
                                    last.then_inc(f.s.full, 1)

        def ffn_tensor(pe, f):
            m, r, s, n_in = Count(), Count(), Count(), Count()
            with loop(pe, B, (m, f.groups * f.units), (r, f.groups * f.units), (s, f.groups * ST), (n_in, f.groups), (T_PE, KT), (N_PE, 1)) as b:
                hold(pe, turn.free, T_PE.now() + 2)
                ffn_tensor_batch(pe, f, m, r, s, n_in, b)
                norm_tensor(pe)

        def ffn_scalar_batch(act, f, m, r):
            with loop(act, f.groups // f.per_turn, (m, f.units * f.per_turn), (r, f.units * f.per_turn)):
                for _ in range(f.per_turn * f.units):
                    act.wait_ge(f.r.free, r.now() + 1)
                    bank = full(act, f.m, m)
                    nc.scalar.activation(f.SILU[:, r.bank(), :], bank, ACT.Silu).then_inc(f.m.free, 1)
                    r.step()

        def ffn_scalar(act, f):
            m, r = Count(), Count()
            act.sem_inc(f.m.free, 2)
            with loop(act, B, (m, f.groups * f.units), (r, f.groups * f.units), (T_ACT, KT)) as b:
                ffn_scalar_batch(act, f, m, r)
                norm_scalar(act, (b + 1) & 1)

        def ffn_vector_batch(v, f, m, r, s, b, between=None, extra=()):
            with loop(v, f.groups // f.per_turn, (m, f.units * f.per_turn), (r, f.units * f.per_turn),
                      (s, ST * f.per_turn), *extra) as turn_:
                for q in range(f.per_turn):
                    for u in range(f.units):
                        v.wait_ge(f.m.free, m.step() + 2)
                        silu = f.SILU[:, r.bank(), :]
                        bank = full(v, f.r, r)
                        nc.vector.tensor_tensor(f.HIDDEN[:, u, :], silu, bank, ALU.mult).then_inc(f.r.free, 1)
                        if between:
                            between(turn_, u)
                    for st in range(ST):
                        if between and st % 2 == 0:
                            between(turn_, f.units + st // 2)
                        bank = full(v, f.s, s)
                        xb = X[:, ds(b * ST + st, 1), :].rearrange("p a n -> p (a n)")
                        nc.vector.scalar_tensor_tensor(out=xb, in0=bank, scalar=f.scale(b, turn_ * f.per_turn + q, st), in1=xb,
                                                       op0=ALU.mult, op1=ALU.add).then_inc(f.s.free, 1)
            v.wait_ge(f.s.free, s.now() + 2)
            v.sem_inc(x_done, 1)

        def ffn_vector(v, f):
            m, r, s = Count(), Count(), Count()
            v.sem_inc(f.r.free, 2)
            v.sem_inc(f.s.free, 2)
            with loop(v, B, (m, f.groups * f.units), (r, f.groups * f.units), (s, f.groups * ST), (T_V, KT), (N_V, 1)) as b:
                norm_vector(v, (b + 1) & 3)
                T_V.step(KT)
                ffn_vector_batch(v, f, m, r, s, b)

        l0f = Ffn("l0f", 1, l0_w13, w2h, UG, HID // P // UG, 1, lambda b, g, st: G[:, 4:5], ((wh_stored, 16),), ST, ST)
        assert l0f.groups == ST
        L0_M, L0_R = UG * ST + 2 + ST, UG * ST + ST
        HAD_M = HID // P

        def l0_tensor(pe):
            m, r, s, n_in = Count(), Count(), Count(), Count()

            def similarities(b):
                for w in (WQ0, WK0):
                    nc.tensor.matmul(start_job(pe, l0f.m, m), w, CT[:, ds(b * S, S)], start=True, stop=True).then_inc(l0f.m.full, 1)
                pe.wait_ge(l0f.m.free, m.now() + 2)
                for st in range(ST):
                    nc.tensor.matmul(start_job(pe, l0f.m, m), QT0[:, st * P:(st + 1) * P], KT0, start=True, stop=True)\
                      .then_inc(l0f.m.full, 1)

            def turn_graph(b):
                pe.wait_ge(graph_ready, b * ST + ST + 1)
                for j in range(ST):
                    bank = start_job(pe, l0f.r, r)
                    for i in range(ST):
                        last = nc.tensor.transpose(bank[:, i * P:(i + 1) * P], GRAPH[:, i, j * P:(j + 1) * P], ID[:, :])
                    last.then_inc(l0f.r.full, 1)

            pe.wait_ge(l0_w, 32)
            similarities(0)
            pe.wait_ge(butterflies, 8)
            for t in range(HAD_M):
                nc.tensor.matmul(start_job(pe, l0f.m, m), HAD, WH[0][:, t, :], start=True, stop=True).then_inc(l0f.m.full, 1)
            turn_graph(0)
            N_PE.step()
            norm_tensor(pe)
            with loop(pe, B - 1, (m, L0_M), (r, L0_R), (s, ST * ST), (n_in, ST), (T_PE, KT), (N_PE, 2)) as b:
                hold(pe, turn.free, T_PE.now() + 2)
                similarities(b + 1)
                ffn_tensor_batch(pe, l0f, m, r, s, n_in, b)
                turn_graph(b + 1)
                N_PE.step()
                norm_tensor(pe)
            pe.wait_ge(turn.free, T_PE.now() + 2)
            ffn_tensor_batch(pe, l0f, m, r, s, n_in, B - 1)
            norm_tensor(pe)

        def l0_scalar(act):
            m, r = Count(), Count()
            act.sem_inc(l0f.m.free, 2)

            def similarities(b):
                for dst in (QT0, KT0):
                    nc.scalar.copy(dst, full(act, l0f.m, m)).then_inc(l0f.m.free, 1)
                act.wait_ge(graph_ready, b * ST + 1)
                for st in range(ST):
                    bank = full(act, l0f.m, m)
                    nc.scalar.activation(SIM[:, st, :], bank, ACT.Copy, scale=float(1.0 / (L0_HEAD ** 0.5 * L0_HEADS)))
                    nc.scalar.activation(GRAPH[:, st, :], bank, ACT.Sigmoid, scale=float(1.0 / (L0_HEAD ** 0.5 * L0_HEADS)))\
                      .then_inc(l0f.m.free, 1)
            similarities(0)
            for t in range(HAD_M):
                nc.scalar.activation(WH[1][:, t, :], full(act, l0f.m, m), ACT.Copy, scale=float(HID ** -0.5)).then_inc(l0f.m.free, 1)
            r.step(ST)
            norm_scalar(act, 0)
            with loop(act, B - 1, (m, L0_M), (r, L0_R), (T_ACT, KT)) as b:
                similarities(b + 1)
                ffn_scalar_batch(act, l0f, m, r)
                r.step(ST)
                norm_scalar(act, (b + 1) & 1)
            ffn_scalar_batch(act, l0f, m, r)
            norm_scalar(act, 0)

        def l0_vector(v):
            m, r, s = Count(), Count(), Count()
            v.sem_inc(l0f.r.free, 2)
            v.sem_inc(l0f.s.free, 2)
            v.sem_inc(graph_ready, 1)
            v.wait_ge(gc_ready, 1)
            steps = 1 + 2 * TOP_ROUNDS - 1 + 1
            rows = lambda b, st: X[:, ds(b * ST + st, 1), :].rearrange("p a n -> p (a n)")

            def add_norm(b):
                v.wait_ge(xn_ready, N_V.now())
                for st in range(ST):
                    nc.vector.scalar_tensor_tensor(out=rows(b, st), in0=XN[:, st, :], scalar=GC[:, 1:2], in1=rows(b, st),
                                                   op0=ALU.mult, op1=ALU.add).then_inc(vec, 1)
                    V.step()

            def search(t0, t1, b, st):
                if t0 == 0:
                    link(v, nc.vector.tensor_copy(WORK.rearrange("p (a n) -> p a n", a=1), SIM[:, ds(st, 1), :]), True)
                for t in range(t0, t1):
                    link(v, nc.vector.max(TOP, WORK), t < TOP_ROUNDS - 1)
                    if t < TOP_ROUNDS - 1:
                        link(v, nc.vector.match_replace(WORK, TOP, WORK, -3.0e38), True)
                if t0 < TOP_ROUNDS and t1 == TOP_ROUNDS:
                    done = b * ST + st + 2
                    at = (TOPK - 1) % 8
                    one = lambda t: t[:, ds(st, 1), :].rearrange("p a n -> p (a n)")
                    nc.vector.scalar_tensor_tensor(out=one(GRAPH), in0=one(SIM), scalar=TOP[:, at:at + 1],
                                                   in1=one(GRAPH), op0=ALU.is_ge, op1=ALU.mult).then_inc(graph_ready, 1)
                    v.wait_ge(graph_ready, done)
                    link(v, nc.vector.scalar_tensor_tensor(out=rows(b, st), in0=one(GRAPH), scalar=GC[:, 2:3], in1=rows(b, st),
                                                           op0=ALU.mult, op1=ALU.add))

            def add_graph(b):
                v.wait_ge(graph_ready, b * ST + ST + 1)
                for st in range(ST):
                    nc.vector.scalar_tensor_tensor(out=rows(b, st), in0=full(v, l0f.r, r), scalar=GC[:, 2:3], in1=rows(b, st),
                                                   op0=ALU.mult, op1=ALU.add).then_inc(l0f.r.free, 1)
                v.wait_ge(l0f.r.free, r.now() + 2)
                v.sem_inc(x_done, 1)

            assert UG == 4
            places = [TOP_ROUNDS * k // 20 for k in (0, 4, 8, 11, 13, 13, 20)]
            add_norm(0)
            m.step(2 + ST)
            v.wait_ge(l0f.m.free, m.now() + 2)
            with loop(v, ST, (V, steps)) as st:
                search(0, TOP_ROUNDS, 0, st)
            add_graph(0)
            m.step(HAD_M)
            norm_vector(v, 0)
            T_V.step(KT)
            v.wait_ge(x_rest, 16)
            with loop(v, B - 1, (m, L0_M), (r, L0_R), (s, ST * ST), (V, ST + ST * steps), (T_V, KT), (N_V, 2)) as b:
                norm_vector(v, b + 1)
                add_norm(b + 1)
                m.step(2 + ST)
                hold(v, l0f.m.free, m.now() + 2)
                ffn_vector_batch(v, l0f, m, r, s, b, lambda g, k: search(places[k], places[k + 1], b + 1, g), ((V, steps),))
                add_graph(b + 1)
                norm_vector(v, b + 1)
                T_V.step(KT)
            norm_vector(v, 0)
            T_V.step(KT)
            ffn_vector_batch(v, l0f, m, r, s, B - 1)

        l1m, l1r, l1s = rings("l1")
        a = area(FFN_AREA)
        WK1, CTB, KVT1, OUT1 = a(C), a(S), a(S), a(S)
        CT1 = a(B * S)
        KV1 = a(ST, C)
        PROB1 = a(ST, S)
        ROWS1 = a(2, S)
        BKR, BK1 = a(C), a(1)
        l1_w, ctb_ready = sem("l1_w"), sem("ctb_ready")
        var1_ready, root1_ready, norm1_ready, exp1_done, prob1_used = [sem(n) for n in (
            "var1_ready", "root1_ready", "norm1_ready", "exp1_done", "prob1_used")]

        def l1_sync(sp):
            sp.wait_ge(x_done, 2 * B)
            sp.dma_start(WK1, l1_wk).then_inc(l1_w, 16)
            sp.dma_start(CT1, ctx_t).then_inc(l1_w, 16)
            sp.dma_start(BK1, l1_bk).then_inc(l1_w, 16)
            sp.dma_start(BKR, l1_bk_row.to_broadcast([P, C])).then_inc(l1_w, 16)
            sp.dma_start(ROWS1, l1_ln.rearrange("(o a) n -> o a n", o=1).to_broadcast([P, 2, S])).then_inc(l1_w, 16)

        def l1_tensor(pe):
            m, r, s = Count(), Count(), Count()
            pe.wait_ge(x_done, 2 * B)
            pe.wait_ge(l1_w, 80)
            with loop(pe, B, (m, 2), (r, 1 + 1), (s, ST), (T_PE, KT), (N_PE, 1)) as b:
                hold(pe, turn.free, T_PE.now() + 2)
                hold(pe, ctb_ready, b + 1)
                nc.tensor.matmul(start_job(pe, l1m, m), WK1, CTB, start=True, stop=True).then_inc(l1m.full, 1)
                for half in range(2):
                    bank = start_job(pe, l1r, r)
                    for j in range(2):
                        jt = 2 * half + j
                        last = nc.tensor.matmul(bank[:, j * C:(j + 1) * C], CTB[:, jt * P:(jt + 1) * P], WK1, start=True, stop=True)
                    last.then_inc(l1r.full, 1)
                hold(pe, l1r.free, r.now() + 2)
                bank = start_job(pe, l1m, m)
                for jt in range(ST):
                    last = nc.tensor.matmul(bank.rearrange("p (a n) -> p a n", a=1), KV1[:, jt, :], XT[:, ds(b & 1, 1), jt, :],
                                            start=jt == 0, stop=jt == ST - 1)
                last.then_inc(l1m.full, 1)
                pe.wait_ge(l1m.free, m.now() + 2)
                for st in range(ST):
                    nc.tensor.matmul(start_job(pe, l1s, s), OUT1[:, st * P:(st + 1) * P], KVT1, start=True, stop=True)\
                      .then_inc(l1s.full, 1)
                norm_tensor(pe)

        def l1_scalar(act):
            m, s = Count(), Count()
            act.sem_inc(l1m.free, 2)
            act.sem_inc(l1s.free, 2)
            with loop(act, B, (m, 2), (s, ST), (T_ACT, KT)) as b:
                nc.scalar.activation(KVT1, full(act, l1m, m), ACT.Identity, bias=BK1).then_inc(l1m.free, 1)
                nc.scalar.copy(OUT1, full(act, l1m, m)).then_inc(l1m.free, 1)
                act.wait_ge(prob1_used, b + 1)
                for st in range(ST):
                    nc.scalar.copy(PROB1[:, st, :], full(act, l1s, s)).then_inc(l1s.free, 1)
                norm_scalar(act, (b + 1) & 1)
                act.wait_ge(norm1_ready, b + 1)
                for st in range(ST):
                    nc.scalar.activation(PROB1[:, st, :], PROB1[:, st, :], ACT.Exp, bias=NEGM1[:, st:st + 1],
                                         accum_out=SUM1[:, st:st + 1]).then_inc(exp1_done, 1)

        def l1_vector(v):
            r, s = Count(), Count()
            v.sem_inc(l1r.free, 2)
            v.sem_inc(prob1_used, 1)
            v.wait_ge(l1_w, 80)
            scale = float(512 ** -0.5)
            with loop(v, B, (r, 2), (s, ST), (V, 2 * ST - 1 + 7), (T_V, KT), (N_V, 1)) as b:
                for half in range(2):
                    bank = full(v, l1r, r)
                    nc.vector.tensor_tensor(KV1[:, 2 * half:2 * half + 2, :], bank[:, 0:2 * C].rearrange("p (j c) -> p j c", j=2),
                                            BKR.rearrange("p (a c) -> p a c", a=1).to_broadcast([P, 2, C]), ALU.add)\
                      .then_inc(l1r.free, 1)
                norm_vector(v, (b + 1) & 3)
                T_V.step(KT)
                for st in range(ST):
                    s.step()
                    hold(v, l1s.free, s.now() + 2)
                    nc.vector.bn_stats(STAT[:, st, :], PROB1[:, st, :]).then_inc(vec, 1)
                    V.step()
                hold(v, vec, V.now())
                for st in range(ST):
                    last = nc.vector.bn_aggr(MV[:, st, :], STAT[:, st, :])
                link(v, last)
                nc.vector.tensor_scalar(VAR1, MV[:, :, 1], scale * scale, EPS_INNER, ALU.mult, ALU.add).then_inc(var1_ready, 1)
                v.wait_ge(root1_ready, b + 1)
                link(v, nc.vector.tensor_scalar(RS1, RS1, scale, None, ALU.mult))
                for st in range(ST):
                    last = nc.vector.tensor_scalar(PROB1[:, st, :], PROB1[:, st, :], MV[:, st, 0:1], RS1[:, st:st + 1],
                                                   ALU.subtract, ALU.mult)
                link(v, last)
                for row, op in ((0, ALU.mult), (1, ALU.add)):
                    link(v, nc.vector.tensor_tensor(PROB1, PROB1, ROWS1[:, row:row + 1, :].to_broadcast([P, ST, S]), op))
                nc.vector.tensor_reduce(NEGM1, PROB1, op=ALU.max, axis=AX.X, negate=True).then_inc(norm1_ready, 1)
                v.wait_ge(exp1_done, b * ST + ST)
                link(v, nc.vector.reciprocal(SUM1, SUM1))
                link(v, nc.vector.tensor_scalar(SUM1, SUM1, G[:, 1:2], None, ALU.mult))
                for st in range(ST):
                    xb = X[:, ds(b * ST + st, 1), :].rearrange("p a n -> p (a n)")
                    last = nc.vector.scalar_tensor_tensor(out=xb, in0=PROB1[:, st, :], scalar=SUM1[:, st:st + 1], in1=xb,
                                                          op0=ALU.mult, op1=ALU.add)
                    if st < ST - 1:
                        last.then_inc(vec, 1)
                        V.step()
                last.then_inc(prob1_used, 1)
                v.wait_ge(prob1_used, b + 2)
                v.sem_inc(x_done, 1)

        def l1_pool(pool):
            pool.wait_ge(l1_w, 80)
            with loop(pool, B, (N_P, 1)) as b:
                pool.wait_ge(l1r.free, b * 2 + 2)
                nc.gpsimd.tensor_copy(CTB, CT1[:, ds(b * S, S)]).then_inc(ctb_ready, 1)
                norm_pool(pool)
                pool.wait_ge(var1_ready, b + 1)
                nc.gpsimd.tensor_tensor(RS1, VAR1, HALF[:, :], ALU.pow).then_inc(root1_ready, 1)

        la, lr, ls = rings("l1f")
        a = area()
        AGG, D1, D2, BC, GATE = a(KT, D), a(KT, HID), a(HID // P, D), a(KT, D), a(KT, D)
        COLS = a(2 * KT)
        COL = {}
        COL["bc"], COL["gate"] = COLS[:, 0:KT], COLS[:, KT:2 * KT]
        OROWS = a(2, D)
        BCT, T0 = a(4 * B), a(4 * B)
        assert a.here() <= FFN_AREA
        a = area(FFN_AREA)
        GT, OT, ON = a(KT, S), a(KT, S), a(ST, D)
        XL, INR = a(D), a(2, D)
        SL, ML, VL, RL = a(6), a(2), a(1), a(1)
        TH, TR = a(D), a(D)
        assert a.here() <= AREA
        a = area(FFN_AREA)
        TB = a(4, D)
        TB = {k: TB[0:B, i, :] for i, k in enumerate(("agg", "d2", "pn_g", "pn_b"))}
        D1ROW, HROW = a(D), a(D)
        TURNED = a(KT, 32)
        HTURNED = a(KT, P)
        PART, SUM4A = a(D), a(32)
        TB_ALL = AR[0:B, FFN_AREA:FFN_AREA + 4 * D]
        l1f_w, l1f_in, xl_in = sem("l1f_w"), sem("l1f_in"), sem("xl_in")
        th_ready, root_in, root_out = sem("th_ready"), sem("root_in"), sem("root_out")
        gelu_done, mix_done, out_norm = sem("gelu_done"), sem("mix_done"), sem("out_norm")
        t0_done = sem("t0_done")
        ROOTS = 2 + 1 + K_STEPS

        def l1f_sync_weights(sp):
            for dst, src in ((AGG, l1_agg), (D1, l1_d1), (D2, l1_d2), (BC, l1_bc), (GATE, l1_gate), (COLS, l1_cols)):
                sp.dma_start(dst, src).then_inc(l1f_w, 16)
            sp.dma_start(OROWS, l1_rows.rearrange("(o a) n -> o a n", o=1).to_broadcast([P, 2, D])).then_inc(l1f_w, 16)

        def l1f_sync(sp):
            sp.wait_ge(x_done, 3 * B)
            for b in range(B):
                sp.dma_start(XL[b:b + 1, :], X[P - 1:P, b * ST + ST - 1, :]).then_inc(xl_in, 16)
            sp.dma_start(TB_ALL, l1_trows.to_broadcast([B, 4 * D])).then_inc(xl_in, 16)
            for n in range(4):
                sp.dma_start(D1ROW[32 * n:32 * n + 32, :], l1_d1row[n:n + 1, :].to_broadcast([32, D])).then_inc(xl_in, 16)
            sp.dma_start(SUM4A, sum4).then_inc(xl_in, 16)
            sp.dma_start(INR[0:B, :, :], l1_inrows.rearrange("(o a) n -> o a n", o=1).to_broadcast([B, 2, D])).then_inc(xl_in, 16)

        def cols(t):
            return t.rearrange("p (m b) -> p m b", b=B)

        def over_b(col, n):
            return col.rearrange("p (m o) -> p m o", o=1).to_broadcast([P, n, B])

        def turn_rows(pe, n, of):
            hold(pe, lr.free, n.now() + 1)
            bank = start_job(pe, lr, n, waited=True)
            for k in range(KT):
                last = nc.tensor.transpose(bank[:, k * B:(k + 1) * B], of[0:B, k * P:(k + 1) * P], ID[0:B, 0:B])
            last.then_inc(lr.full, 1)

        def row_product(pe, n, of, w, tiles_in):
            bank = start_job(pe, lr, n)
            for k in range(tiles_in):
                last = nc.tensor.matmul(bank[0:B, :], of[:, k * B:(k + 1) * B], w[:, k, :], start=k == 0, stop=k == tiles_in - 1)
            last.then_inc(lr.full, 1)

        def small_products(pe, n, w, of, tiles_in, tiles_out):
            bank = start_job(pe, lr, n)
            for mt in range(tiles_out):
                for kt in range(tiles_in):
                    last = nc.tensor.matmul(bank[:, mt * B:(mt + 1) * B], w[:, kt, mt * P:(mt + 1) * P], of[:, kt, 0:B],
                                            start=kt == 0, stop=kt == tiles_in - 1)
            last.then_inc(lr.full, 1)

        def l1f_tensor(pe):
            m, r, s, th, gl = Count(), Count(), Count(), Count(), Count()
            pe.wait_ge(x_done, 3 * B)
            pe.wait_ge(l1f_w, 7 * 16)
            pe.wait_ge(th_ready, th.step())
            bank = start_job(pe, la, m)
            for kt in range(KT):
                last = nc.tensor.transpose(bank[:, kt * B:(kt + 1) * B], XL[0:B, kt * P:(kt + 1) * P], ID[0:B, 0:B])
            last.then_inc(la.full, 1)
            pe.wait_ge(la.free, m.now() + 2)
            row_product(pe, r, T0, AGG, KT)
            with loop(pe, K_STEPS, (r, 6), (th, 1), (gl, 1)):
                hold(pe, th_ready, th.step())
                turn_rows(pe, r, TR)
                hold(pe, lr.free, r.now() + 2)
                bank = start_job(pe, lr, r)
                for kt in range(KT):
                    for n in range(4):
                        last = nc.tensor.matmul(bank[32 * n:32 * n + 32, :], TURNED[:, kt, :], D1[:, kt, n * D:(n + 1) * D],
                                                start=kt == 0, stop=kt == KT - 1)
                last.then_inc(lr.full, 1)
                hold(pe, gelu_done, gl.step())
                for half in range(2):
                    bank = start_job(pe, lr, r)
                    for c in range(2):
                        at = (2 * half + c) * P
                        last = nc.tensor.transpose(bank[:, c * P:(c + 1) * P], HROW[:, at:at + P], ID[:, :])
                    last.then_inc(lr.full, 1)
                hold(pe, lr.free, r.now() + 2)
                bank = start_job(pe, lr, r)
                for c in range(4):
                    for n in range(4):
                        last = nc.tensor.matmul(bank[32 * n:32 * n + 32, :], HTURNED[:, c, 32 * n:32 * n + 32], D2[:, 4 * n + c, :],
                                                start=c == 0, stop=c == 3)
                last.then_inc(lr.full, 1)
                hold(pe, lr.free, r.now() + 2)
                nc.tensor.matmul(start_job(pe, lr, r)[0:32, :], SUM4A, PART, start=True, stop=True).then_inc(lr.full, 1)
            pe.wait_ge(th_ready, th.step())
            turn_rows(pe, r, TH)
            pe.wait_ge(lr.free, r.now() + 2)
            small_products(pe, r, BC, TURNED, KT, KT)
            m.step()
            bank = BM[:, 1, :]
            nc.tensor.matmul(bank[:, 0:P], ID[:, :], ID[:, :], start=True, stop=True).then_inc(la.full, 1)
            with loop(pe, B, (m, KT), (s, ST), (T_PE, KT), (N_PE, 1)) as b:
                hold(pe, turn.free, T_PE.now() + 2)
                for mt in range(KT):
                    bank = start_job(pe, la, m)
                    for kt in range(KT):
                        last = nc.tensor.matmul(bank.rearrange("p (a n) -> p a n", a=1), GATE[:, kt, mt * P:(mt + 1) * P],
                                                XT[:, ds(b & 1, 1), kt, :], start=kt == 0, stop=kt == KT - 1)
                    last.then_inc(la.full, 1)
                for st in range(ST):
                    if st == 0:
                        hold(pe, mix_done, b * KT + KT + 1)
                    bank = start_job(pe, ls, s)
                    for mt in range(KT):
                        last = nc.tensor.transpose(bank[:, mt * P:(mt + 1) * P], OT[:, mt, st * P:(st + 1) * P], ID[:, :])
                    last.then_inc(ls.full, 1)
                norm_tensor(pe)

        def l1f_scalar(act):
            m, s = Count(), Count()
            act.sem_inc(la.free, 2)
            act.sem_inc(ls.free, 2)
            nc.scalar.copy(T0, full(act, la, m)[:, 0:4 * B]).then_inc(la.free, 1)
            with act.Fori(0, K_STEPS) as k:
                act.wait_ge(t0_done, k + 1)
                nc.scalar.activation(HROW, HROW, ACT.Gelu).then_inc(gelu_done, 1)
            nc.scalar.copy(T0[:, 0:1], full(act, la, m)[:, 0:1]).then_inc(la.free, 1)
            with loop(act, B, (m, KT), (s, ST), (T_ACT, KT)) as b:
                act.wait_ge(mix_done, b * KT + 1)
                for mt in range(KT):
                    nc.scalar.activation(GT[:, mt, :], full(act, la, m), ACT.Sigmoid, bias=COL["gate"][:, mt:mt + 1]).then_inc(la.free, 1)
                act.wait_ge(out_norm, b * 2 + 1)
                for st in range(ST):
                    nc.scalar.copy(ON[:, st, :], full(act, ls, s)).then_inc(ls.free, 1)
                norm_scalar(act, (b + 1) & 1)

        def l1f_vector(v):
            m, r, s, root = Count(), Count(), Count(), Count()
            for q in (lr.free, mix_done, out_norm):
                v.sem_inc(q, 2 if q is lr.free else 1)
            v.wait_ge(l1f_w, 7 * 16)
            link(v, nc.vector.tensor_scalar(OROWS, OROWS, G[:, 5:6], None, ALU.mult))
            v.wait_ge(xl_in, 11 * 16)
            nc.vector.memset(TURNED, 0.0).then_inc(vec, 1)
            V.step()
            for eps in (EPS_BLOCK, EPS_INNER):
                link(v, nc.vector.bn_stats(SL[0:B, :], XL[0:B, :]))
                link(v, nc.vector.bn_aggr(ML[0:B, :], SL[0:B, :]))
                nc.vector.tensor_scalar(VL[0:B, :], ML[0:B, 1:2], eps, None, ALU.add).then_inc(root_in, 1)
                v.wait_ge(root_out, root.step())
                link(v, nc.vector.tensor_scalar(XL[0:B, :], XL[0:B, :], ML[0:B, 0:1], RL[0:B, :], ALU.subtract, ALU.mult))
            link(v, nc.vector.tensor_tensor(XL[0:B, :], XL[0:B, :], INR[0:B, 0, :], ALU.mult))
            nc.vector.tensor_tensor(XL[0:B, :], XL[0:B, :], INR[0:B, 1, :], ALU.add).then_inc(th_ready, 1)

            def norm_thought():
                link(v, nc.vector.bn_stats(SL[0:B, :], TH[0:B, :]), True)
                link(v, nc.vector.bn_aggr(ML[0:B, :], SL[0:B, :]))
                nc.vector.tensor_scalar(VL[0:B, :], ML[0:B, 1:2], EPS_INNER, None, ALU.add).then_inc(root_in, 1)
                v.wait_ge(root_out, root.step())
                link(v, nc.vector.tensor_scalar(TR[0:B, :], TH[0:B, :], ML[0:B, 0:1], RL[0:B, :], ALU.subtract, ALU.mult))
                link(v, nc.vector.tensor_tensor(TR[0:B, :], TR[0:B, :], TB["pn_g"], ALU.mult))
                nc.vector.tensor_tensor(TR[0:B, :], TR[0:B, :], TB["pn_b"], ALU.add).then_inc(th_ready, 1)

            bank = full(v, lr, r)
            nc.vector.tensor_tensor(TH[0:B, :], bank[0:B, :], TB["agg"], ALU.add).then_inc(lr.free, 1)
            v.wait_ge(lr.free, r.now() + 2)
            norm_thought()
            turned = TURNED[:, :, 0:B]
            with loop(v, K_STEPS, (r, 6), (V, 5), (root, 1)):
                nc.vector.tensor_copy(turned, cols(full(v, lr, r)[:, 0:4 * B])).then_inc(lr.free, 1)
                nc.vector.tensor_tensor(HROW, full(v, lr, r), D1ROW, ALU.add).then_inc(lr.free, 1)
                v.wait_ge(lr.free, r.now() + 2)
                v.sem_inc(t0_done, 1)
                for half in range(2):
                    nc.vector.tensor_copy(HTURNED[:, 2 * half:2 * half + 2, :], full(v, lr, r)[:, 0:2 * P].rearrange("p (c n) -> p c n", c=2))\
                      .then_inc(lr.free, 1)
                nc.vector.tensor_copy(PART, full(v, lr, r)).then_inc(lr.free, 1)
                bank = full(v, lr, r)
                link(v, nc.vector.tensor_tensor(TR[0:B, :], bank[0:B, :], TB["d2"], ALU.add))
                nc.vector.tensor_tensor(TH[0:B, :], TH[0:B, :], TR[0:B, :], ALU.add).then_inc(lr.free, 1)
                hold(v, lr.free, r.now() + 2)
                norm_thought()
            nc.vector.tensor_copy(turned, cols(full(v, lr, r)[:, 0:4 * B])).then_inc(lr.free, 1)
            bank = full(v, lr, r)
            nc.vector.tensor_tensor(cols(BCT), cols(bank[:, 0:4 * B]), over_b(COL["bc"], 4), ALU.add).then_inc(lr.free, 1)
            v.wait_ge(lr.free, r.now() + 2)
            m.step(2)
            with loop(v, B, (m, KT), (s, ST), (V, ST + 1 + 1 + 2), (T_V, KT), (N_V, 1), (root, 1)) as b:
                norm_vector(v, (b + 1) & 3)
                T_V.step(KT)
                for mt in range(KT):
                    m.step()
                    v.wait_ge(la.free, m.now() + 2)
                    one = lambda t: t.rearrange("p (a n) -> p a n", a=1)
                    nc.vector.scalar_tensor_tensor(out=one(OT[:, mt, :]), in0=one(GT[:, mt, :]), scalar=BCT[:, ds(mt * B + b, 1)],
                                                   in1=XT[:, ds(b & 1, 1), mt, :], op0=ALU.mult, op1=ALU.add).then_inc(mix_done, 1)
                for st in range(ST):
                    s.step()
                    hold(v, ls.free, s.now() + 2)
                    nc.vector.bn_stats(STAT[:, st, :], ON[:, st, :]).then_inc(vec, 1)
                    V.step()
                hold(v, vec, V.now())
                for st in range(ST):
                    last = nc.vector.bn_aggr(MV[:, st, :], STAT[:, st, :])
                link(v, last)
                nc.vector.tensor_scalar(VAR1, MV[:, :, 1], EPS_INNER, None, ALU.add).then_inc(root_in, 1)
                v.wait_ge(root_out, root.step())
                for st in range(ST):
                    last = nc.vector.tensor_scalar(ON[:, st, :], ON[:, st, :], MV[:, st, 0:1], RS1[:, st:st + 1],
                                                   ALU.subtract, ALU.mult)
                link(v, last)
                link(v, nc.vector.tensor_tensor(ON, ON, OROWS[:, 0:1, :].to_broadcast([P, ST, D]), ALU.mult))
                nc.vector.tensor_tensor(ON, ON, OROWS[:, 1:2, :].to_broadcast([P, ST, D]), ALU.add).then_inc(out_norm, 1)
                v.wait_ge(out_norm, b * 2 + 2)
                xb = X[:, ds(b * ST, ST), :]
                nc.vector.tensor_tensor(xb, xb, ON, ALU.add).then_inc(out_norm, 1)
                v.wait_ge(out_norm, b * 2 + 3)
                v.sem_inc(x_done, 1)
                v.sem_inc(vec, 1)
                V.step()

        def l1f_pool(pool):
            for n in range(ROOTS):
                pool.wait_ge(root_in, n + 1)
                nc.gpsimd.tensor_tensor(RL[0:B, :], VL[0:B, :], HALF[0:B, 0:1], ALU.pow).then_inc(root_out, 1)
            with loop(pool, B, (N_P, 1)) as b:
                norm_pool(pool)
                pool.wait_ge(root_in, b + ROOTS + 1)
                nc.gpsimd.tensor_tensor(RS1, VAR1, HALF[:, :], ALU.pow).then_inc(root_out, 1)

        ar, as_ = ring(BR, "l2_r"), ring(BS, "l2_s")
        aq = Ring(BM[:, 0:1, :], sem("l2_q_full"), sem("l2_q_free"))
        ao = Ring(BM[:, 1:2, :], sem("l2_out_full"), sem("l2_out_free"))
        a = area()
        CN2 = a(B * ST, C)
        KRAW = a(KVH, S)
        QHI, QLO = a(ST, D), a(ST, D)
        QST = a(2, ST, P)
        PROB2, PROBT2 = a(2 * ST, S), a(ST, S)
        VWIN = a(2 * ST, 3 * HD)
        OUT2, OUTS, TMP2 = a(S), a(S), a(S)
        SUM4 = a(32)
        SUM2, RS2, NEG2 = a(2 * ST), a(ST * 8), a(2 * ST)
        KPARTS = sb("KPARTS", [P, KVH, S], F32R)
        QPARTS = sb("QPARTS", [P, 2, S], F32R)
        HG = QH // 8
        zeroed, kraw_in, cn2_in, kparts_ready, q_cut = [sem(n) for n in ("zeroed", "kraw_in", "cn2_in", "kparts_ready", "q_cut")]
        q_staged, v_staged, max_done, sum4_in, khi_ready = [sem(n) for n in ("q_staged", "v_staged", "max_done", "sum4_in", "khi_ready")]

        def l2_sync(sp):
            sp.wait_ge(x_done, 4 * B)
            sp.dma_start(SUM4, sum4).then_inc(sum4_in, 16)
            sp.dma_start(CN2, ctx_n.rearrange("(n p) d -> p n d", p=P)).then_inc(cn2_in, 16)
            sp.wait_ge(zeroed, 3)
            with sp.Fori(0, B) as b:
                sp.wait_ge(kparts_ready, 2 * b + 2)
                for q in range(4):
                    sp.dma_start(KRAW[32 * q:32 * q + HD, :, :],
                                 ctx_t[:, ds(b * S, S)].rearrange("(k d) t -> d k t", d=HD)).then_inc(kraw_in, 16)

        def l2_tensor(pe):
            r, s, q, o, vs = Count(), Count(), Count(), Count(), Count()
            pe.wait_ge(x_done, 4 * B)
            pe.wait_ge(sum4_in, 16)

            def turn_queries(j):
                hold(pe, q_staged, q.now() + 1)
                bank = start_job(pe, aq, q)
                for st in range(ST):
                    last = nc.tensor.transpose(bank[:, st * P:(st + 1) * P], QST[:, j % 2, st, :], ID[:, :])
                last.then_inc(aq.full, 1)

            def scores(j, st, key):
                nc.tensor.matmul(start_job(pe, as_, s).rearrange("p (a n) -> p a n", a=1),
                                 QPARTS[:, j % 2, st * P:(st + 1) * P], KPARTS[:, ds(key, 1), :],
                                 start=True, stop=True).then_inc(as_.full, 1)

            def mix_values(j, lt, bank, copied):
                pe.wait_ge(*copied)
                at = 0 if j % 2 else HD
                return nc.tensor.matmul(bank[32 * lt:32 * lt + 32, :], VWIN[:, (j // 4) * ST + lt, at:at + 32], PROBT2[:, lt, :],
                                        start=j % 2 == 0, stop=j % 2 == 1)

            def sum_parts(pair):
                hold(pe, ao.free, o.now() + 1)
                bank = start_job(pe, ar, r)
                nc.tensor.matmul(bank[32 * pair:32 * pair + 32, :], SUM4, OUT2, start=True, stop=True).then_inc(ar.full, 1)

            with loop(pe, B, (r, 2 * QH + 6 * HG), (s, ST * QH + ST), (q, QH + 2), (o, 4 * HG), (T_PE, 2 * QH + KT), (N_PE, 1), (vs, 2 * HG)) as b:
                hold(pe, kparts_ready, 2 * b + 4)
                turn_queries(0)
                turn_queries(1)
                hold(pe, aq.free, q.now())
                for st in range(ST):
                    scores(0, st, 0)
                with loop(pe, HG, (r, 22), (s, ST * 8), (q, 8), (o, 4), (T_PE, 16), (vs, 2)) as hg:
                    for j in range(8):
                        copied = [None] * ST
                        hold(pe, aq.free, q.now() + 1)
                        exped = s.now() + 2
                        for k in range(ST):
                            scores(j + 1, k, (hg * 2 + (j + 1) // 4) & (KVH - 1))
                            if k == 0:
                                hold(pe, as_.free, exped)
                            job, n = (turn, T_PE) if k % 2 == 0 else (ar, r)
                            bank = start_job(pe, job, n)
                            for st in range(ST):
                                last = nc.tensor.transpose(bank[:, st * P:(st + 1) * P], PROB2[:, (j % 2) * ST + st, k * P:(k + 1) * P], ID[:, :])
                            last.then_inc(job.full, 1)
                            copied[k] = job.free, n.now() + 2
                            if k == 0 and j % 2 == 0 and j:
                                sum_parts(j // 2 - 1)
                            if k == 1 and j % 2 == 0:
                                out_bank = start_job(pe, ao, o)
                            if k == 1 and j % 4 == 0:
                                hold(pe, v_staged, vs.step())
                            if k:
                                mix_values(j, k - 1, out_bank, copied[k - 1])
                            if k == 1:
                                turn_queries(j)
                        last = mix_values(j, ST - 1, out_bank, copied[ST - 1])
                        if j % 2:
                            last.then_inc(ao.full, 1)
                    sum_parts(3)
                    hold(pe, ar.free, r.now() + 2)
                    for half in range(2):
                        bank = start_job(pe, ar, r)
                        for st in range(2):
                            at = (2 * half + st) * P
                            last = nc.tensor.transpose(bank[:, st * P:(st + 1) * P], OUTS[:, at:at + P], ID[:, :])
                        last.then_inc(ar.full, 1)
                norm_tensor(pe)

        def l2_scalar(act):
            s, q, o = Count(), Count(), Count()
            act.sem_inc(as_.free, 2)
            act.sem_inc(aq.free, 1)
            act.sem_inc(ao.free, 1)

            def queries(j):
                nc.scalar.copy(QPARTS[:, j % 2, :], full(act, aq, q)).then_inc(aq.free, 1)

            def exps(j, st):
                act.wait_ge(max_done, s.now() + 1)
                bank = full(act, as_, s)
                nc.scalar.activation(PROB2[:, (j % 2) * ST + st, :], bank, ACT.Exp, bias=NEG2[:, (j % 2) * ST + st:(j % 2) * ST + st + 1],
                                     accum_out=SUM2[:, (j % 2) * ST + st:(j % 2) * ST + st + 1]).then_inc(as_.free, 1)

            with loop(act, B, (s, ST * QH + ST), (q, QH + 2), (o, 4 * HG), (T_ACT, 2 * QH + KT)) as b:
                queries(0)
                queries(1)
                for st in range(ST):
                    exps(0, st)
                with loop(act, HG, (s, ST * 8), (q, 8), (o, 4), (T_ACT, 16)) as hg:
                    for j in range(8):
                        for st in range(ST):
                            if st % 2 == 0:
                                nc.scalar.copy(PROBT2[:, st, :], full(act, turn, T_ACT)).then_inc(turn.free, 1)
                            exps(j + 1, st)
                            if st == 1:
                                queries(j)
                        if j % 2:
                            nc.scalar.copy(OUT2, full(act, ao, o)).then_inc(ao.free, 1)
                norm_scalar(act, (b + 1) & 1)

        def l2_vector(v):
            r, s, q = Count(), Count(), Count()
            v.sem_inc(ar.free, 2)
            v.sem_inc(kparts_ready, 2)

            def maximum(j, st):
                at = (j % 2) * ST + st
                nc.vector.tensor_reduce(NEG2[:, at:at + 1], full(v, as_, s), op=ALU.max, axis=AX.X, negate=True).then_inc(max_done, 1)

            with loop(v, B, (r, 2 * QH + 6 * HG), (s, ST * QH + ST), (q, QH + 2), (V, 1 + (8 + 3) * HG), (T_V, 2 * QH + KT), (N_V, 1)) as b:
                v.wait_ge(kraw_in, b * 64 + 64)
                nc.vector.tensor_copy(KPARTS[:, :, :], KRAW).then_inc(khi_ready, 1)
                v.wait_ge(khi_ready, b + 1)
                low = KVH // 2
                nc.vector.tensor_tensor(KPARTS[64:128, 0:low, :], KRAW[64:128, 0:low, :], KPARTS[64:128, 0:low, :].bitcast(F32), ALU.subtract)\
                  .then_inc(kparts_ready, 1)
                v.wait_ge(aq.free, q.now() + 1)
                q.step(QH + 2)
                link(v, nc.vector.tensor_scalar(QHI.bitcast(F32R), XN[:, :, :], HD ** -0.5, None, ALU.mult))
                nc.vector.scalar_tensor_tensor(out=QLO, in0=XN[:, :, :], scalar=HD ** -0.5, in1=QHI, op0=ALU.mult, op1=ALU.subtract)\
                  .then_inc(q_cut, 1)
                v.wait_ge(q_cut, b + 1)
                for st in range(ST):
                    maximum(0, st)
                norm_vector(v, (b + 1) & 3)
                with loop(v, HG, (r, 22), (s, ST * 8), (V, 11), (T_V, 16)) as hg:
                    def take_pair(pair):
                        rows = slice(32 * pair, 32 * pair + 32)
                        nc.vector.tensor_copy(OUTS[rows, :], full(v, ar, r)[rows, :]).then_inc(ar.free, 1)

                    for j in range(8):
                        hold(v, as_.free, s.now() + 2)
                        nc.vector.reciprocal(RS2.rearrange("p (s e) -> p s e", e=8)[:, :, j:j + 1],
                                             SUM2[:, (j % 2) * ST:(j % 2) * ST + ST].rearrange("p (s o) -> p s o", o=1)).then_inc(vec, 1)
                        V.step()
                        for st in range(ST):
                            maximum(j + 1, st)
                            if st == 0 and j % 2 == 0 and j:
                                take_pair(j // 2 - 1)
                            if st % 2 == 1:
                                nc.vector.tensor_copy(PROBT2[:, st, :], full(v, ar, r)).then_inc(ar.free, 1)
                        T_V.step(2)
                    take_pair(3)
                    v.wait_ge(vec, V.now())
                    link(v, nc.vector.tensor_scalar(RS2, RS2, G[:, 2:3], None, ALU.mult))
                    for half in range(2):
                        bank = full(v, ar, r)
                        last = nc.vector.tensor_tensor(TMP2[:, half * 2 * P:(half + 1) * 2 * P].rearrange("p (a d) -> p a d", d=HD),
                                                       bank[:, 0:2 * P].rearrange("p (a d) -> p a d", d=HD),
                                                       RS2[:, half * 16:(half + 1) * 16].rearrange("p (a o) -> p a o", o=1).to_broadcast([P, 16, HD]), ALU.mult)
                        last.then_inc(ar.free, 1)
                    v.wait_ge(ar.free, r.now() + 2)
                    xb = X[:, ds(b * ST, ST), ds(hg * 8 * HD, 8 * HD)]
                    link(v, nc.vector.tensor_tensor(xb, xb, TMP2.rearrange("p (s n) -> p s n", s=ST), ALU.add))
                    v.sem_inc(vec, 1)
                    V.step()
                T_V.step(KT)
                v.sem_inc(x_done, 1)

        def l2_pool(pool):
            q = Count()
            pool.wait_ge(x_done, 4 * B)
            for t in (KRAW, QST, VWIN):
                nc.gpsimd.memset(t, 0.0).then_inc(zeroed, 1)
            pool.wait_ge(zeroed, 3)
            pool.wait_ge(cn2_in, 16)

            def stage_queries(j, head):
                to = QST[:, j % 2, :, :].rearrange("p s (a two w) -> p s a two w", two=2, w=32)
                for part, of in ((0, QHI), (1, QLO)):
                    src = of[:, :, ds(head * HD, HD)].rearrange("p s (a d) -> p s a d", a=1)
                    last = nc.gpsimd.tensor_copy(to[:, :, :, part, 0:HD], src.to_broadcast([P, ST, 2, HD]))
                last.then_inc(q_staged, 1)

            def stage_values(u, group):
                nc.gpsimd.tensor_copy(VWIN[:, u * ST:(u + 1) * ST, HD:2 * HD],
                                      CN2[:, ds(((group >> 2) & 3) * ST, ST), ds(((group & 3) * 2 + u) * HD, HD)]).then_inc(v_staged, 1)
            nc.gpsimd.tensor_copy(VWIN[:, 0:ST, HD:2 * HD], CN2[:, 0:ST, 0:HD]).then_inc(v_staged, 1)
            with loop(pool, B, (q, QH + 2), (N_P, 1)) as b:
                hold(pool, v_staged, b * (2 * HG) + 1)
                pool.wait_ge(khi_ready, b + 1)
                low = slice(KVH // 2, KVH)
                nc.gpsimd.tensor_tensor(KPARTS[64:128, low, :], KRAW[64:128, low, :], KPARTS[64:128, low, :].bitcast(F32), ALU.subtract)\
                  .then_inc(kparts_ready, 1)
                hold(pool, kparts_ready, 2 * b + 4)
                hold(pool, q_cut, b + 1)
                hold(pool, aq.free, q.now() + 1)
                for j in range(2):
                    stage_queries(j, b * 0 + j)
                    q.step()
                norm_pool(pool)
                with loop(pool, HG, (q, 8)) as hg:
                    hold(pool, ao.free, (b * HG + hg) * 4 + 1)
                    stage_values(1, b * HG + hg)
                    for j in range(8):
                        hold(pool, aq.free, q.now())
                        stage_queries(j, (hg * 8 + j + 2) & (QH - 1))
                        q.step()
                        if j == 5:
                            hold(pool, ao.free, (b * HG + hg) * 4 + 3)
                            stage_values(0, b * HG + hg + 1)

        xnd = nc.dram_tensor("xnd", [B * S, D], F32, kind="Internal").ap()
        table = nc.dram_tensor("table", [P * TW, 1], I32, kind="Internal").ap()
        made = nc.dram_tensor("made", [NT * P, D], F32, kind="Internal").ap()
        em, er, es = rings("l2f")
        et = ring(BT, "l2f_t")
        a = area()
        EW1 = a(E * KT, 2 * I)
        EW2 = a(2, EK * D)
        XG, XGT = a(2, D), a(2, KT * P)
        EHT = a(2, EK * P)
        RW = a(KT, E)
        TRI, ONE = a(P), a(P)
        EC = a(E + 16 + TW)
        TOK = a(B * ST).bitcast(I32)
        n128 = B * ST * E
        MX0, MX1, MS, EX, WT0, WT1, POS0, POS1 = [a(B * ST) for _ in range(8)]
        IDX0, IDX1, YP0, YP1 = [a(B * ST).bitcast(I32) for _ in range(4)]
        NTL, END0, END1, START = a(E), a(E), a(E), a(E)
        EXF = a(TW)
        EXPERT, SLOTS = a(TW).bitcast(I32), a(TW).bitcast(I32)
        IX = [a(1).bitcast(I32) for _ in range(2)]
        here = a.here()
        a, a2 = area(here), area(here)
        LG, LG2, EQ, OH0, OH1, OHS, RANK, TOTAL, SCAN0, SCAN1 = [a(B * ST, E) for _ in range(10)]
        CMP, LT = a(TW, E), a(S)
        ESILU, EHID, YE = a2(2, I), a2(2, I), a2(2, D)
        YG = [XG[:, 0, :], XG[:, 1, :], XGT[:, 0, :], XGT[:, 1, :]]
        ew_in, xnd_in, router_in = sem("ew_in"), sem("xnd_in"), sem("router_in")
        pair_exp_in, pair_exp, ones_ready, routed = sem("pair_exp_in"), sem("pair_exp"), sem("ones_ready"), sem("routed")
        table_zero, table_in, slots_in = sem("table_zero"), sem("table_in"), sem("slots_in")
        ix_ready = sem("ix_ready")
        xg_in, ew2_in, y_stored = [[sem(f"{n}{u}") for u in range(2)] for n in ("xg_in", "ew2_in", "y_stored")]
        y_ready, yg_used, e_zero = sem("y_ready"), sem("yg_used"), sem("e_zero")
        yg_in = [sem(f"yg_in{k}") for k in range(4)]
        ZERO = sb("ZERO", [P, TW], I32)
        ROUTE_R = B + 2

        def moe_sync(sp):
            sp.wait_ge(x_done, 5 * B)
            for dst, src in ((RW, l2_router), (EC, moe_row.to_broadcast([P, E + 16 + TW])), (TRI, moe_tri), (TOK, moe_token)):
                sp.dma_start(dst, src).then_inc(router_in, 16)
            for b in range(B):
                sp.wait_ge(xn_ready, 5 * B + b + 1)
                sp.dma_start(xnd[b * S:(b + 1) * S, :].rearrange("(s p) d -> p s d", p=P), XN[:, :, :]).then_inc(xnd_in, 16)
            for e in range(E):
                sp.dma_start(EW1[:, e * KT:(e + 1) * KT, :], l2_w12[:, e * KT:(e + 1) * KT, :]).then_inc(ew_in, 16)
            sp.wait_ge(table_in, 2 * B * ST * 16)
            sp.dma_start(SLOTS, table.rearrange("(p n) o -> p (n o)", p=P)).then_inc(slots_in, 16)
            sp.wait_ge(routed, 1)

            def down(u, t):
                e = sp.value_load(EXPERT[0:1, ds(t, 1)], min_val=0, max_val=E - 1)
                sp.dma_start(EW2[:, u, :].rearrange("p (a n) -> p a n", a=1), l2_w2[ds(e, 1)].rearrange("a p n -> p a n"))\
                  .then_inc(ew2_in[u], 16)
            down(1, 0)
            down(0, 0)
            with sp.Fori(0, NT // 2) as i:
                for u in range(2):
                    sp.wait_ge(er.full, ROUTE_R + i * 4 + 2 * u + 2)
                    down(1 - u, i * 2 + u + 1)
                    sp.wait_ge(y_ready, i * 2 + u + 1)
                    sp.dma_start(made[ds((i * 2 + u) * P, P), :], YE[:, u, :]).then_inc(y_stored[u], 16)

        def moe_tensor(pe):
            m, r, s, t = Count(), Count(), Count(), Count()
            pe.wait_ge(x_done, 5 * B)
            pe.wait_ge(router_in, 64)
            for b in range(B):
                pe.wait_ge(turn.free, T_PE.now() + 2)
                bank = start_job(pe, em, m)
                for kt in range(KT):
                    last = nc.tensor.matmul(bank[0:E, :], RW[:, kt, :], XT[:, b % 2, kt, :], start=kt == 0, stop=kt == KT - 1)
                last.then_inc(em.full, 1)
                pe.wait_ge(em.free, m.now() + 2)
                bank = start_job(pe, er, r)
                for st in range(ST):
                    last = nc.tensor.transpose(bank[:, st * E:(st + 1) * E], LT[0:E, st * P:(st + 1) * P], ID[0:E, 0:E])
                last.then_inc(er.full, 1)
                if b < B - 1:
                    norm_tensor(pe)
            pe.wait_ge(ones_ready, 2)
            for w in (TRI, ONE):
                nc.tensor.matmul(start_job(pe, er, r)[:, 0:n128], w, OHS.rearrange("p t e -> p (t e)"), start=True, stop=True)\
                  .then_inc(er.full, 1)
            pe.wait_ge(turn.free, T_PE.now() + 2)
            pe.wait_ge(routed, 1)
            pe.wait_ge(ew_in, E * 16)
            pe.wait_ge(e_zero, 1)
            return m, r, s, t

        def moe_tensor_tiles(pe, m, r, s, t):
            def turn_tile(u, i):
                pe.wait_ge(xg_in[u], i * 16 + 16)
                bank = start_job(pe, et, t)
                for kt in range(KT):
                    last = nc.tensor.transpose(bank[:, kt * P:(kt + 1) * P], XG[:, u, kt * P:(kt + 1) * P], ID[:, :])
                last.then_inc(et.full, 1)

            turn_tile(0, 0)
            with loop(pe, NT // 2, (m, 2), (r, 4), (s, 2), (t, 2)) as i:
                for u in range(2):
                    e = pe.value_load(EXPERT[0:1, ds(i * 2 + u, 1)], min_val=0, max_val=E - 1)
                    hold(pe, et.free, t.now() + 2)
                    for job, n, c in ((em, m, 0), (er, r, I)):
                        bank = start_job(pe, job, n)
                        for kt in range(KT):
                            last = nc.tensor.matmul(bank[:, 0:I].rearrange("p (a n) -> p a n", a=1), XGT[:, u, kt * P:(kt + 1) * P],
                                                    EW1[:, ds(e * KT + kt, 1), c:c + I], start=kt == 0, stop=kt == KT - 1)
                        last.then_inc(job.full, 1)
                    up_done = r.now() + 2
                    turn_tile(1 - u, i + u)
                    hold(pe, es.free, s.now() + 2)
                    pe.wait_ge(ew2_in[1 - u], (i + 1) * 16)
                    bank = start_job(pe, er, r)
                    for k in range(EK):
                        rows = min(P, I - k * P)
                        last = nc.tensor.matmul(bank, EHT[0:rows, 1 - u, k * P:(k + 1) * P], EW2[0:rows, 1 - u, k * D:(k + 1) * D],
                                                start=k == 0, stop=k == EK - 1)
                    last.then_inc(er.full, 1)
                    hold(pe, er.free, up_done)
                    bank = start_job(pe, es, s)
                    for k in range(EK):
                        rows = min(P, I - k * P)
                        last = nc.tensor.transpose(bank[0:rows, k * P:(k + 1) * P], EHID[:, u, k * P:k * P + rows], ID[:, :])
                    last.then_inc(es.full, 1)
            pe.wait_ge(et.free, t.now() + 2)
            pe.wait_ge(er.free, r.now() + 2)
            pe.wait_ge(es.free, s.now() + 2)

        def moe_scalar(act):
            m, s, t = Count(), Count(), Count()
            for q in (em, es, et):
                act.sem_inc(q.free, 2)
            for b in range(B):
                nc.scalar.copy(LT[0:E, :], full(act, em, m)[0:E, :]).then_inc(em.free, 1)
                if b < B - 1:
                    norm_scalar(act, (b + 1) & 1)
            act.wait_ge(pair_exp_in, 1)
            nc.scalar.activation(EX, EX, ACT.Exp).then_inc(pair_exp, 1)

            def rows(u):
                nc.scalar.copy(XGT[:, u, :], full(act, et, t)).then_inc(et.free, 1)
            rows(0)
            with loop(act, NT // 2, (m, 2), (s, 2), (t, 2)) as i:
                for u in range(2):
                    nc.scalar.activation(ESILU[:, u, :], full(act, em, m)[:, 0:I], ACT.Silu).then_inc(em.free, 1)
                    rows(1 - u)
                    bank = full(act, es, s)
                    nc.scalar.copy(EHT[:, u, 0:2 * P], bank[:, 0:2 * P])
                    nc.scalar.copy(EHT[0:I - 2 * P, u, 2 * P:], bank[0:I - 2 * P, 2 * P:EK * P]).then_inc(es.free, 1)

        def moe_vector(v):
            r, m = Count(), Count()
            one = lambda t, n: t.rearrange("p (t o) -> p t o", o=1).to_broadcast([P, B * ST, n])
            per_e = lambda t, n=B * ST: t.rearrange("p (o e) -> p o e", o=1).to_broadcast([P, n, E])
            tt = nc.vector.tensor_tensor
            v.sem_inc(er.free, 2)
            for u in range(2):
                v.sem_inc(y_stored[u], 16)
            v.wait_ge(router_in, 64)
            nc.vector.memset(ONE, 1.0).then_inc(ones_ready, 1)
            for b in range(B):
                bank = full(v, er, r)
                nc.vector.tensor_copy(LG[:, b * ST:(b + 1) * ST, :], bank[:, 0:ST * E].rearrange("p (s e) -> p s e", e=E)).then_inc(er.free, 1)
                if b < B - 1:
                    v.wait_ge(xnd_in, 16 * (b + 1))
                    norm_vector(v, b + 1)
                    T_V.step(KT)
            v.wait_ge(er.free, r.now() + 2)
            for mx, lg, oh in ((MX0, LG, OH0), (MX1, LG2, OH1)):
                if oh is OH1:
                    link(v, nc.vector.tensor_scalar(LG2, OH0, -1.0e30, None, ALU.mult))
                    link(v, tt(LG2, LG2, LG, ALU.add))
                link(v, nc.vector.tensor_reduce(mx, lg, op=ALU.max, axis=AX.X))
                link(v, tt(EQ, lg, one(mx, E), ALU.is_ge))
                link(v, tt(EQ, EQ, per_e(EC[:, 0:E]), ALU.mult))
                link(v, nc.vector.tensor_reduce(MS, EQ, op=ALU.max, axis=AX.X))
                link(v, tt(oh, EQ, one(MS, E), ALU.is_equal))
            tt(OHS, OH0, OH1, ALU.add).then_inc(ones_ready, 1)
            tt(EX, MX1, MX0, ALU.subtract).then_inc(pair_exp_in, 1)
            v.wait_ge(pair_exp, 1)
            link(v, nc.vector.tensor_scalar(WT0, EX, 1.0, None, ALU.add))
            link(v, nc.vector.reciprocal(WT0, WT0))
            link(v, nc.vector.tensor_scalar(WT0, WT0, G[:, 6:7], None, ALU.mult))
            link(v, tt(WT1, EX, WT0, ALU.mult))
            nc.vector.tensor_copy(RANK, full(v, er, r)[:, 0:n128].rearrange("p (t e) -> p t e", e=E)).then_inc(er.free, 1)
            bank = full(v, er, r)[:, 0:n128].rearrange("p (t e) -> p t e", e=E)
            nc.vector.tensor_copy(TOTAL, bank)
            nc.vector.tensor_copy(SCAN0, bank).then_inc(er.free, 1)
            v.wait_ge(er.free, r.now() + 2)

            def scan(of, to, n, cut):
                w = 1
                while w < n:
                    nc.vector.tensor_copy(cut(to, 0, w), cut(of, 0, w)).then_inc(vec, 1)
                    V.step()
                    link(v, tt(cut(to, w, n), cut(of, w, n), cut(of, 0, n - w), ALU.add))
                    of, to, w = to, of, 2 * w
                return of
            incl = scan(SCAN0, SCAN1, B * ST, lambda t, i, j: t[:, i:j, :])
            link(v, tt(TOTAL, incl, TOTAL, ALU.subtract))
            link(v, tt(RANK, RANK, TOTAL, ALU.add))
            count = incl[:, B * ST - 1, :]
            c3 = CMP.rearrange("p a b -> p (a b)")[:, 0:E * 16].rearrange("p (e t) -> p e t", e=E)
            link(v, tt(c3, count.rearrange("p (e o) -> p e o", o=1).to_broadcast([P, E, 16]),
                       EC[:, E:E + 16].rearrange("p (o t) -> p o t", o=1).to_broadcast([P, E, 16]), ALU.is_gt))
            link(v, nc.vector.tensor_reduce(NTL, c3, op=ALU.add, axis=AX.X))
            link(v, nc.vector.tensor_copy(END0, NTL))
            end = scan(END0, END1, E, lambda t, i, j: t[:, i:j])
            link(v, tt(START, end, NTL, ALU.subtract))
            link(v, nc.vector.tensor_scalar(START, START, float(P), None, ALU.mult))
            link(v, tt(RANK, RANK, per_e(START), ALU.add))
            for oh, pos, idx, yp in ((OH0, POS0, IDX0, YP0), (OH1, POS1, IDX1, YP1)):
                link(v, tt(EQ, oh, RANK, ALU.mult))
                link(v, nc.vector.tensor_reduce(pos, EQ, op=ALU.add, axis=AX.X))
                link(v, nc.vector.tensor_scalar(yp, pos, float(P), None, ALU.add))
                link(v, nc.vector.tensor_copy(idx, pos))
                link(v, nc.vector.tensor_scalar(idx, idx, 7, None, ALU.arith_shift_right))
                link(v, nc.vector.tensor_copy(MS, idx))
                link(v, nc.vector.tensor_scalar(MS, MS, float(1 - P * TW), None, ALU.mult))
                link(v, nc.vector.scalar_tensor_tensor(out=MS, in0=pos, scalar=float(TW), in1=MS, op0=ALU.mult, op1=ALU.add))
                link(v, nc.vector.tensor_copy(idx, MS))
            link(v, tt(CMP, EC[:, E + 16:].rearrange("p (t o) -> p t o", o=1).to_broadcast([P, TW, E]), per_e(end, TW), ALU.is_ge))
            link(v, nc.vector.tensor_reduce(EXF, CMP, op=ALU.add, axis=AX.X))
            nc.vector.tensor_scalar(EXPERT, EXF, float(E - 1), None, ALU.min).then_inc(routed, 1)

            m.step(B)
            with loop(v, NT // 2, (m, 2), (r, 4)) as i:
                for u in range(2):
                    bank = full(v, er, r)
                    v.wait_ge(em.free, m.step() + 2)
                    tt(EHID[:, u, :], ESILU[:, u, :], bank[:, 0:I], ALU.mult).then_inc(er.free, 1)
                    v.wait_ge(y_stored[u], i * 16 + 16)
                    nc.vector.tensor_copy(YE[:, u, :], full(v, er, r)).then_inc(y_ready, 1)
                    v.wait_ge(y_ready, i * 2 + u + 1)
                    v.sem_inc(er.free, 1)
            l3_context(v)
            for k in range(2 * B * ST):
                tile, j = divmod(k, 2)
                v.wait_ge(yg_in[k % 4], 16 * (k // 4) + 16)
                nc.vector.scalar_tensor_tensor(out=X[:, tile, :], in0=YG[k % 4], scalar=(WT0, WT1)[j][:, tile:tile + 1],
                                               in1=X[:, tile, :], op0=ALU.mult, op1=ALU.add).then_inc(yg_used, 1)
                v.wait_ge(yg_used, k + 1)
            v.sem_inc(x_done, B)
            norm_vector(v, 0)
            T_V.step(KT)

        def moe_pool(pool):
            t = Count()
            nc.gpsimd.memset(EHT, 0.0).then_inc(e_zero, 1)
            for b in range(B - 1):
                norm_pool(pool)
            pool.wait_ge(routed, 1)
            pool.wait_ge(table_zero, 16)
            for tile in range(B * ST):
                for idx in (IDX0, IDX1):
                    nc.gpsimd.indirect_dma_start(out=table, out_offset=bass.IndirectOffsetOnAxis(ap=idx[:, tile:tile + 1], axis=0),
                                                 in_=TOK[:, tile:tile + 1], in_offset=None).then_inc(table_in, 16)
            pool.wait_ge(slots_in, 16)
            pool.wait_ge(xnd_in, B * 16)

            def gather(u, i, n):
                nc.gpsimd.tensor_copy(IX[u], SLOTS[:, ds(i, 1)]).then_inc(ix_ready, 1)
                hold(pool, ix_ready, n)
                nc.gpsimd.indirect_dma_start(out=XG[:, u, :], out_offset=None, in_=xnd,
                                             in_offset=bass.IndirectOffsetOnAxis(ap=IX[u], axis=0)).then_inc(xg_in[u], 16)
            gather(0, 0, 1)
            gather(1, 1, 2)
            with pool.Fori(0, NT // 2) as i:
                for u in range(2):
                    pool.wait_ge(et.full, i * 2 + u + 1)
                    gather(u, i * 2 + u + 2, i * 2 + u + 3)
            for u in range(2):
                pool.wait_ge(y_stored[u], (NT // 2 + 1) * 16)
                pool.wait_ge(xg_in[u], (NT // 2 + 1) * 16)
            pool.wait_ge(er.full, ROUTE_R + 2 * NT)
            pool.wait_ge(et.free, NT + 3)
            for k in range(2 * B * ST):
                tile, j = divmod(k, 2)
                if k >= 4:
                    pool.wait_ge(yg_used, k - 3)
                nc.gpsimd.indirect_dma_start(out=YG[k % 4], out_offset=None, in_=made,
                                             in_offset=bass.IndirectOffsetOnAxis(ap=(YP0, YP1)[j][:, tile:tile + 1], axis=0))\
                  .then_inc(yg_in[k % 4], 16)
            norm_pool(pool)

        lm, lr3, ls3 = rings("l3")
        mh = nc.dram_tensor("mh", [LH, P, 3 * C], F32, kind="Internal").ap()
        WSN = KT * P + LQ + 3 * C
        FTN = C + D + LQ + C
        a = area()
        W3 = a(LH, D)
        ROPE = a(6, S)
        KVN, KVT = a(B * ST, C), a(B * S)
        KVC = a(ST, C)
        WS = a(2, WSN)
        FT, MST = a(2, FTN), a(2, 3 * C)
        ROPEK = a(2 * ST, C)
        QB = a(4, S)
        assert a.here() <= E * KT * 2 * I + 2 * EK * D
        RQ = a(3, S)
        QHK, QP, CC = a(S), a(S), a(S)
        SUM3, RS3, NEG3 = a(2 * ST), a(2 * ST), a(2 * ST)
        KV_TMP = QB.rearrange("p a n -> p (a n)").rearrange("p (t c) -> p t c", c=C)
        PROB3, PROBT3 = a(ST, S), a(ST, S)
        l3_in, rope_in, kv_ready, kvc_ready = sem("l3_in"), sem("rope_in"), sem("kv_ready"), sem("kvc_ready")
        ft_in, ws_in, m_stored = [[sem(f"{n}{u}") for u in range(2)] for n in ("ft_in", "ws_in", "m_stored")]
        max3_done, rotated, cos_ready = sem("max3_done"), sem("rotated"), sem("cos_ready")
        FOLD_M = 2 * LH + ST
        HEAD_M = 5
        PRO_M = 4

        def l3_sync(sp):
            sp.wait_ge(er.full, ROUTE_R + 2 * NT)
            for u in range(2):
                sp.wait_ge(ew2_in[u], (NT // 2 + 1) * 16)

            def fold(u, h):
                sp.dma_start(FT[:, u, :].rearrange("p (a n) -> p a n", a=1), l3_fold[ds(h, 1)].rearrange("a p n -> p a n")).then_inc(ft_in[u], 16)

            def weights(u, h):
                ws = WS[:, u, :].rearrange("p (a n) -> p a n", a=1)
                sp.dma_start(ws[:, :, 0:KT * P + LQ], l3_wq[ds(h, 1)].rearrange("a p n -> p a n")).then_inc(ws_in[u], 16)
                sp.dma_start(ws[:, :, KT * P + LQ:], mh[ds(h, 1)].rearrange("a p n -> p a n")).then_inc(ws_in[u], 16)
            for u in range(2):
                fold(u, u)
            for dst, src in ((KVN, ctx_n.rearrange("(n p) d -> p n d", p=P)), (ROPEK, rope_k)):
                sp.dma_start(dst, src).then_inc(l3_in, 16)
            with sp.Fori(0, LH // 2) as i:
                for u in range(2):
                    hold(sp, lm.full, i * 4 + 2 * u + 2)
                    fold(u, (i * 2 + u + 2) & (LH - 1))
                    hold(sp, lm.free, i * 4 + 2 * u + 4)
                    sp.dma_start(mh[ds(i * 2 + u, 1)].rearrange("a p n -> p a n"), MST[:, u, :].rearrange("p (a n) -> p a n", a=1))\
                      .then_inc(m_stored[u], 16)
            sp.dma_start(ROPE, rope_q).then_inc(rope_in, 16)
            for u in range(2):
                sp.wait_ge(m_stored[u], (LH // 2 + 1) * 16)
            for u in range(2):
                weights(u, u)
            with sp.Fori(0, B * LH // 2) as i:
                for u in range(2):
                    hold(sp, lm.full, i * 2 * HEAD_M + (2 + u) * HEAD_M + FOLD_M + PRO_M - 2 * HEAD_M)
                    weights(u, (i * 2 + u + 2) & (LH - 1))

        def l3_tensor(pe):
            m, r, s, w = Count(), Count(), Count(), Count()
            one = lambda t: t.rearrange("p (a n) -> p a n", a=1)
            with loop(pe, LH // 2, (m, 4)) as i:
                for u in range(2):
                    pe.wait_ge(ft_in[u], i * 16 + 16)
                    bank = start_job(pe, lm, m)
                    nc.tensor.matmul(bank, FT[:, u, 0:C], FT[:, u, C:C + D], start=True, stop=True).then_inc(lm.full, 1)
                    bank = start_job(pe, lm, m)
                    for k in range(3):
                        last = nc.tensor.matmul(bank[:, k * C:(k + 1) * C], FT[:, u, C + D + k * P:C + D + (k + 1) * P],
                                                FT[:, u, C + D + LQ:], start=True, stop=True)
                    last.then_inc(lm.full, 1)
            pe.wait_ge(kv_ready, 1)
            for t in range(ST):
                bank = start_job(pe, lm, m)
                for k in range(ST):
                    last = nc.tensor.transpose(bank[:, k * P:(k + 1) * P], KVN[:, t * ST + k, :], ID[:, :])
                last.then_inc(lm.full, 1)

            def head_queries(u, half, bank, kts):
                for kt in kts:
                    last = nc.tensor.matmul(one(bank), WS[:, u, kt * P:(kt + 1) * P], XT[:, ds(half, 1), kt, :],
                                            start=kt == 0, stop=kt == KT - 1)
                    if kt == KT - 1:
                        last.then_inc(lm.full, 1)

            def big_queries(u):
                hold(pe, lm.free, m.now() + 2)
                for k, job, n in ((2, lr3, r), (0, lm, m), (1, lm, m)):
                    nc.tensor.matmul(start_job(pe, job, n), WS[:, u, (KT + k) * P:(KT + k + 1) * P], QHK, start=True, stop=True)\
                      .then_inc(job.full, 1)

            def score_queries(u):
                hold(pe, rotated, w.step())
                bank = start_job(pe, lm, m)
                for k in range(3):
                    last = nc.tensor.matmul(bank, WS[:, u, KT * P + LQ + k * C:KT * P + LQ + (k + 1) * C], RQ[:, k, :],
                                            start=k == 0, stop=k == 2)
                last.then_inc(lm.full, 1)

            norm_tensor(pe)
            pe.wait_ge(turn.free, T_PE.now() + 2)
            pe.wait_ge(ws_in[0], 32)
            head_queries(0, 0, start_job(pe, lm, m), range(KT))
            big_queries(0)
            score_queries(0)
            def two_heads(b, hp):
                for u in range(2):
                    hold(pe, lm.free, m.now() + 2)
                    half, n = (b & 1, 32) if u == 0 else (((b * 8 + hp + 1) >> 3) & 1, 64)
                    for st in range(ST):
                        nc.tensor.matmul(start_job(pe, ls3, s), QP[:, st * P:(st + 1) * P], KVT[:, ds(b * S, S)], start=True, stop=True)\
                          .then_inc(ls3.full, 1)
                        if st == 1:
                            pe.wait_ge(ws_in[1 - u], b * (16 * LH) + hp * 32 + n)
                            bank = start_job(pe, lm, m)
                            head_queries(1 - u, half, bank, range(0, 2))
                    head_queries(1 - u, half, bank, range(2, KT))
                    hold(pe, ls3.free, s.now() + 2)

                    def turn_probs(lts):
                        for lt in lts:
                            bank = start_job(pe, turn, T_PE)
                            for st in range(ST):
                                last = nc.tensor.transpose(bank[:, st * P:(st + 1) * P], PROB3[:, st, lt * P:(lt + 1) * P], ID[:, :])
                            last.then_inc(turn.full, 1)
                    turn_probs((0, 1))
                    big_queries(1 - u)
                    turn_probs((2, 3))
                    if u == 0:
                        hold(pe, kvc_ready, b + 1)
                    bank = start_job(pe, lm, m)
                    for lt in range(ST):
                        pe.wait_ge(turn.free, T_PE.now() + lt - 1)
                        last = nc.tensor.matmul(bank, KVC[:, lt, :], PROBT3[:, lt, :], start=lt == 0, stop=lt == ST - 1)
                    last.then_inc(lm.full, 1)
                    score_queries(1 - u)
                    hold(pe, lm.free, m.now() + 1)
                    for st in range(ST):
                        nc.tensor.matmul(one(start_job(pe, lr3, r)), CC[:, st * P:(st + 1) * P], W3[:, ds(hp * 2 + u, 1), :],
                                         start=True, stop=True).then_inc(lr3.full, 1)

            with loop(pe, B, (m, HEAD_M * LH), (r, (ST + 1) * LH), (s, ST * LH), (w, LH), (T_PE, KT + ST * LH), (N_PE, 1)) as b:
                with loop(pe, LH // 2 - 1, (m, 2 * HEAD_M), (r, 2 * (ST + 1)), (s, 2 * ST), (w, 2), (T_PE, 2 * ST)) as hp:
                    two_heads(b, hp)
                norm_tensor(pe)
                two_heads(b, LH // 2 - 1)
            pe.wait_ge(lm.free, m.now() + 2)

        def l3_scalar(act):
            m, s, w = Count(), Count(), Count()
            act.sem_inc(lm.free, 2)
            act.sem_inc(ls3.free, 2)
            for u in range(2):
                act.sem_inc(m_stored[u], 16)
            with loop(act, LH // 2, (m, 4)) as i:
                for u in range(2):
                    nc.scalar.copy(W3[:, ds(i * 2 + u, 1), :], full(act, lm, m).rearrange("p (a n) -> p a n", a=1)).then_inc(lm.free, 1)
                    act.wait_ge(m_stored[u], i * 16 + 16)
                    nc.scalar.copy(MST[:, u, :], full(act, lm, m)[:, 0:3 * C]).then_inc(lm.free, 1)
            for t in range(ST):
                nc.scalar.copy(KVT[:, t * S:(t + 1) * S], full(act, lm, m)).then_inc(lm.free, 1)

            def big_queries(first=False):
                if not first:
                    act.wait_ge(rotated, w.now())
                for k in range(2):
                    nc.scalar.copy(QB[:, k, :], full(act, lm, m)).then_inc(lm.free, 1)
                w.step()
            norm_scalar(act, 0)
            nc.scalar.copy(QHK, full(act, lm, m)).then_inc(lm.free, 1)
            big_queries(True)
            nc.scalar.copy(QP, full(act, lm, m)).then_inc(lm.free, 1)
            def two_heads():
                for u in range(2):
                    for st in range(ST):
                        act.wait_ge(max3_done, s.now() + 1)
                        bank = full(act, ls3, s)
                        nc.scalar.activation(PROB3[:, st, :], bank, ACT.Exp, bias=NEG3[:, u * ST + st:u * ST + st + 1],
                                             accum_out=SUM3[:, u * ST + st:u * ST + st + 1]).then_inc(ls3.free, 1)
                    nc.scalar.copy(QHK, full(act, lm, m)).then_inc(lm.free, 1)
                    for lt in (0, 1):
                        nc.scalar.copy(PROBT3[:, lt, :], full(act, turn, T_ACT)).then_inc(turn.free, 1)
                    big_queries()
                    for lt in (2, 3):
                        nc.scalar.copy(PROBT3[:, lt, :], full(act, turn, T_ACT)).then_inc(turn.free, 1)
                    nc.scalar.copy(CC, full(act, lm, m)).then_inc(lm.free, 1)
                    nc.scalar.copy(QP, full(act, lm, m)).then_inc(lm.free, 1)

            with loop(act, B, (m, HEAD_M * LH), (s, ST * LH), (w, LH), (T_ACT, KT + ST * LH)) as b:
                with loop(act, LH // 2 - 1, (m, 2 * HEAD_M), (s, 2 * ST), (w, 2), (T_ACT, 2 * ST)) as hp:
                    two_heads()
                norm_scalar(act, (b + 1) & 1)
                two_heads()

        def l3_context(v):
            tt = nc.vector.tensor_tensor
            v.wait_ge(l3_in, 32)
            kv = lambda t, i, j: t[:, :, i:j].rearrange("p (b s) c -> p b s c", b=B)
            tab = lambda k, i, j: ROPEK[:, k * ST:(k + 1) * ST, i:j].rearrange("p (o s) c -> p o s c", o=1).to_broadcast([P, B, ST, j - i])
            tt(kv(KV_TMP, 0, 64), kv(KVN, 64, 128), tab(1, 0, 64), ALU.mult)
            link(v, tt(kv(KV_TMP, 64, 128), kv(KVN, 0, 64), tab(1, 64, 128), ALU.mult))
            link(v, tt(kv(KVN, 0, 128), kv(KVN, 0, 128), tab(0, 0, 128), ALU.mult))
            tt(KVN, KVN, KV_TMP, ALU.add).then_inc(kv_ready, 1)

        def l3_vector(v):
            m, r, s, w = Count(), Count(), Count(), Count()
            tt = nc.vector.tensor_tensor
            v.sem_inc(lr3.free, 2)
            m.step(FOLD_M)

            def rotate():
                bank = full(v, lr3, r)
                tt(RQ[:, 2, :], bank, ROPE[:, 4, :], ALU.mult)
                tt(QB[64:128, 2, :], bank[0:64, :], ROPE[0:64, 5, :], ALU.mult)
                link(v, tt(QB[0:64, 2, :], bank[64:128, :], ROPE[64:128, 5, :], ALU.mult))
                tt(RQ[:, 2, :], RQ[:, 2, :], QB[:, 2, :], ALU.add).then_inc(lr3.free, 1)
                w.step()
                v.wait_ge(lm.free, m.now() + 5)
                tt(QB[:, 3, :], QB[:, 1, :], ROPE[:, 1, :], ALU.mult)
                v.wait_ge(lr3.free, r.now() + 2)
                link(v, tt(QB[:, 2, :], QB[:, 0, :], ROPE[:, 3, :], ALU.mult))
                v.wait_ge(cos_ready, w.now())
                tt(RQ[:, 0, :], RQ[:, 0, :], QB[:, 3, :], ALU.subtract)
                tt(RQ[:, 1, :], RQ[:, 1, :], QB[:, 2, :], ALU.add).then_inc(rotated, 1)
            v.wait_ge(rope_in, 16)
            rotate()
            m.step(PRO_M)
            with loop(v, B, (m, HEAD_M * LH), (r, (ST + 1) * LH), (s, ST * LH), (w, LH), (V, 4 * LH), (T_V, KT + ST * LH), (N_V, 1)) as b:
                norm_vector(v, (b + 1) & 3)
                T_V.step(KT)
                with loop(v, LH // 2, (m, 2 * HEAD_M), (r, 2 * (ST + 1)), (s, 2 * ST), (w, 2), (V, 8), (T_V, 2 * ST)) as hp:
                    for u in range(2):
                        for st in range(ST):
                            nc.vector.tensor_reduce(NEG3[:, u * ST + st:u * ST + st + 1], full(v, ls3, s), op=ALU.max, axis=AX.X,
                                                    negate=True).then_inc(max3_done, 1)
                        hold(v, ls3.free, s.now() + 2)
                        link(v, nc.vector.reciprocal(RS3[:, u * ST:(u + 1) * ST], SUM3[:, u * ST:(u + 1) * ST]))
                        link(v, nc.vector.tensor_scalar(RS3[:, u * ST:(u + 1) * ST], RS3[:, u * ST:(u + 1) * ST], G[:, 3:4], None, ALU.mult))
                        rotate()
                        m.step(HEAD_M)
                        for st in range(ST):
                            bank = full(v, lr3, r)
                            xb = X[:, ds(b * ST + st, 1), :].rearrange("p a n -> p (a n)")
                            nc.vector.scalar_tensor_tensor(out=xb, in0=bank, scalar=RS3[:, u * ST + st:u * ST + st + 1], in1=xb,
                                                           op0=ALU.mult, op1=ALU.add).then_inc(lr3.free, 1)
                        T_V.step(ST)
                v.wait_ge(lr3.free, r.now() + 2)
                v.sem_inc(x_done, 1)

        def l3_pool(pool):
            m = Count()
            tt = nc.gpsimd.tensor_tensor
            m.step(FOLD_M)

            def rotate():
                pool.wait_ge(lm.free, m.now() + 5)
                tt(RQ[:, 0, :], QB[:, 0, :], ROPE[:, 0, :], ALU.mult)
                tt(RQ[:, 1, :], QB[:, 1, :], ROPE[:, 2, :], ALU.mult).then_inc(cos_ready, 1)
            pool.wait_ge(rope_in, 16)
            rotate()
            m.step(PRO_M)
            with loop(pool, B, (m, HEAD_M * LH), (N_P, 1)) as b:
                hold(pool, lm.full, m.now())
                nc.gpsimd.tensor_copy(KVC, KVN[:, ds(b * ST, ST), :]).then_inc(kvc_ready, 1)
                norm_pool(pool)
                with loop(pool, LH // 2, (m, 2 * HEAD_M)) as hp:
                    for u in range(2):
                        rotate()
                        m.step(HEAD_M)

        l3f = Ffn("l3f", 7, l3_w13, l3_w2, UG, HID // P // UG, 1, lambda b, g, st: G[:, 7:8])

        def l3f_begin(sp):
            sp.wait_ge(x_done, 7 * B)
            sp.wait_ge(lm.free, FOLD_M + PRO_M + B * LH * HEAD_M + 2)
            for u in range(2):
                sp.wait_ge(ws_in[u], (B * LH + 2) * 16)

        block = ctx.enter_context(nc.Block())
        stored = sem("stored")
        zero_ready = sem("zero_ready")

        @block.sync
        def _(sp):
            x_tiles = x.rearrange("(n p) d -> p n d", p=P)
            sp.dma_start(X[:, 0:ST, :], x_tiles[:, 0:ST, :]).then_inc(loaded, 16)
            sp.dma_start(CT, ctx_t).then_inc(loaded, 16)
            sp.dma_start(ID[:, :], ident).then_inc(loaded, 16)
            sp.dma_start(G[:, :], gates.rearrange("(a n) -> a n", a=1).to_broadcast([P, 8])).then_inc(loaded, 16)
            sp.dma_start(GC[:, 0:1], gamma_raw.rearrange("(a n) -> a n", a=1).to_broadcast([P, 1])).then_inc(loaded, 16)
            sp.dma_start(WQ0, l0_wq).then_inc(l0_w, 16)
            sp.dma_start(WK0, l0_wk).then_inc(l0_w, 16)
            sp.dma_start(HAD, hadamard).then_inc(l0_had, 16)
            sp.dma_start(WH[0], l0_w2).then_inc(l0_had, 16)
            sp.dma_start(X[:, ST:, :], x_tiles[:, ST:, :]).then_inc(x_rest, 16)
            sp.wait_ge(zero_ready, 1)
            sp.dma_start(table.rearrange("(p n) o -> p (n o)", p=P), ZERO[:, :]).then_inc(table_zero, 16)
            sp.wait_ge(l0f.m.free, 2 + ST + HAD_M + 2)
            sp.dma_start(w2h.rearrange("g p n -> p g n"), WH[1].rearrange("p (g u) n -> p g (u n)", u=UG)).then_inc(wh_stored, 16)
            ffn_sync(sp, l0f, lambda sp: sp.wait_ge(wh_stored, 16))
            l1_sync(sp)
            l1f_sync_weights(sp)
            l1f_sync(sp)
            l2_sync(sp)
            moe_sync(sp)
            l3_sync(sp)
            ffn_sync(sp, l3f, l3f_begin)
            sp.wait_ge(stored, B * 16)

        @block.tensor
        def _(pe):
            pe.wait_ge(loaded, 80)
            l0_tensor(pe)
            l1_tensor(pe)
            l1f_tensor(pe)
            l2_tensor(pe)
            moe_tensor_tiles(pe, *moe_tensor(pe))
            l3_tensor(pe)
            ffn_tensor(pe, l3f)

        @block.scalar
        def _(act):
            act.sem_inc(turn.free, 2)
            act.wait_ge(loaded, 80)
            nc.scalar.activation(G[:, :], G[:, :], ACT.Tanh).then_inc(g_ready, 1)
            nc.scalar.activation(GC[:, 0:1], GC[:, 0:1], ACT.Sigmoid).then_inc(g_ready, 1)
            l0_scalar(act)
            l1_scalar(act)
            l1f_scalar(act)
            l2_scalar(act)
            moe_scalar(act)
            l3_scalar(act)
            ffn_scalar(act, l3f)

        @block.vector
        def _(v):
            v.wait_ge(loaded, 80)
            norm_vector(v, 0)
            v.wait_ge(g_ready, 2)
            link(v, nc.vector.tensor_scalar(GC[:, 1:2], GC[:, 0:1], -1.0, 1.0, ALU.mult, ALU.add))
            link(v, nc.vector.tensor_scalar(GC[:, 1:2], GC[:, 1:2], G[:, 0:1], None, ALU.mult))
            nc.vector.tensor_scalar(GC[:, 2:3], GC[:, 0:1], G[:, 0:1], 0.5, ALU.mult, ALU.mult).then_inc(gc_ready, 1)
            l0_vector(v)
            l1_vector(v)
            l1f_vector(v)
            l2_vector(v)
            moe_vector(v)
            l3_vector(v)
            ffn_vector(v, l3f)

        @block.gpsimd
        def _(pool):
            nc.gpsimd.memset(ZERO[:, :], 0).then_inc(zero_ready, 1)
            nc.gpsimd.memset(HALF[:, :], -0.5).then_inc(consts, 1)
            pool.wait_ge(consts, 1)
            norm_pool(pool)
            had_pool(pool)
            with loop(pool, 2 * B, (N_P, 1)):
                norm_pool(pool)
            l1_pool(pool)
            l1f_pool(pool)
            l2_pool(pool)
            pool.wait_ge(x_done, 5 * B)
            moe_pool(pool)
            l3_pool(pool)
            with loop(pool, B, (N_P, 1)) as b:
                norm_pool(pool)
                pool.wait_ge(x_done, b + (7 * B + 1))
                nc.gpsimd.dma_start(out[ds(b * S, S), :].rearrange("(n p) d -> p n d", p=P), X[:, ds(b * ST, ST), :]).then_inc(stored, 16)


def layouts(inp):
    import numpy as np

    f = {k: np.asarray(v) for k, v in inp.items()}
    c = np.ascontiguousarray

    def up_tiles(wg, wu):
        n = wg.shape[0] // P
        w = np.stack([wg, wu]).reshape(2, n, P, KT, P)
        return c(w.transpose(1, 4, 3, 0, 2)).reshape(n, P, KT * 2 * P)

    def cut(w):
        return c(w.reshape(-1, P, w.shape[-1]).transpose(1, 0, 2))

    o = {}
    o["x"] = f["x"].reshape(B * S, D)
    ctx = f["ctx_512"].reshape(B * S, C)
    o["ctx_n"], o["ctx_t"] = ctx, c(ctx.T)
    o["gates"] = np.concatenate([f["g_xattn"], f["g_ffn"]])
    o["gamma_raw"] = f["L0_xattn_gamma_raw"].reshape(1)
    o["ident"] = np.eye(P, dtype=np.float32)
    had = np.ones((1, 1), np.float32)
    while len(had) < P:
        had = np.block([[had, had], [had, -had]])
    o["hadamard"] = had.astype(np.float32)
    o["l0_w13"] = up_tiles(f["L0_ffn_W1"], f["L0_ffn_W3"])
    o["l0_w2"] = cut(f["L0_ffn_W2"].T)
    row = lambda *n: np.stack([f["L1_" + k] for k in n])
    col = lambda k: f["L1_ffn_" + k].reshape(-1, P).T
    o["l1_wk"], o["l1_bk"] = c(f["L1_xattn_W_k"].T), f["L1_xattn_b_k"].reshape(P, 1)
    o["l1_bk_row"] = f["L1_xattn_b_k"].reshape(1, C)
    o["l1_ln"] = row("xattn_ln_gamma", "xattn_ln_beta")
    o["l1_rows"] = row("ffn_out_gamma", "ffn_out_beta")
    o["l1_inrows"] = row("ffn_in_gamma", "ffn_in_beta")
    o["l1_cols"] = c(np.concatenate([col(k) for k in ("bc_b", "gate_b")], 1))
    o["l1_trows"] = np.concatenate([f["L1_ffn_" + k] for k in ("agg_b", "d2_b", "pn_gamma", "pn_beta")])[None]
    o["l1_d1row"] = f["L1_ffn_d1_b"].reshape(4, D)
    for k, n in (("l1_agg", "agg_w"), ("l1_d1", "d1_w"), ("l1_d2", "d2_w"), ("l1_bc", "bc_w"), ("l1_gate", "gate_w")):
        o[k] = cut(f["L1_ffn_" + n])
    o["sum4"] = np.tile(np.eye(32, dtype=np.float32), (4, 1))
    o["l2_router"] = cut(f["L2_ffn_router_w"].T)
    o["l2_w12"] = c(f["L2_ffn_w1"].reshape(E, 2 * I, KT, P).transpose(3, 0, 2, 1)).reshape(P, E * KT, 2 * I)
    w2 = np.zeros((E, EK * P, D), np.float32)
    w2[:, :I] = f["L2_ffn_w2"].transpose(0, 2, 1)
    o["l2_w2"] = c(w2.reshape(E, EK, P, D).transpose(0, 2, 1, 3)).reshape(E, P, EK * D)
    o["moe_row"] = np.concatenate([8.0 - np.arange(E), 128.0 * np.arange(16), np.arange(TW)]).astype(np.float32)[None]
    o["moe_tri"] = np.triu(np.ones((P, P), np.float32), 1)
    o["moe_token"] = (np.arange(B * ST)[None, :] * P + np.arange(P)[:, None]).astype(np.int32)
    order = np.concatenate([np.arange(128), np.arange(192, 320), np.arange(128, 192), np.arange(320, 384)])
    wq = f["L3_xattn_Wq"].reshape(LH, LK, KT, P).transpose(0, 3, 2, 1).reshape(LH, P, KT * LK)
    o["l3_wq"] = np.concatenate([wq, f["L3_xattn_w_kc_q"][:, :, order]], 2)
    wo = f["L3_xattn_Wo"].reshape(D, LH, LK).transpose(1, 2, 0)
    qr_kr = np.zeros((LH, P, LQ + C), np.float32)
    qr_kr[:, :LR, :LQ] = f["L3_xattn_W_qr"][:, order, :].transpose(0, 2, 1)
    qr_kr[:, :LR, LQ:] = f["L3_xattn_W_kr"].transpose(0, 2, 1)
    o["l3_fold"] = np.concatenate([f["L3_xattn_w_kc_kv"], wo, qr_kr], 2)

    def rope(dim):
        inv = (np.float32(1) / np.float32(10000) ** (np.arange(0, dim, 2, dtype=np.float32) / np.float32(dim))).astype(np.float32)
        at = np.repeat(np.arange(S, dtype=np.float32)[:, None] * inv, 2, axis=1).astype(np.float64)
        return np.cos(at).astype(np.float32), np.sin(at).astype(np.float32)
    cos, sin = rope(LQ)
    cos, sin = cos.T[order].reshape(3, P, S).copy(), sin.T[order].reshape(3, P, S).copy()
    sin[2] = np.concatenate([sin[2, 64:], -sin[2, :64]])
    o["rope_q"] = c(np.stack([cos, sin], 1).reshape(6, P, S).transpose(1, 0, 2))
    cos, sin = rope(C)
    sin[:, :C // 2] *= -1
    o["rope_k"] = c(np.stack([cos, sin]).reshape(2 * ST, P, C).transpose(1, 0, 2))
    o["l3_w13"] = up_tiles(f["L3_ffn_w_gate"], f["L3_ffn_w_up"])
    o["l3_w2"] = c(f["L3_ffn_w_down"].T.reshape(HID // P // UG, UG, P, D).transpose(0, 2, 1, 3)).reshape(HID // P // UG, P, UG * D)
    o["l0_wq"], o["l0_wk"] = c(f["L0_xattn_Wq"].T), c(f["L0_xattn_Wk"].T)
    return o


LOADED = """x ctx_n ctx_t gates gamma_raw ident l0_wq l0_wk hadamard l0_w13 l0_w2 l1_wk l1_bk l1_bk_row l1_ln l1_rows l1_inrows l1_cols l1_trows l1_d1row l1_agg l1_d1 l1_d2 l1_bc l1_gate sum4 l2_router l2_w12 l2_w2 moe_row moe_tri moe_token l3_wq l3_fold rope_q rope_k l3_w13 l3_w2""".split()


def kernel(**inputs):
    import numpy as np
    import concourse.bacc as bacc
    from concourse.bass_utils import run_bass_kernel_spmd

    nc = bacc.Bacc("TRN2", target_bir_lowering=False, num_devices=1)
    laid = layouts(inputs)
    arrays = {f"{name}_dram": np.ascontiguousarray(laid[name]) for name in LOADED}
    args = [nc.dram_tensor(f"{name}_dram", arrays[f"{name}_dram"].shape, mybir.dt.from_np(arrays[f"{name}_dram"].dtype),
                           kind="ExternalInput").ap() for name in LOADED]
    out = nc.dram_tensor("out_dram", (B * S, D), F32, kind="ExternalOutput").ap()
    flamingo(nc, *args, out)
    return run_bass_kernel_spmd(nc, [arrays], core_ids=[0]).results[0]["out_dram"].reshape(B, S, D)
```
